# Optimizing a Trainium2 kernel written in Bass

```python
import numpy as np
import jax
import jax.numpy as jnp

def _softmax(x, axis=-1):
    return jax.nn.softmax(x, axis=axis)

def _gelu(x):
    return jax.nn.gelu(x, approximate=True)

def _silu(x):
    return jax.nn.silu(x)

def _sigmoid(x):
    return jax.nn.sigmoid(x)

def _layernorm(x, axis=-1, eps=1e-05):
    m = jnp.mean(x, axis=axis, keepdims=True)
    v = jnp.var(x, axis=axis, keepdims=True)
    return (x - m) / jnp.sqrt(v + eps)

def _scatter_add(tgt, idx, src, axis=0):
    return tgt.at[idx].add(src)

def _segment_sum(src, seg, n):
    return jax.ops.segment_sum(src, seg, n)
kernel_name = 'mk_cond_seq_d4_seqx_r8_da2dca'

def setup_inputs(seed: int=0):
    np.random.seed(seed)
    _w = jnp.asarray

    def _rec_inputs():
        import jax
        import jax.numpy as jnp
        _rk = jax.random.key(seed)
        x = 1.648e-05 + 1 * jax.random.normal(jax.random.fold_in(_rk, 1), (2, 512, 144), jnp.float32)
        _lenS = 512 - jax.random.randint(jax.random.fold_in(_rk, 7), (2,), 0, max(1, 512 // 4) + 1, jnp.int32)
        _lenS2 = 512 - jax.random.randint(jax.random.fold_in(_rk, 8), (2,), 0, max(1, 512 // 4) + 1, jnp.int32)
        cond_1152 = 0.00914911 + 1.00357 * jax.random.normal(jax.random.fold_in(_rk, 11), (2, 144), jnp.float32)
        return (x, cond_1152)
    x, cond_1152 = _rec_inputs()

    def _L0_cond_setup():
        import jax, jax.numpy as jnp
        import numpy as np
        B, L, C = (8, 128, 144)
        H = 16
        D = C // H
        FF = int(C * 4.0)
        EPS = 1e-06

        def _layernorm(x):
            mu = jnp.mean(x, axis=-1, keepdims=True)
            var = jnp.mean(jnp.square(x - mu), axis=-1, keepdims=True)
            return (x - mu) * jax.lax.rsqrt(var + EPS)

        def _modulate(x, shift, scale):
            return x * (1.0 + scale) + shift

        def _attention(h, W_qkv, b_qkv, W_proj, b_proj):
            b, l, c = h.shape
            qkv = h @ W_qkv + b_qkv
            qkv = qkv.reshape(b, l, 3, H, D)
            q, k, v = (qkv[:, :, 0], qkv[:, :, 1], qkv[:, :, 2])
            scale = D ** (-0.5)
            scores = jnp.einsum('blhd,bmhd->bhlm', q * scale, k)
            attn = jax.nn.softmax(scores, axis=-1)
            o = jnp.einsum('bhlm,bmhd->blhd', attn, v).reshape(b, l, c)
            return o @ W_proj + b_proj
        key = jax.random.key(seed)
        ks = jax.random.split(key, 12)
        s = 0.02
        return {'x': jax.random.normal(ks[0], (B, L, C), jnp.float32), 'c': jax.random.normal(ks[1], (B, 1, C), jnp.float32), 'W_qkv': jax.random.normal(ks[2], (C, 3 * C), jnp.float32) * s, 'b_qkv': jnp.zeros((3 * C,), jnp.float32), 'W_proj': jax.random.normal(ks[3], (C, C), jnp.float32) * s, 'b_proj': jnp.zeros((C,), jnp.float32), 'W_fc1': jax.random.normal(ks[4], (C, FF), jnp.float32) * s, 'b_fc1': jnp.zeros((FF,), jnp.float32), 'W_fc2': jax.random.normal(ks[5], (FF, C), jnp.float32) * s, 'b_fc2': jnp.zeros((C,), jnp.float32), 'W_ada': jax.random.normal(ks[6], (C, 6 * C), jnp.float32) * s, 'b_ada': jnp.zeros((6 * C,), jnp.float32)}
    _L0_cond_all = _L0_cond_setup()
    _L0_cond_in = {k: v for k, v in _L0_cond_all.items() if k in ('W_qkv', 'b_qkv', 'W_proj', 'b_proj', 'W_fc1', 'b_fc1', 'W_fc2', 'b_fc2', 'W_ada', 'b_ada')}
    del _L0_cond_all

    def _L1_cond_setup():
        import jax, jax.numpy as jnp
        import numpy as np
        N, T, D, H = (32, 128, 144, 16)
        DH = D // H
        MLP = int(D * 4.0)
        EPS = 1e-06

        def _layernorm(x):
            m = jnp.mean(x, axis=-1, keepdims=True)
            v = jnp.var(x, axis=-1, keepdims=True)
            return (x - m) * jax.lax.rsqrt(v + EPS)

        def _modulate(x, shift, scale):
            return x * (1.0 + scale[:, None, :]) + shift[:, None, :]

        def _attention(x, qkv_w, qkv_b, proj_w, proj_b):
            n, t, d = x.shape
            scale = DH ** (-0.5)
            qkv = x @ qkv_w + qkv_b
            qkv = qkv.reshape(n, t, 3, H, DH)
            q, k, v = (qkv[:, :, 0], qkv[:, :, 1], qkv[:, :, 2])
            attn = jnp.einsum('nthd,ntkd->nthk', q * scale, k)
            attn = jax.nn.softmax(attn, axis=-1)
            out = jnp.einsum('nthk,ntkd->nthd', attn, v)
            out = out.transpose(0, 2, 1, 3).reshape(n, t, d)
            return out @ proj_w + proj_b

        def _mlp(x, fc1_w, fc1_b, fc2_w, fc2_b):
            h = jax.nn.gelu(x @ fc1_w + fc1_b, approximate=False)
            return h @ fc2_w + fc2_b
        key = jax.random.key(seed)
        ks = jax.random.split(key, 14)
        s = 0.02
        return {'x': jax.random.normal(ks[0], (N, T, D), jnp.float32), 'c': jax.random.normal(ks[1], (N, D), jnp.float32), 'qkv_w': jax.random.normal(ks[2], (D, 3 * D), jnp.float32) * s, 'qkv_b': jax.random.normal(ks[3], (3 * D,), jnp.float32) * s, 'proj_w': jax.random.normal(ks[4], (D, D), jnp.float32) * s, 'proj_b': jax.random.normal(ks[5], (D,), jnp.float32) * s, 'fc1_w': jax.random.normal(ks[6], (D, MLP), jnp.float32) * s, 'fc1_b': jax.random.normal(ks[7], (MLP,), jnp.float32) * s, 'fc2_w': jax.random.normal(ks[8], (MLP, D), jnp.float32) * s, 'fc2_b': jax.random.normal(ks[9], (D,), jnp.float32) * s, 'ada_w': jax.random.normal(ks[10], (D, 6 * D), jnp.float32) * s, 'ada_b': jax.random.normal(ks[11], (6 * D,), jnp.float32) * s}
    _L1_cond_all = _L1_cond_setup()
    _L1_cond_in = {k: v for k, v in _L1_cond_all.items() if k in ('qkv_w', 'qkv_b', 'proj_w', 'proj_b', 'fc1_w', 'fc1_b', 'fc2_w', 'fc2_b', 'ada_w', 'ada_b')}
    del _L1_cond_all

    def _L2_cond_setup():
        import jax, jax.numpy as jnp
        import numpy as np
        from jax.scipy.linalg import expm
        N, D, COND_DIM = (144, 64, 144)
        B, T = (16, 128)

        def _rotation(cond, W, b):
            v = jax.nn.silu(cond) @ W.T + b
            iu, ju = jnp.triu_indices(D, k=1)
            A = jnp.zeros((cond.shape[0], D, D), dtype=v.dtype)
            A = A.at[:, iu, ju].set(v).at[:, ju, iu].set(-v)
            return expm(A)
        key = jax.random.key(seed)
        k1, k2, k3, k4, k5 = jax.random.split(key, 5)
        x = jax.random.normal(k1, (B, T, N), dtype=jnp.float32)
        cond = jax.random.normal(k2, (B, COND_DIM), dtype=jnp.float32)
        P = jax.random.normal(k3, (N, D), dtype=jnp.float32)
        n_skew = D * (D - 1) // 2
        bound = 1.0 / np.sqrt(COND_DIM)
        W = jax.random.uniform(k4, (n_skew, COND_DIM), minval=-bound, maxval=bound, dtype=jnp.float32)
        b = jax.random.uniform(k5, (n_skew,), minval=-bound, maxval=bound, dtype=jnp.float32)
        return {'x': x, 'cond': cond, 'P': P, 'W': W, 'b': b}
    _L2_cond_all = _L2_cond_setup()
    _L2_cond_in = {k: v for k, v in _L2_cond_all.items() if k in ('P', 'W', 'b')}
    del _L2_cond_all

    def _L3_cond_setup():
        import jax, jax.numpy as jnp
        import numpy as np
        NUM_HEADS = 16
        NUM_EXPERTS = 4
        TOP_K = 2
        LN_EPS = 1e-06

        def _ln(h):
            mu = jnp.mean(h, axis=-1, keepdims=True)
            var = jnp.var(h, axis=-1, keepdims=True)
            return (h - mu) * jax.lax.rsqrt(var + LN_EPS)

        def _modulate(h, shift, scale):
            return h * (1.0 + scale[:, None, :]) + shift[:, None, :]
        key = jax.random.key(seed)
        ks = jax.random.split(key, 12)
        B, N, C = (8, 128, 144)
        H = 4 * C
        E = NUM_EXPERTS
        s = 0.02
        return {'x': jax.random.normal(ks[0], (B, N, C), jnp.float32), 'c': jax.random.normal(ks[1], (B, C), jnp.float32), 'w_adaln': jax.random.normal(ks[2], (C, 6 * C), jnp.float32) * s, 'b_adaln': jnp.zeros((6 * C,), jnp.float32), 'w_qkv': jax.random.normal(ks[3], (C, 3 * C), jnp.float32) * s, 'b_qkv': jnp.zeros((3 * C,), jnp.float32), 'w_proj': jax.random.normal(ks[4], (C, C), jnp.float32) * s, 'b_proj': jnp.zeros((C,), jnp.float32), 'w_gate': jax.random.normal(ks[5], (C, E), jnp.float32) * s, 'w1': jax.random.normal(ks[6], (E, C, H), jnp.float32) * s, 'b1': jnp.zeros((E, H), jnp.float32), 'w2': jax.random.normal(ks[7], (E, H, C), jnp.float32) * s, 'b2': jnp.zeros((E, C), jnp.float32)}
    _L3_cond_all = _L3_cond_setup()
    _L3_cond_in = {k: v for k, v in _L3_cond_all.items() if k in ('w_adaln', 'b_adaln', 'w_qkv', 'b_qkv', 'w_proj', 'b_proj', 'w_gate', 'w1', 'b1', 'w2', 'b2')}
    del _L3_cond_all
    return {'x': x, 'cond_1152': cond_1152, 'L0_cond_W_qkv': _L0_cond_in['W_qkv'], 'L0_cond_b_qkv': _L0_cond_in['b_qkv'], 'L0_cond_W_proj': _L0_cond_in['W_proj'], 'L0_cond_b_proj': _L0_cond_in['b_proj'], 'L0_cond_W_fc1': _L0_cond_in['W_fc1'], 'L0_cond_b_fc1': _L0_cond_in['b_fc1'], 'L0_cond_W_fc2': _L0_cond_in['W_fc2'], 'L0_cond_b_fc2': _L0_cond_in['b_fc2'], 'L0_cond_W_ada': _L0_cond_in['W_ada'], 'L0_cond_b_ada': _L0_cond_in['b_ada'], 'L1_cond_qkv_w': _L1_cond_in['qkv_w'], 'L1_cond_qkv_b': _L1_cond_in['qkv_b'], 'L1_cond_proj_w': _L1_cond_in['proj_w'], 'L1_cond_proj_b': _L1_cond_in['proj_b'], 'L1_cond_fc1_w': _L1_cond_in['fc1_w'], 'L1_cond_fc1_b': _L1_cond_in['fc1_b'], 'L1_cond_fc2_w': _L1_cond_in['fc2_w'], 'L1_cond_fc2_b': _L1_cond_in['fc2_b'], 'L1_cond_ada_w': _L1_cond_in['ada_w'], 'L1_cond_ada_b': _L1_cond_in['ada_b'], 'L2_cond_P': _L2_cond_in['P'], 'L2_cond_W': _L2_cond_in['W'], 'L2_cond_b': _L2_cond_in['b'], 'L3_cond_w_adaln': _L3_cond_in['w_adaln'], 'L3_cond_b_adaln': _L3_cond_in['b_adaln'], 'L3_cond_w_qkv': _L3_cond_in['w_qkv'], 'L3_cond_b_qkv': _L3_cond_in['b_qkv'], 'L3_cond_w_proj': _L3_cond_in['w_proj'], 'L3_cond_b_proj': _L3_cond_in['b_proj'], 'L3_cond_w_gate': _L3_cond_in['w_gate'], 'L3_cond_w1': _L3_cond_in['w1'], 'L3_cond_b1': _L3_cond_in['b1'], 'L3_cond_w2': _L3_cond_in['w2'], 'L3_cond_b2': _L3_cond_in['b2']}

def reference(x, cond_1152, L0_cond_W_qkv, L0_cond_b_qkv, L0_cond_W_proj, L0_cond_b_proj, L0_cond_W_fc1, L0_cond_b_fc1, L0_cond_W_fc2, L0_cond_b_fc2, L0_cond_W_ada, L0_cond_b_ada, L1_cond_qkv_w, L1_cond_qkv_b, L1_cond_proj_w, L1_cond_proj_b, L1_cond_fc1_w, L1_cond_fc1_b, L1_cond_fc2_w, L1_cond_fc2_b, L1_cond_ada_w, L1_cond_ada_b, L2_cond_P, L2_cond_W, L2_cond_b, L3_cond_w_adaln, L3_cond_b_adaln, L3_cond_w_qkv, L3_cond_b_qkv, L3_cond_w_proj, L3_cond_b_proj, L3_cond_w_gate, L3_cond_w1, L3_cond_b1, L3_cond_w2, L3_cond_b2):
    import jax
    import jax.numpy as jnp

    def _L0_cond_ref(x, c, W_qkv, b_qkv, W_proj, b_proj, W_fc1, b_fc1, W_fc2, b_fc2, W_ada, b_ada):
        import jax, jax.numpy as jnp
        import numpy as np
        B, L, C = (8, 128, 144)
        H = 16
        D = C // H
        FF = int(C * 4.0)
        EPS = 1e-06

        def _layernorm(x):
            mu = jnp.mean(x, axis=-1, keepdims=True)
            var = jnp.mean(jnp.square(x - mu), axis=-1, keepdims=True)
            return (x - mu) * jax.lax.rsqrt(var + EPS)

        def _modulate(x, shift, scale):
            return x * (1.0 + scale) + shift

        def _attention(h, W_qkv, b_qkv, W_proj, b_proj):
            b, l, c = h.shape
            qkv = h @ W_qkv + b_qkv
            qkv = qkv.reshape(b, l, 3, H, D)
            q, k, v = (qkv[:, :, 0], qkv[:, :, 1], qkv[:, :, 2])
            scale = D ** (-0.5)
            scores = jnp.einsum('blhd,bmhd->bhlm', q * scale, k)
            attn = jax.nn.softmax(scores, axis=-1)
            o = jnp.einsum('bhlm,bmhd->blhd', attn, v).reshape(b, l, c)
            return o @ W_proj + b_proj
        ada = jax.nn.silu(c) @ W_ada + b_ada
        shift_msa, scale_msa, gate_msa, shift_mlp, scale_mlp, gate_mlp = jnp.split(ada, 6, axis=-1)
        h = _modulate(_layernorm(x), shift_msa, scale_msa)
        x = x + gate_msa * _attention(h, W_qkv, b_qkv, W_proj, b_proj)
        h = _modulate(_layernorm(x), shift_mlp, scale_mlp)
        mlp = jax.nn.gelu(h @ W_fc1 + b_fc1, approximate=True) @ W_fc2 + b_fc2
        x = x + gate_mlp * mlp
        return x

    def _L1_cond_ref(x, c, qkv_w, qkv_b, proj_w, proj_b, fc1_w, fc1_b, fc2_w, fc2_b, ada_w, ada_b):
        import jax, jax.numpy as jnp
        import numpy as np
        N, T, D, H = (32, 128, 144, 16)
        DH = D // H
        MLP = int(D * 4.0)
        EPS = 1e-06

        def _layernorm(x):
            m = jnp.mean(x, axis=-1, keepdims=True)
            v = jnp.var(x, axis=-1, keepdims=True)
            return (x - m) * jax.lax.rsqrt(v + EPS)

        def _modulate(x, shift, scale):
            return x * (1.0 + scale[:, None, :]) + shift[:, None, :]

        def _attention(x, qkv_w, qkv_b, proj_w, proj_b):
            n, t, d = x.shape
            scale = DH ** (-0.5)
            qkv = x @ qkv_w + qkv_b
            qkv = qkv.reshape(n, t, 3, H, DH)
            q, k, v = (qkv[:, :, 0], qkv[:, :, 1], qkv[:, :, 2])
            attn = jnp.einsum('nthd,ntkd->nthk', q * scale, k)
            attn = jax.nn.softmax(attn, axis=-1)
            out = jnp.einsum('nthk,ntkd->nthd', attn, v)
            out = out.transpose(0, 2, 1, 3).reshape(n, t, d)
            return out @ proj_w + proj_b

        def _mlp(x, fc1_w, fc1_b, fc2_w, fc2_b):
            h = jax.nn.gelu(x @ fc1_w + fc1_b, approximate=False)
            return h @ fc2_w + fc2_b
        ada = jax.nn.silu(c) @ ada_w + ada_b
        shift_msa, scale_msa, gate_msa, shift_mlp, scale_mlp, gate_mlp = jnp.split(ada, 6, axis=1)
        x = x + gate_msa[:, None, :] * _attention(_modulate(_layernorm(x), shift_msa, scale_msa), qkv_w, qkv_b, proj_w, proj_b)
        x = x + gate_mlp[:, None, :] * _mlp(_modulate(_layernorm(x), shift_mlp, scale_mlp), fc1_w, fc1_b, fc2_w, fc2_b)
        return x

    def _L2_cond_ref(x, cond, P, W, b):
        import jax, jax.numpy as jnp
        import numpy as np
        from jax.scipy.linalg import expm
        N, D, COND_DIM = (144, 64, 144)
        B, T = (16, 128)

        def _rotation(cond, W, b):
            v = jax.nn.silu(cond) @ W.T + b
            iu, ju = jnp.triu_indices(D, k=1)
            A = jnp.zeros((cond.shape[0], D, D), dtype=v.dtype)
            A = A.at[:, iu, ju].set(v).at[:, ju, iu].set(-v)
            return expm(A)
        U, _ = jnp.linalg.qr(P)
        R = _rotation(cond, W, b)
        z = jnp.einsum('btn,nd->btd', x, U)
        z_rot = jnp.einsum('btd,bde->bte', z, R)
        x_rot = x + jnp.einsum('btd,nd->btn', z_rot - z, U)
        return x_rot

    def _L3_cond_ref(x, c, w_adaln, b_adaln, w_qkv, b_qkv, w_proj, b_proj, w_gate, w1, b1, w2, b2):
        import jax, jax.numpy as jnp
        import numpy as np
        NUM_HEADS = 16
        NUM_EXPERTS = 4
        TOP_K = 2
        LN_EPS = 1e-06

        def _ln(h):
            mu = jnp.mean(h, axis=-1, keepdims=True)
            var = jnp.var(h, axis=-1, keepdims=True)
            return (h - mu) * jax.lax.rsqrt(var + LN_EPS)

        def _modulate(h, shift, scale):
            return h * (1.0 + scale[:, None, :]) + shift[:, None, :]
        B, N, C = x.shape
        nh = NUM_HEADS
        hd = C // nh
        mod = jax.nn.silu(c) @ w_adaln + b_adaln
        sh_msa, sc_msa, g_msa, sh_mlp, sc_mlp, g_mlp = jnp.split(mod, 6, axis=-1)
        h = _modulate(_ln(x), sh_msa, sc_msa)
        qkv = (h @ w_qkv + b_qkv).reshape(B, N, 3, nh, hd).transpose(2, 0, 3, 1, 4)
        q, k, v = (qkv[0], qkv[1], qkv[2])
        attn = jax.nn.softmax(jnp.einsum('bhqd,bhkd->bhqk', q, k) * hd ** (-0.5), axis=-1)
        o = jnp.einsum('bhqk,bhkd->bhqd', attn, v).transpose(0, 2, 1, 3).reshape(B, N, C)
        o = o @ w_proj + b_proj
        x = x + g_msa[:, None, :] * o
        xn = _modulate(_ln(x), sh_mlp, sc_mlp)
        xf = xn.reshape(-1, C)
        gate_logits = xf @ w_gate
        topk_logits, topk_idx = jax.lax.top_k(gate_logits, TOP_K)
        gates = jax.nn.softmax(topk_logits, axis=-1)
        cw = jnp.sum(jax.nn.one_hot(topk_idx, NUM_EXPERTS, dtype=xf.dtype) * gates[..., None], axis=1)
        hmid = jax.nn.gelu(jnp.einsum('tc,ech->eth', xf, w1) + b1[:, None, :], approximate=True)
        eo = jnp.einsum('eth,ehc->etc', hmid, w2) + b2[:, None, :]
        moe = jnp.einsum('te,etc->tc', cw, eo).reshape(B, N, C)
        return x + g_mlp[:, None, :] * moe
    x = _L0_cond_ref(x, cond_1152[:, None, :], L0_cond_W_qkv, L0_cond_b_qkv, L0_cond_W_proj, L0_cond_b_proj, L0_cond_W_fc1, L0_cond_b_fc1, L0_cond_W_fc2, L0_cond_b_fc2, L0_cond_W_ada, L0_cond_b_ada)
    x = _L1_cond_ref(x, cond_1152, L1_cond_qkv_w, L1_cond_qkv_b, L1_cond_proj_w, L1_cond_proj_b, L1_cond_fc1_w, L1_cond_fc1_b, L1_cond_fc2_w, L1_cond_fc2_b, L1_cond_ada_w, L1_cond_ada_b)
    x = _L2_cond_ref(x, cond_1152, L2_cond_P, L2_cond_W, L2_cond_b)
    x = _L3_cond_ref(x, cond_1152, L3_cond_w_adaln, L3_cond_b_adaln, L3_cond_w_qkv, L3_cond_b_qkv, L3_cond_w_proj, L3_cond_b_proj, L3_cond_w_gate, L3_cond_w1, L3_cond_b1, L3_cond_w2, L3_cond_b2)
    return x

_drawn_inputs = setup_inputs


def setup_inputs(seed=0):
    import zlib

    import numpy as np

    out = dict(_drawn_inputs(seed))
    spreads = {'L0_cond_b_qkv': (0.0, 0.8),
     'L0_cond_b_proj': (0.0, 0.475),
     'L0_cond_b_fc1': (0.0, 0.8),
     'L0_cond_b_fc2': (0.0, 0.512),
     'L0_cond_b_ada': (0.0, 0.5),
     'L3_cond_b_adaln': (0.0, 0.525),
     'L3_cond_b_qkv': (0.0, 0.8),
     'L3_cond_b_proj': (0.0, 0.402),
     'L3_cond_b1': (0.0, 0.8),
     'L3_cond_b2': (0.0, 0.619)}
    factors = {'L0_cond_W_qkv': 8.0,
     'L0_cond_W_proj': 8.0,
     'L0_cond_W_fc1': 5.455,
     'L0_cond_W_fc2': 5.111,
     'L0_cond_W_ada': 2.734,
     'L1_cond_qkv_w': 8.0,
     'L1_cond_qkv_b': 8.0,
     'L1_cond_proj_w': 8.0,
     'L1_cond_proj_b': 8.0,
     'L1_cond_fc1_w': 6.698,
     'L1_cond_fc1_b': 8.0,
     'L1_cond_fc2_w': 6.487,
     'L1_cond_fc2_b': 8.0,
     'L1_cond_ada_w': 5.586,
     'L1_cond_ada_b': 8.0,
     'L3_cond_w_adaln': 2.793,
     'L3_cond_w_qkv': 8.0,
     'L3_cond_w_proj': 8.0,
     'L3_cond_w_gate': 5.119,
     'L3_cond_w1': 7.089,
     'L3_cond_w2': 6.541}
    for name, (base, spread) in spreads.items():
        noise = np.random.default_rng([zlib.crc32(name.encode()), seed]).standard_normal(out[name].shape)
        drawn = base * np.exp(spread * noise) if base else spread * noise
        out[name] = jnp.asarray(drawn.astype(out[name].dtype))
    for name, factor in factors.items():
        out[name] = (out[name] * factor).astype(out[name].dtype)
    return out
```

```python
from contextlib import ExitStack

import concourse.bass as bass
from concourse import mybir
from concourse.alu_op_type import AluOpType as ALU

F32 = mybir.dt.float32
F32R = mybir.dt.float32r
ACT = mybir.ActivationFunctionType
AX = mybir.AxisListType
RED = bass.bass_isa.ReduceOp

B, L, C = 2, 512, 144
T = B * L // 128
H, D = 16, 9
FF = 4 * C
E = 4
NL = 3
TAIL = C - 128
ROT = 64
GR = 4
NG = H // GR
EPS = 1e-6
MC = [(0, 128), (128, 128), (256, 128), (384, 128), (512, 64)]

QC, KC, VC, PC, W1C = 0, 512, 1024, 1184, 1328
COLS = [W1C + FF, W1C + FF, W1C + E * FF + E]
GC = W1C + E * FF
NSQ = 16
TAYLOR = 12
PR, PN = C // 2, 2
AUG = ROT + C


def build(nc, t, out):
    with ExitStack() as ctx:
        def sb(name, shape, dt=F32):
            return ctx.enter_context(nc.sbuf_tensor(name, shape, dt))

        def sem(name):
            return ctx.enter_context(nc.semaphore(name))

        psum = ctx.enter_context(nc.psum_tensor("psum", [128, 8, 512], F32))

        ident = sb("ident", [128, 128])
        neg_lo = sb("neg_lo", [128, 4])
        silu_fix = sb("silu_fix", [17, 2])
        tri = sb("tri", [128, E, E])
        x = sb("x", [128, T, C])
        xe = sb("xe", [128, T, 224])
        tA = sb("tA", [128, B * L])
        tB = sb("tB", [96, B * L], F32R)
        q1 = sb("q1", [128, B * NG, 512], F32R)
        kE = sb("kE", [128, B * NG, 512], F32R)
        kO = sb("kO", [128, B * NG, 512], F32R)
        hi_tmp = sb("hi_tmp", [128, 2, 512], F32R)
        k_tmp = sb("k_tmp", [128, 2, 512], F32R)
        q2 = sb("q2", [128, 2, 512], F32R)
        ws = sb("ws", [128, 8192])
        Vh = ws[:, 0:4096].rearrange("p (t h d) -> p t h d", t=T, h=H)
        Pb = ws[:, 4096:8192].rearrange("p (n s q) -> p n s q", n=4, s=2)
        raw = ws[:, 4096:8192]
        mt = sb("mt", [128, 2, 512])
        nmx = sb("nmx", [128, 2, 16])
        mhi = sb("mhi", [128, 2, 16], F32R)
        oT = sb("oT", [128, 2, 512])
        tBf = oT[:].rearrange("p s q -> p (s q)")
        rden = sb("rden", [128, 16])
        G = sb("G", [128, B, 5, 512])
        Gf = G[:].rearrange("p b m q -> p (b m q)")
        adaA = [Gf[:, 2368 * s:2368 * s + 1184] for s in range(2)]
        adaB = [Gf[0:17, 2368 * s + 1184:2368 * s + 2368] for s in range(2)]
        skA, skB = ws[:, 0:4096], ws[0:17, 4096:8192]
        hq = Gf[:, 0:T * 3 * C].rearrange("p (t c) -> p t c", t=T)
        prod = [ws[:, k * H * H * D:(k + 1) * H * H * D] for k in range(3)]
        hden = ws[:, 6912:6912 + T * H].rearrange("p (t h) -> p t h", t=T)
        hmax = ws[:, 7040:7040 + 2 * H].rearrange("p (t h) -> p t h", t=2)
        tmp = sb("tmp", [128, 4, 2 * C])
        acc = tmp[:].rearrange("p n c -> p (n c)").rearrange("p (t c) -> p t c", c=C)
        WA = sb("WA", [128, COLS[2]])
        WB = sb("WB", [96, COLS[2]], F32R)
        W2 = sb("W2", [128, E, 5, C])
        cA = sb("cA", [128, 4, B])
        cB = sb("cB", [17, 4, B])
        srepA = sb("srepA", [128, B, 128])
        srepB = sb("srepB", [17, B, 128])
        mod = sb("mod", [128, NL, 4, 2, B])
        gates = sb("gates", [128, NL, B, 2 * C])
        stats = sb("stats", [128, T, 6])
        mv = sb("mv", [128, T, 2])
        rstd = sb("rstd", [128, T])
        vare = sb("vare", [128, T])
        power = sb("power", [128, T + 1])
        sgn = sb("sgn", [ROT, ROT])
        thr = sb("thr", [ROT, B, NSQ])
        skew = sb("skew", [ROT, B, ROT])
        skp = sb("skp", [ROT, B, 2, ROT])
        n1 = sb("n1", [ROT, 4, B])
        sq = sb("sq", [ROT, 3, B, NSQ])
        Rm = sb("Rm", [ROT, B, 2, ROT])
        Rk = sb("Rk", [ROT, B, 2, ROT])
        aug = sb("aug", [PR, PN, AUG])
        ge = sb("ge", [PR, PN, ROT])
        vm = sb("vm", [PR, PN])
        vs = sb("vs", [PR, PN])
        qs = sb("qs", [PR, 8])
        w1s = sb("w1s", [PR, AUG])
        us = sb("us", [PR, AUG])
        UTx = sb("UTx", [ROT, 224])
        RU = sb("RU", [ROT, B, C])
        MA = sb("MA", [128, B, C])
        MB = sb("MB", [96, B, C], F32R)
        hS = tBf.rearrange("p (n h k) -> p n h k", n=4, h=H)
        hO = tmp[:].rearrange("p n c -> p (n c)").rearrange("p (t c) -> p t c", c=C)
        MBf = tmp[0:96, 0, :].rearrange("p (b c) -> p b c", b=B)
        lg = sb("lg", [128, T, E])
        m1 = sb("m1", [128, T])
        ahead, tied = (mt[:, k, 0:T * E * E].rearrange("p (t e f) -> p t e f", t=T, e=E) for k in range(2))
        cnt = sb("cnt", [128, 2, T, E])
        cw = sb("cw", [128, T, E])
        den = sb("den", [128, T])

        filled = [sem(f"bank{k}_filled") for k in range(8)]
        drained = [sem(f"bank{k}_drained") for k in range(8)]
        const_in = sem("const_in")
        ada_in = [sem(f"ada{n}_in") for n in range(NL)]
        wa_in = sem("wa_in")
        raw_in = sem("raw_in")
        skew_in = sem("skew_in")
        x_in = sem("x_in")
        preset = sem("preset")
        silu_exp = sem("silu_exp")
        silu_done = sem("silu_done")
        wb_done = sem("wb_done")
        xe_nat = sem("xe_nat")
        xe_dup = sem("xe_dup")
        tB_done = sem("tB_done")
        hi_done = sem("hi_done")
        k_done = sem("k_done")
        mt_done = sem("mt_done")
        x_done = sem("x_done")
        x_final = sem("x_final")
        norm_max = sem("norm_max")
        rm_init = sem("rm_init")
        rm_less_one = sem("rm_less_one")
        rowsum = sem("rowsum")
        vm_done = sem("vm_done")
        sigma_out = sem("sigma_out")
        root_done = sem("root_done")
        var_done = sem("var_done")
        rstd_done = sem("rstd_done")
        kept_done = sem("kept_done")
        w1_done = sem("w1_done")
        ut_done = sem("ut_done")
        m_done = sem("m_done")
        lg_exp = sem("lg_exp")
        hprod_done = sem("hprod_done")
        hs_done = sem("hs_done")
        hp_done = sem("hp_done")
        ho_done = sem("ho_done")
        head_norm = sem("head_norm")
        lg_ready = sem("lg_ready")
        stored = sem("stored")
        dve_step = sem("dve_step")
        pool_step = sem("pool_step")

        ada_h = [t[f"ada{n}"] for n in range(NL)]
        block = ctx.enter_context(nc.Block())

        use = {}
        uses = [0] * 8

        def full(eng, job):
            k, n = use[job]
            eng.wait_ge(filled[k], n)
            return psum[:, k, :]

        def empty(job):
            return drained[use[job][0]]

        def evacuated(eng, job):
            k, n = use[job]
            eng.wait_ge(drained[k], n)

        def by_quarters(ap, s):
            return ap.rearrange("p (v u a) -> p a u v", v=4, u=4) if s == 3 else ap

        def in_order(ap, s):
            return ap.rearrange("p (a u v) -> p a u v", u=4, v=4) if s == 3 else ap

        @block.tensor
        def _(pe):
            def claim(job, k):
                if uses[k]:
                    pe.wait_ge(drained[k], uses[k])
                uses[k] += 1
                use[job] = (k, uses[k])
                return psum[:, k, :]

            def tail_mm(o, lhsT, rhs, stop=True):
                return pe.matmul(o, lhsT, rhs, start=False, stop=stop)

            pe.wait_ge(const_in, 16 * 7)
            pe.wait_ge(silu_done, 1)
            for n in range(NL):
                pe.wait_ge(ada_in[n], 32)
                o = claim(("ada", n), 0)
                for kind in range(4):
                    for ab, (c0, m) in enumerate(((0, 128), (128, 96))):
                        at = (kind * 2 + ab) * B
                        c = kind * 224 + c0
                        pe.matmul(o[0:m, at:at + B], adaA[n % 2][:, c:c + m], cA[:, 3, :], start=True, stop=False)
                        last = tail_mm(o[0:m, at:at + B], adaB[n % 2][:, c:c + m], cB[:, 3, :])
                last.then_inc(filled[0], 1)
                for b in range(B):
                    o = claim(("gate", n, b), 1 + b)
                    pe.matmul(o[:, 0:2 * C], srepA[:, b, :], adaA[n % 2][:, 896:1184], start=True, stop=False)
                    tail_mm(o[:, 0:2 * C], srepB[:, b, :], adaB[n % 2][:, 896:1184]).then_inc(filled[1 + b], 1)

            pe.wait_ge(skew_in, 32)
            o = claim("skew", 3)
            for j in range(ROT):
                pe.matmul(o[0:ROT, 2 * j:2 * j + 2], skA[:, j * ROT:(j + 1) * ROT], cA[:, 3, :], start=True, stop=False)
                last = tail_mm(o[0:ROT, 2 * j:2 * j + 2], skB[:, j * ROT:(j + 1) * ROT], cB[:, 3, :])
            last.then_inc(filled[3], 1)

            for k in range(TAYLOR):
                if k == 0:
                    pe.wait_ge(rm_init, 1)
                o = claim(("taylor", k), 4)
                for b in range(B):
                    for s in range(2):
                        at = (2 * b + s) * ROT
                        last = pe.matmul(o[0:ROT, at:at + ROT], skp[:, b, s, :], Rm[:, b, s, :], start=True, stop=True)
                last.then_inc(filled[4], 1)
            for k in range(NSQ):
                o = claim(("square", k), 4)
                for b in range(B):
                    for s in range(2):
                        at = (2 * b + s) * ROT
                        last = pe.matmul(o[0:ROT, at:at + ROT], Rm[:, b, 1 - s, :], Rm[:, b, s, :], start=True, stop=True)
                last.then_inc(filled[4], 1)

            for i in range(ROT):
                pe.wait_ge(vm_done, i + 1)
                o = claim(("house", i), 5)
                for c in range(PN):
                    pe.matmul(o[0:PR, 0:AUG], vm[:, c:c + 1].broadcast_to([PR, PR]), aug[:, c, :],
                              start=(c == 0), stop=(c == PN - 1))
                pe.matmul(o[0:PR, AUG:2 * AUG], ident[0:PR, i:i + 1].broadcast_to([PR, PR]), aug[:, 0, :],
                          start=True, stop=True).then_inc(filled[5], 1)

            pe.wait_ge(ut_done, 1)
            pe.wait_ge(rm_less_one, 1)
            o = claim("RU", 6)
            for b in range(B):
                last = pe.matmul(o[0:ROT, b * C:(b + 1) * C], Rm[:, b, 1, :], UTx[:, 0:C], start=True, stop=True)
            last.then_inc(filled[6], 1)
            evacuated(pe, "RU")
            for b in range(B):
                o = claim(("MA", b), 6)
                pe.matmul(o[:, 0:C], UTx[:, 0:128], RU[:, b, :], start=True, stop=True)
                pe.matmul(o[0:96, C:2 * C], UTx[:, 128:224], RU[:, b, :], start=True, stop=True).then_inc(filled[6], 1)

            def to_features(s):
                for half in range(2):
                    pe.wait_ge(xe_dup, 2 * (2 * s + half + 1))
                    o = claim(("tA", s, half), 2 * half)
                    for j in range(4):
                        last = pe.transpose(o[:, j * 128:(j + 1) * 128], xe[:, 4 * half + j, 0:128], ident[:])
                    last.then_inc(filled[2 * half], 1)
                    o = claim(("tB", s, half), 2 * half + 1)
                    for j in range(4):
                        last = pe.transpose(o[0:96, j * 128:(j + 1) * 128], xe[:, 4 * half + j, 128:224], ident[:])
                    last.then_inc(filled[2 * half + 1], 1)

            def ready(s, half):
                evacuated(pe, ("tA", s, half))
                pe.wait_ge(tB_done, 2 * s + half + 1)

            def token_major(name, s, wa, wb, width, banks):
                for pair in range(T // 2):
                    if pair % 2 == 0:
                        ready(s, pair // 2)
                    k = banks[pair % len(banks)]
                    o = claim((*name, pair), k)
                    for j in range(2):
                        tok = slice((2 * pair + j) * 128, (2 * pair + j + 1) * 128)
                        pe.matmul(o[:, j * width:(j + 1) * width], tA[:, tok], wa(pair // 2), start=True, stop=False)
                        last = tail_mm(o[:, j * width:(j + 1) * width], tB[:, tok], wb(pair // 2))
                    last.then_inc(filled[k], 1)

            def st_mm(n, i, kb):
                if kb == 0:
                    evacuated(pe, ("mt", n, i))
                for pr, kx in ((0, kE), (1, kO)):
                    claim(("st", n, i, kb, pr), 2 * pr)
                    for s in range(2):
                        rows = slice(64 * s, 64 * s + 64)
                        last = pe.matmul(psum[:, 2 * pr + s, :], kx[rows, i, kb * 128:(kb + 1) * 128],
                                         q2[rows, i % 2, :], start=True, stop=True)
                    last.then_inc(filled[2 * pr], 1)

            def pv_mm(n, i, kb):
                if kb == 0:
                    claim(("pv", n, i), 6)
                unit = ((n // 2 * 8 + i) * 4 + kb) * 2
                for pr in range(2):
                    evacuated(pe, ("st", n, i, kb, pr))
                for c in range(GR):
                    pr, s = c % 2, c // 2
                    last = pe.matmul(psum[32 * c:32 * c + 32, 6, :], Vh[:, (i // NG) * 4 + kb, (i % NG) * GR + c, :],
                                     Pb[:, (unit + pr) % 4, s, :], start=(kb == 0), stop=(kb == 3))
                if kb == 3:
                    last.then_inc(filled[6], 1)

            def mx_mm(n, i, qt):
                for j, c in enumerate((0, 2, 1, 3)):
                    kx = kE if c % 2 == 0 else kO
                    rows = slice(64 * (c // 2), 64 * (c // 2) + 64)
                    k = 4 + j % 2
                    o = claim(("mx", n, i, qt, c), k)
                    pe.matmul(o, q1[rows, i, qt * 128:(qt + 1) * 128], kx[rows, i, :],
                              start=True, stop=True).then_inc(filled[k], 1)

            def mt_mm(n, i):
                pe.wait_ge(mt_done, 2 * (n // 2 * 8 + i + 1))
                o = claim(("mt", n, i), 7)
                for qt in range(4):
                    last = pe.transpose(o[:, qt * 128:(qt + 1) * 128], mt[:, i % 2, qt * 128:(qt + 1) * 128], ident[:])
                last.then_inc(filled[7], 1)

            def ot_mm(n, i):
                evacuated(pe, ("pv", n, i))
                o = claim(("ot", n, i), 7)
                for qt in range(4):
                    last = pe.transpose(o[:, qt * 128:(qt + 1) * 128], oT[:, i % 2, qt * 128:(qt + 1) * 128], ident[:])
                last.then_inc(filled[7], 1)

            def hidden(n, e, b, s):
                ready(s, b)
                for m, (c0, w) in enumerate(MC):
                    k = m % 4
                    o = claim(("f1", n, e, b, m), k)
                    c = W1C + e * FF + c0
                    pe.matmul(o[0:w, :], WA[:, c:c + w], tA[:, b * L:(b + 1) * L], start=True, stop=False)
                    tail_mm(o[0:w, :], WB[:, c:c + w], tB[:, b * L:(b + 1) * L]).then_inc(filled[k], 1)

            def back(n, e, b):
                for m in range(1, 5):
                    evacuated(pe, ("f1", n, e, b, m))
                for pair in range(2):
                    k = 4 + (2 * b + pair) % 4
                    o = claim(("f2", n, e, 2 * b + pair), k)
                    for j in range(2):
                        tok = slice((2 * pair + j) * 128, (2 * pair + j + 1) * 128)
                        for m, (c0, w) in enumerate(MC):
                            w += m == 4
                            last = pe.matmul(o[:, j * C:(j + 1) * C], G[0:w, b, m, tok], W2[0:w, e, m, :],
                                             start=(m == 0), stop=(m == 4))
                    last.then_inc(filled[k], 1)

            def attention_mm(n, s):
                token_major(("v", n), s, lambda b: WA[:, VC:VC + 160], lambda b: WB[:, VC:VC + 160], 160, [4, 5, 6, 7])
                for i in range(B * NG):
                    b, g = divmod(i, NG)
                    for part, c0 in ((0, QC), (1, KC)):
                        k = (2 * i + part) % 8
                        o = claim(("qk", n, i, part), k)
                        c = c0 + g * 128
                        pe.matmul(o, WA[:, c:c + 128], tA[:, b * L:(b + 1) * L], start=True, stop=False)
                        tail_mm(o, WB[:, c:c + 128], tB[:, b * L:(b + 1) * L]).then_inc(filled[k], 1)
                for pair in range(T // 2):
                    evacuated(pe, ("v", n, pair))
                if n == 2:
                    pe.wait_ge(preset, 12)
                for i in range(-1, B * NG):
                    if i + 1 < B * NG:
                        evacuated(pe, ("qk", n, i + 1, 0))
                        pe.wait_ge(k_done, 2 * (n // 2 * 8 + i + 2))
                    for kb in range(4):
                        if i >= 0:
                            st_mm(n, i, kb)
                        if i + 1 < B * NG:
                            mx_mm(n, i + 1, kb)
                        if i >= 0 and kb >= 1:
                            pv_mm(n, i, kb - 1)
                        if i >= 1 and kb == 0:
                            pv_mm(n, i - 1, 3)
                        if i >= 1 and kb == 1:
                            ot_mm(n, i - 1)
                    if i + 1 < B * NG:
                        mt_mm(n, i + 1)
                pv_mm(n, B * NG - 1, 3)
                ot_mm(n, B * NG - 1)

            for n in range(NL):
                s = [0, 3, 7][n]
                to_features(s)
                pe.wait_ge(wa_in, 32 * (n + 1))
                pe.wait_ge(wb_done, n + 1)
                if n == 1:
                    for j in range(T):
                        b, v = divmod(j, 4)
                        if v == 0:
                            ready(s, b)
                        o = claim(("hqkv", j), j)
                        tok = slice(j * 128, (j + 1) * 128)
                        pe.matmul(o[:, 0:3 * C], tA[:, tok], WA[:, 0:3 * C], start=True, stop=False)
                        tail_mm(o[:, 0:3 * C], tB[:, tok], WB[:, 0:3 * C]).then_inc(filled[j], 1)
                else:
                    attention_mm(n, s)
                to_features(s + 1)
                token_major(("proj", n), s + 1, lambda b: WA[:, PC:PC + C], lambda b: WB[:, PC:PC + C], C, [4, 5, 6, 7])
                to_features(s + 2)
                if n == NL - 1:
                    o = claim("logits", 7)
                    for tt in range(T):
                        ready(s + 2, tt // 4)
                        tok = slice(tt * 128, (tt + 1) * 128)
                        pe.matmul(o[:, tt * E:(tt + 1) * E], tA[:, tok], WA[:, GC:GC + E], start=True, stop=False)
                        last = tail_mm(o[:, tt * E:(tt + 1) * E], tB[:, tok], WB[:, GC:GC + E])
                    last.then_inc(filled[7], 1)
                if n == 1:
                    pe.wait_ge(preset, 11)
                for e in range(E if n == NL - 1 else 1):
                    for b in range(B):
                        hidden(n, e, b, s + 2)
                        if b == 1:
                            back(n, e, 0)
                    back(n, e, 1)
                if n == 1:
                    to_features(6)
                    pe.wait_ge(m_done, 2)
                    token_major(("rot",), 6, lambda b: MA[:, b, :], lambda b: MB[:, b, :], C, [4, 5, 6, 7])

        @block.sync
        def _(sp):
            for name, dst in (("ident", ident[:]), ("neg_lo", neg_lo[:]), ("silu_fix", silu_fix[:]), ("tri", tri[:]),
                              ("condA", cA[:, 0, :]), ("condB", cB[:, 0, :]), ("thr", thr[:])):
                sp.dma_start(dst, t[name]).then_inc(const_in, 16)
            for n in range(NL):
                if n == 2:
                    for b in range(B):
                        evacuated(sp, ("gate", 0, b))
                sp.dma_start(adaA[n % 2], ada_h[n][0:128, :]).then_inc(ada_in[n], 16)
                sp.dma_start(adaB[n % 2], ada_h[n][128:145, :]).then_inc(ada_in[n], 16)
                if n == 0:
                    sp.dma_start(skA, t["skew_w"][0:128, :]).then_inc(skew_in, 16)
                    sp.dma_start(skB, t["skew_w"][128:145, :]).then_inc(skew_in, 16)
                    for name, dst in (("sgn", sgn[:]), ("aug", aug[:]), ("ge", ge[:]),
                                      ("x", x[:])):
                        src = t[name].rearrange("(t p) c -> p t c", p=128) if name == "x" else t[name]
                        sp.dma_start(dst, src).then_inc(x_in, 16)
            evacuated(sp, "skew")
            for n in range(NL):
                if n:
                    sp.wait_ge(x_done, 8 * n)
                sp.dma_start(raw[0:96, 0:COLS[n]], t[f"wb{n}"]).then_inc(raw_in, 16)
                sp.dma_start(WA[:, 0:COLS[n]], t[f"wa{n}"]).then_inc(wa_in, 16)
                ne = E if n == NL - 1 else 1
                sp.dma_start(W2[:, 0:ne, :, :], t[f"w2{n}"]).then_inc(wa_in, 16)
            for pair in range(T // 2):
                sp.wait_ge(x_final, pair + 1)
                sp.dma_start(out.rearrange("(t p) c -> p t c", p=128)[:, 2 * pair:2 * pair + 2, :],
                             x[:, 2 * pair:2 * pair + 2, :]).then_inc(stored, 16)
            sp.wait_ge(stored, 16 * (T // 2))

        @block.vector
        def _(dve):
            steps = [0]

            def then(ins):
                steps[0] += 1
                ins.then_inc(dve_step, 1)
                dve.wait_ge(dve_step, steps[0])

            dve.memset(mt[:], 0.0).then_inc(preset, 1)
            dve.memset(xe[:], 0.0).then_inc(preset, 1)
            dve.wait_ge(preset, 2)
            for k in range(3):
                at = 128 + 32 * k + TAIL
                dve.memset(xe[:, :, at:at + 1], 1.0).then_inc(preset, 1)
            dve.memset(UTx[:], 0.0).then_inc(preset, 1)
            dve.memset(power[:, 0:T], -0.5).then_inc(preset, 1)
            dve.memset(power[:, T:T + 1], 0.5).then_inc(preset, 1)
            dve.wait_ge(preset, 8)

            dve.wait_ge(silu_exp, 2)
            dve.tensor_scalar(cA[:, 2, :], cA[:, 1, :], 1.0, None, ALU.add)
            then(dve.tensor_scalar(cB[:, 2, :], cB[:, 1, :], 1.0, None, ALU.add))
            dve.reciprocal(cA[:, 2, :], cA[:, 2, :])
            then(dve.reciprocal(cB[:, 2, :], cB[:, 2, :]))
            dve.tensor_tensor(cA[:, 3, :], cA[:, 0, :], cA[:, 2, :], ALU.mult)
            then(dve.tensor_tensor(cB[:, 2, :], cB[:, 0, :], cB[:, 2, :], ALU.mult))
            then(dve.tensor_scalar(cB[:, 3, :], cB[:, 2, :], silu_fix[:, 0:1], silu_fix[:, 1:2], ALU.mult, ALU.add))
            dve.tensor_copy(srepA[:], cA[:, 3, :].unsqueeze(2).broadcast_to([128, B, 128]))
            dve.tensor_copy(srepB[:], cB[:, 3, :].unsqueeze(2).broadcast_to([17, B, 128])).then_inc(silu_done, 1)

            for n in range(NL):
                v = full(dve, ("ada", n))[:, 0:16].rearrange("p (k a b) -> p k a b", k=4, a=2)
                for kind in range(4):
                    dve.tensor_scalar(mod[:, n, kind, 0, :], v[:, kind, 0, :], float(kind % 2), None, ALU.add)
                    ins = dve.tensor_scalar(mod[0:96, n, kind, 1, :], v[0:96, kind, 1, :], float(kind % 2), None, ALU.add)
                ins.then_inc(empty(("ada", n)), 1)
                for b in range(B):
                    o = full(dve, ("gate", n, b))
                    dve.tensor_copy(gates[:, n, b, :], o[:, 0:2 * C]).then_inc(empty(("gate", n, b)), 1)

            dve.wait_ge(x_in, 64)
            o = full(dve, "skew")
            for b in range(B):
                ins = dve.tensor_tensor(skew[:, b, :], o[0:ROT, b:2 * ROT:2], sgn[:], ALU.mult)
            ins.then_inc(empty("skew"), 1)
            evacuated(dve, "skew")
            dve.tensor_reduce(n1[:, 0, :], skew[:], AX.X, ALU.add, apply_absolute_value=True).then_inc(rowsum, 1)
            dve.wait_ge(norm_max, 1)
            then(dve.tensor_tensor(sq[:, 0], n1[:, 1, :].unsqueeze(2).broadcast_to([ROT, B, NSQ]), thr[:], ALU.is_gt))
            dve.tensor_scalar(sq[:, 1], sq[:, 0], -1.0, 1.0, ALU.mult, ALU.add)
            then(dve.tensor_scalar(sq[:, 2], sq[:, 0], -0.5, 1.0, ALU.mult, ALU.add))
            w = NSQ
            while w > 1:
                w //= 2
                then(dve.tensor_tensor(sq[:, 2, :, 0:w], sq[:, 2, :, 0:w], sq[:, 2, :, w:2 * w], ALU.mult))
            for b in range(B):
                then(dve.tensor_scalar(skp[:, b, 1, :], skew[:, b, :], sq[:, 2, b, 0:1], None, ALU.mult))
                dve.tensor_scalar(skp[:, b, 0, :], skp[:, b, 1, :], -1.0, None, ALU.mult)
            eye = ident[0:ROT, 0:ROT].unsqueeze(1).broadcast_to([ROT, 2 * B, ROT])
            Rm4 = Rm[:].rearrange("p b s n -> p (b s) n")
            dve.tensor_copy(Rm4, eye).then_inc(rm_init, 1)

            def kept(k):
                for b in range(B):
                    dve.tensor_scalar(Rk[:, b], Rm[:, b], sq[:, 1, b, k:k + 1], None, ALU.mult).then_inc(kept_done, 1)

            for k in range(TAYLOR):
                job = ("taylor", k)
                o = full(dve, job)[0:ROT, 0:4 * ROT].rearrange("p (a n) -> p a n", n=ROT)
                for a in range(2 * B):
                    ins = dve.scalar_tensor_tensor(Rm4[:, a, :], o[:, a, :], 1.0 / (TAYLOR - k), ident[0:ROT, 0:ROT], ALU.mult, ALU.add)
                ins.then_inc(empty(job), 1)
            for k in range(NSQ):
                evacuated(dve, ("taylor", TAYLOR - 1) if k == 0 else ("square", k - 1))
                kept(k)
                job = ("square", k)
                o = full(dve, job)
                dve.wait_ge(kept_done, B * (k + 1))
                for b in range(B):
                    ins = dve.scalar_tensor_tensor(Rm[:, b].rearrange("p s n -> p (s n)"), o[0:ROT, b * 128:(b + 1) * 128],
                                                   sq[:, 0, b, k:k + 1], Rk[:, b].rearrange("p s n -> p (s n)"), ALU.mult, ALU.add)
                ins.then_inc(empty(job), 1)
            evacuated(dve, ("square", NSQ - 1))
            for a in range(2 * B):
                ins = dve.tensor_tensor(Rm4[:, a, :], Rm4[:, a, :], ident[0:ROT, 0:ROT], ALU.subtract)
            ins.then_inc(rm_less_one, 1)

            for i in range(ROT):
                dve.tensor_tensor(vm[:], aug[:, :, i], ge[:, :, i], ALU.mult).then_inc(vm_done, 1)
                job = ("house", i)
                o = full(dve, job)
                sigma, alpha, root, sign2, beta, scl, negb = (qs[:, c:c + 1] for c in range(7))
                dve.tensor_copy(qs[:, 0:2], o[0:PR, i:i + AUG + 1:AUG]).then_inc(sigma_out, 1)
                dve.wait_ge(sigma_out, i + 1)
                then(dve.tensor_scalar(sign2, alpha, 0.0, -2.0, ALU.is_ge, ALU.mult))
                dve.wait_ge(root_done, i + 1)
                then(dve.tensor_scalar(beta, sign2, 1.0, root, ALU.add, ALU.mult))
                dve.tensor_scalar(negb, beta, -1.0, None, ALU.mult)
                then(dve.scalar_tensor_tensor(scl, alpha, beta, sigma, ALU.mult, ALU.subtract))
                then(dve.tensor_scalar(scl, scl, -1e-30, None, ALU.min))
                dve.reciprocal(scl, scl)
                then(dve.scalar_tensor_tensor(vm[:, 0:1], ident[0:PR, i:i + 1], negb, vm[:, 0:1], ALU.mult, ALU.add))
                dve.tensor_scalar(vs[:], vm[:], scl, -1.0, ALU.mult, ALU.mult)
                dve.wait_ge(w1_done, i + 1)
                dve.scalar_tensor_tensor(us[:], o[0:PR, AUG:2 * AUG], beta, w1s[:], ALU.mult, ALU.subtract).then_inc(empty(job), 1)
                evacuated(dve, job)
                for c in range(PN):
                    ins = dve.scalar_tensor_tensor(aug[:, c, :], us[:], vs[:, c:c + 1], aug[:, c, :], ALU.mult, ALU.add)
                then(ins)
            then(dve.tensor_copy(UTx[:, 0:C], aug[0:ROT, 0, ROT:AUG]))
            for k in range(1, 3):
                ins = dve.tensor_copy(UTx[:, 128 + 32 * k:128 + 32 * k + TAIL], UTx[:, 128:C])
            ins.then_inc(ut_done, 1)
            o = full(dve, "RU")
            dve.tensor_copy(RU[:].rearrange("p b c -> p (b c)"), o[0:ROT, 0:2 * C]).then_inc(empty("RU"), 1)
            for b in range(B):
                job = ("MA", b)
                o = full(dve, job)
                dve.tensor_copy(MA[:, b, :], o[:, 0:C])
                dve.tensor_copy(MB[:, b, :], o[0:96, C:2 * C])
                dve.tensor_copy(MBf[:, b, :], o[0:96, C:2 * C]).then_inc(empty(job), 1)
                evacuated(dve, job)
                dve.tensor_tensor(MB[64:96, b, :], MBf[64:96, b, :], MB[64:96, b, :].bitcast(F32), ALU.subtract).then_inc(m_done, 1)

            dve.memset(ws[:, 0:4096], 0.0).then_inc(preset, 1)
            dve.memset(G[64:65, :, 4, :], 1.0).then_inc(preset, 1)

            norms = [0]

            def layernorm(s):
                for tt in range(T):
                    ins = dve.bn_stats(stats[:, tt, :], x[:, tt, :])
                then(ins)
                for tt in range(T):
                    ins = dve.bn_aggr(mv[:, tt, :], stats[:, tt, :])
                then(ins)
                dve.tensor_scalar(vare[:], mv[:, :, 1], EPS, None, ALU.add).then_inc(var_done, 1)
                norms[0] += 1
                dve.wait_ge(rstd_done, norms[0])
                for tt in range(T):
                    dve.tensor_scalar(xe[:, tt, 0:C], x[:, tt, :], mv[:, tt, 0:1], rstd[:, tt:tt + 1],
                                      ALU.subtract, ALU.mult).then_inc(xe_nat, 1)

            def mains(s, n, kind):
                for half in range(2):
                    job = ("tA", s, half)
                    o = full(dve, job)
                    dst, o = by_quarters(tA[:, half * L:(half + 1) * L], s), in_order(o, s)
                    if kind is None:
                        ins = dve.tensor_copy(dst, o)
                    else:
                        ins = dve.tensor_scalar(dst, o, mod[:, n, kind + 1, 0, half:half + 1],
                                                mod[:, n, kind, 0, half:half + 1], ALU.mult, ALU.add)
                    ins.then_inc(empty(job), 1)

            sent = [0]

            def gated(name, n, which):
                for pair in range(T // 2):
                    job = (*name, pair)
                    o = full(dve, job)
                    if sent[0] >= 4:
                        dve.wait_ge(x_done, sent[0] - 3)
                    gt = gates[:, n, pair // 2, which * C:(which + 1) * C].unsqueeze(1).broadcast_to([128, 2, C])
                    dve.tensor_tensor(tmp[:, sent[0] % 4, :].rearrange("p (j c) -> p j c", j=2),
                                      o[:, 0:2 * C].rearrange("p (j c) -> p j c", j=2), gt, ALU.mult).then_inc(empty(job), 1)
                    sent[0] += 1

            def normalised(n, i):
                b, g = divmod(i, NG)
                job = ("ot", n, i)
                o = full(dve, job)
                then(dve.reciprocal(rden[:], o[:, D::32]))
                heads = o.rearrange("p (q c d) -> p q c d", q=4, c=GR)
                dst = xe[:, 4 * b:4 * b + 4, g * GR * D:(g + 1) * GR * D].rearrange("p q (c d) -> p q c d", c=GR)
                rd = rden[:].rearrange("p (q c) -> p q c", q=4)
                for qt in range(4):
                    ins = dve.tensor_tensor(dst[:, qt], heads[:, qt, :, 0:D], rd[:, qt].unsqueeze(2).broadcast_to([128, GR, D]), ALU.mult)
                ins.then_inc(empty(job), 1)

            def attention(n):
                for i in range(B * NG):
                    for part, dst in ((0, q1[:, i, :]), (1, k_tmp[:, i % 2, :])):
                        job = ("qk", n, i, part)
                        o = full(dve, job)
                        dve.wait_ge(hi_done, n // 2 * 16 + 2 * i + part + 1)
                        if part == 1 and n // 2 * 8 + i >= 2:
                            dve.wait_ge(k_done, 2 * (n // 2 * 8 + i - 1))
                        dve.scalar_tensor_tensor(dst, hi_tmp[:, part, :].bitcast(F32), neg_lo[:, part:part + 1], o,
                                                 ALU.mult, ALU.add).then_inc(empty(job), 1)
                for i in range(-1, B * NG):
                    for kb in range(4):
                        if i + 1 < B * NG:
                            for c in (0, 2, 1, 3):
                                job = ("mx", n, i + 1, kb, c)
                                o = full(dve, job)
                                dve.tensor_reduce(nmx[:, (i + 1) % 2, kb * 4 + c:kb * 4 + c + 1], o, AX.X, ALU.max,
                                                  negate=True).then_inc(empty(job), 1)
                        if i >= 1 and kb == 2:
                            normalised(n, i - 1)
                    if i + 1 < B * NG:
                        job = ("mt", n, i + 1)
                        o = full(dve, job)
                        dve.tensor_tensor(q2[:, (i + 1) % 2, :], q1[:, i + 1, :].bitcast(F32), o, ALU.add).then_inc(empty(job), 1)
                normalised(n, B * NG - 1)
                dve.wait_ge(empty(("ot", n, B * NG - 1)), use[("ot", n, B * NG - 1)][1])

            def heads():
                for j in range(T + 1):
                    if j < T:
                        S = hS[:, j % 4]
                        dve.wait_ge(hprod_done, j + 1)
                        if j >= 4:
                            dve.wait_ge(ho_done, j - 3)
                        then(dve.tensor_reduce(S, prod[j % 2].rearrange("p (h k d) -> p h k d", h=H, k=H), AX.X, ALU.add))
                        then(dve.tensor_reduce(hmax[:, j % 2], S, AX.X, ALU.max))
                        dve.tensor_tensor(S, S, hmax[:, j % 2].unsqueeze(2).broadcast_to([128, H, H]), ALU.subtract).then_inc(hs_done, 1)
                    if j >= 1:
                        t1 = j - 1
                        S = hS[:, t1 % 4]
                        dve.wait_ge(hp_done, t1 + 1)
                        dve.tensor_reduce(hden[:, t1], S, AX.X, ALU.add)
                        pv = prod[2].rearrange("p (h d k) -> p h d k", h=H, d=D)
                        vv = hq[:, t1, 2 * C:3 * C].rearrange("p (k d) -> p d k", k=H)
                        if t1:
                            dve.wait_ge(ho_done, t1)
                        then(dve.tensor_tensor(pv, S.unsqueeze(2).broadcast_to([128, H, D, H]),
                                               vv.unsqueeze(1).broadcast_to([128, H, D, H]), ALU.mult))
                        dve.reciprocal(hden[:, t1], hden[:, t1])
                        dve.tensor_reduce(hO[:, t1, :].rearrange("p (h d) -> p h d", h=H), pv, AX.X, ALU.add).then_inc(ho_done, 1)
                dve.wait_ge(ho_done, T)
                for b in range(B):
                    dst = xe[:, 4 * b:4 * b + 4, 0:C]
                    for u in range(4):
                        for hh in range(4):
                            fr, to = slice(32 * u, 32 * u + 32), slice(32 * hh, 32 * hh + 32)
                            src = hO[fr, 4 * b:4 * b + 4, :].rearrange("p v (g h d) -> p h g v d", h=4, d=D)[:, hh]
                            rd = hden[fr, 4 * b:4 * b + 4, :].rearrange("p v (g h) -> p h g v", h=4)[:, hh]
                            d = dst[to, :, 4 * u * D:4 * (u + 1) * D].rearrange("p g (v d) -> p g v d", v=4)
                            ins = dve.tensor_tensor(d, src, rd.unsqueeze(3).broadcast_to([32, 4, 4, D]), ALU.mult)
                    ins.then_inc(head_norm, 1)
                dve.wait_ge(head_norm, B)
                dve.memset(G[64:65, :, 4, :], 1.0).then_inc(preset, 1)
                dve.memset(ws[:, 0:4096], 0.0).then_inc(preset, 1)

            for n in range(NL):
                s = [0, 3, 7][n]
                if n == 1:
                    dve.wait_ge(x_done, 8)
                layernorm(s)
                mains(s, n, 0)
                if n == 1:
                    heads()
                else:
                    attention(n)
                mains(s + 1, n, None)
                gated(("proj", n), n, 0)
                dve.wait_ge(x_done, sent[0])
                layernorm(s + 2)
                mains(s + 2, n, 2)
                if n < NL - 1:
                    gated(("f2", n, 0), n, 1)
                    dve.wait_ge(x_done, sent[0])
                else:
                    o = full(dve, "logits")
                    dve.tensor_copy(lg[:].rearrange("p t e -> p (t e)"), o[:, 0:T * E]).then_inc(empty("logits"), 1)
                    evacuated(dve, "logits")
                    then(dve.tensor_reduce(m1[:], lg[:], AX.X, ALU.max))
                    other = lg[:].unsqueeze(2).broadcast_to([128, T, E, E])
                    own = lg[:].unsqueeze(3).broadcast_to([128, T, E, E])
                    dve.tensor_tensor(ahead, other, own, ALU.is_gt)
                    then(dve.tensor_tensor(tied, other, own, ALU.is_equal))
                    then(dve.tensor_tensor(tied, tied, tri[:].unsqueeze(1).broadcast_to([128, T, E, E]), ALU.mult))
                    then(dve.tensor_tensor(ahead, ahead, tied, ALU.add))
                    then(dve.tensor_reduce(cnt[:, 0], ahead, AX.X, ALU.add))
                    then(dve.tensor_scalar(cnt[:, 0], cnt[:, 0], 1.5, None, ALU.is_lt))
                    dve.tensor_tensor(cw[:], lg[:], m1[:].unsqueeze(2).broadcast_to([128, T, E]), ALU.subtract).then_inc(lg_ready, 1)
                    dve.wait_ge(lg_exp, 1)
                    then(dve.tensor_tensor(cw[:], cnt[:, 1], cnt[:, 0], ALU.mult))
                    then(dve.tensor_reduce(den[:], cw[:], AX.X, ALU.add))
                    then(dve.reciprocal(den[:], den[:]))
                    then(dve.tensor_tensor(cw[:], cw[:], den[:].unsqueeze(2).broadcast_to([128, T, E]), ALU.mult))
                    for e in range(E):
                        for pair in range(T // 2):
                            job = ("f2", n, e, pair)
                            o = full(dve, job)
                            for j in range(2):
                                tt = 2 * pair + j
                                if e == 0:
                                    ins = dve.tensor_scalar(acc[:, tt, :], o[:, j * C:(j + 1) * C], cw[:, tt, e:e + 1], None, ALU.mult)
                                else:
                                    ins = dve.scalar_tensor_tensor(acc[:, tt, :], o[:, j * C:(j + 1) * C], cw[:, tt, e:e + 1],
                                                                   acc[:, tt, :], ALU.mult, ALU.add)
                            ins.then_inc(empty(job), 1)
                            evacuated(dve, job)
                            if e == E - 1:
                                gt = gates[:, n, pair // 2, C:2 * C].unsqueeze(1).broadcast_to([128, 2, C])
                                xs, ac = x[:, 2 * pair:2 * pair + 2, :], acc[:, 2 * pair:2 * pair + 2, :]
                                then(dve.tensor_tensor(ac, ac, gt, ALU.mult))
                                dve.tensor_tensor(xs, xs, ac, ALU.add).then_inc(x_final, 1)
                if n == 1:
                    for tt in range(T):
                        dve.tensor_copy(xe[:, tt, 0:C], x[:, tt, :]).then_inc(xe_nat, 1)
                    mains(6, n, None)
                    for pair in range(T // 2):
                        job = ("rot", pair)
                        o = full(dve, job)
                        xs = x[:, 2 * pair:2 * pair + 2, :].rearrange("p t c -> p (t c)")
                        ins = dve.tensor_tensor(xs, xs, o[:, 0:2 * C], ALU.add).then_inc(empty(job), 1)
                    evacuated(dve, job)

        @block.scalar
        def _(act):
            act.wait_ge(const_in, 16 * 7)
            act.activation(cA[:, 1, :], cA[:, 0, :], ACT.Exp, scale=-1.0).then_inc(silu_exp, 1)
            act.activation(cB[:, 1, :], cB[:, 0, :], ACT.Exp, scale=-1.0).then_inc(silu_exp, 1)
            for i in range(ROT):
                o = full(act, ("house", i))
                act.wait_ge(sigma_out, i + 1)
                act.activation(w1s[:], o[0:PR, 0:AUG], ACT.Copy).then_inc(w1_done, 1)

            def tails(s, n, kind):
                for half in range(2):
                    job = ("tB", s, half)
                    o = full(act, job)
                    for dst, rows in ((tB, slice(0, 96)), (tBf, slice(32, 64))):
                        d, r = by_quarters(dst[rows, half * L:(half + 1) * L], s), in_order(o[rows, :], s)
                        if kind is None:
                            ins = act.activation(d, r, ACT.Copy)
                        else:
                            ins = act.activation(d, r, ACT.Identity, scale=mod[rows, n, kind + 1, 1, half:half + 1],
                                                 bias=mod[rows, n, kind, 1, half:half + 1])
                    ins.then_inc(empty(job), 1)

            def out_copy(n, i):
                job = ("pv", n, i)
                act.activation(oT[:, i % 2, :], full(act, job), ACT.Copy).then_inc(empty(job), 1)

            def attention(n):
                for pair in range(T // 2):
                    job = ("v", n, pair)
                    o = full(act, job)
                    act.activation(Vh[:, 2 * pair:2 * pair + 2, :, 0:10].rearrange("p t h d -> p (t h) d"),
                                   o[:, 0:320].rearrange("p (h d) -> p h d", d=10), ACT.Copy).then_inc(empty(job), 1)
                for i in range(B * NG):
                    for part in range(2):
                        job = ("qk", n, i, part)
                        o = full(act, job)
                        if i:
                            evacuated(act, ("qk", n, i - 1, part))
                        act.activation(hi_tmp[:, part, :], o, ACT.Copy).then_inc(hi_done, 1)
                for i in range(B * NG):
                    for kb in range(4):
                        for pr in range(2):
                            job = ("st", n, i, kb, pr)
                            full(act, job)
                            unit = ((n // 2 * 8 + i) * 4 + kb) * 2 + pr
                            act.activation(Pb[:, unit % 4], psum[:, 2 * pr:2 * pr + 2, :], ACT.Exp,
                                           scale=float(D) ** -0.5).then_inc(empty(job), 1)
                        if i >= 1 and kb == 0:
                            out_copy(n, i - 1)
                out_copy(n, B * NG - 1)

            def heads():
                for j in range(T):
                    job = ("hqkv", j)
                    act.activation(hq[:, j, :], full(act, job)[:, 0:3 * C], ACT.Copy).then_inc(empty(job), 1)
                for j in range(T):
                    act.wait_ge(hs_done, j + 1)
                    act.activation(hS[:, j % 4], hS[:, j % 4], ACT.Exp, scale=float(D) ** -0.5).then_inc(hp_done, 1)

            act.wait_ge(preset, 10)
            for n in range(NL):
                s = [0, 3, 7][n]
                evacuated(act, ("ada", n))
                tails(s, n, 0)
                if n == 1:
                    heads()
                else:
                    attention(n)
                tails(s + 1, n, None)
                tails(s + 2, n, 2)
                if n == NL - 1:
                    act.wait_ge(lg_ready, 1)
                    act.activation(cnt[:, 1], cw[:], ACT.Exp).then_inc(lg_exp, 1)
                func = ACT.Gelu if n == 1 else ACT.Gelu_apprx_tanh
                for e in range(E if n == NL - 1 else 1):
                    for b in range(B):
                        for m, (c0, w) in enumerate(MC):
                            job = ("f1", n, e, b, m)
                            o = full(act, job)
                            act.activation(G[0:w, b, m, :], o[0:w, :], func).then_inc(empty(job), 1)
                if n == 1:
                    tails(6, n, None)

        @block.gpsimd
        def _(pool):

            raised = {}

            def signal(ins, s):
                raised[s.name] = raised.get(s.name, 0) + 1
                ins.then_inc(s, 1)
                pool.wait_ge(s, raised[s.name])

            halves = [0]

            def tail_copies(half, job=None):
                if job == "heads":
                    pool.wait_ge(head_norm, half + 1)
                elif job:
                    evacuated(pool, job)
                else:
                    halves[0] += 1
                    pool.wait_ge(xe_nat, 4 * halves[0])
                rows = xe[:, 4 * half:4 * half + 4, :]
                for k in range(1, 3):
                    at = 128 + 32 * k
                    signal(pool.tensor_copy(rows[:, :, at:at + TAIL], rows[:, :, 128:C]), xe_dup)

            def tail_lows(s):
                for half in range(2):
                    evacuated(pool, ("tB", s, half))
                    cols = slice(half * L, (half + 1) * L)
                    signal(pool.tensor_tensor(tB[32:64, cols], tBf[32:64, cols], tB[32:64, cols].bitcast(F32),
                                       ALU.subtract), tB_done)

            def add_to_x(name):
                for pair in range(T // 2):
                    evacuated(pool, (*name, pair))
                    xs = x[:, 2 * pair:2 * pair + 2, :].rearrange("p t c -> p (t c)")
                    signal(pool.tensor_tensor(xs, xs, tmp[:, pair % 4, :], ALU.add), x_done)

            def max_rows(n, i):
                for c in (1, 3):
                    evacuated(pool, ("mx", n, i, 3, c))
                m = nmx[:, i % 2, :]
                signal(pool.tensor_copy(mhi[:, i % 2, :], m), pool_step)
                signal(pool.tensor_copy(mt[:, i % 2, 27::32], mhi[:, i % 2, :].bitcast(F32)), mt_done)
                signal(pool.tensor_tensor(mt[:, i % 2, 28::32], m, mhi[:, i % 2, :].bitcast(F32), ALU.subtract), mt_done)

            norms = [0]

            def rstds():
                norms[0] += 1
                pool.wait_ge(var_done, norms[0])
                signal(pool.tensor_tensor(rstd[:], vare[:], power[:, 0:T], ALU.pow), rstd_done)

            def attention(n):
                for i in range(B * NG):
                    evacuated(pool, ("qk", n, i, 1))
                    for dst, col in ((kE, 2), (kO, 3)):
                        signal(pool.tensor_scalar(dst[:, i, :], k_tmp[:, i % 2, :].bitcast(F32), neg_lo[:, col:col + 1], None,
                                           ALU.mult), k_done)
                for i in range(B * NG):
                    max_rows(n, i)
                    if i == 5:
                        tail_copies(0, ("ot", n, 3))
                tail_copies(1, ("ot", n, 7))

            def heads():
                for j in range(T):
                    evacuated(pool, ("hqkv", j))
                    if j >= 2:
                        pool.wait_ge(hs_done, j - 1)
                    q, k = (hq[:, j, p * C:(p + 1) * C].rearrange("p (h d) -> p h d", h=H) for p in range(2))
                    pj = prod[j % 2].rearrange("p (h k d) -> p h k d", h=H, k=H)
                    signal(pool.tensor_tensor(pj, q.unsqueeze(2).broadcast_to([128, H, H, D]),
                                              k.unsqueeze(1).broadcast_to([128, H, H, D]), ALU.mult), hprod_done)
                for half in range(2):
                    tail_copies(half, "heads")

            pool.wait_ge(rowsum, 1)
            signal(pool.partition_all_reduce(n1[:, 1, :], n1[:, 0, :], ROT, RED.max), norm_max)
            for i in range(ROT):
                pool.wait_ge(sigma_out, i + 1)
                signal(pool.tensor_tensor(qs[:, 2:3], qs[:, 0:1], power[0:PR, T:T + 1], ALU.pow), root_done)
            for n in range(NL):
                s = [0, 3, 7][n]
                pool.wait_ge(raw_in, 16 * (n + 1))
                signal(pool.tensor_copy(WB[:, 0:COLS[n]], raw[0:96, 0:COLS[n]]), pool_step)
                signal(pool.tensor_tensor(WB[64:96, 0:COLS[n]], raw[64:96, 0:COLS[n]], WB[64:96, 0:COLS[n]].bitcast(F32),
                                   ALU.subtract), wb_done)
                rstds()
                for half in range(2):
                    tail_copies(half)
                tail_lows(s)
                if n == 1:
                    heads()
                else:
                    attention(n)
                tail_lows(s + 1)
                add_to_x(("proj", n))
                rstds()
                for half in range(2):
                    tail_copies(half)
                tail_lows(s + 2)
                if n < NL - 1:
                    add_to_x(("f2", n, 0))
                if n == 1:
                    for half in range(2):
                        tail_copies(half)
                    tail_lows(6)


def constants():
    import numpy as np

    ident = np.eye(128, dtype=np.float32)
    r = np.arange(128) % 32
    neg_lo = np.zeros((128, 4), np.float32)
    neg_lo[:, 0] = np.where((r >= D) & (r < 2 * D), -1, 0)
    neg_lo[:, 1] = np.where((r >= 2 * D) & (r < 3 * D), -1, 0)
    neg_lo[:, 2] = np.arange(128) // 32 % 2 == 0
    neg_lo[:, 3] = np.arange(128) // 32 % 2 == 1
    silu_fix = np.zeros((17, 2), np.float32)
    silu_fix[:16, 0] = 1
    silu_fix[16, 1] = 1
    tri = np.broadcast_to(np.tril(np.ones((E, E), np.float32), -1), (128, E, E))
    thr = np.broadcast_to(2.0 ** np.arange(NSQ, dtype=np.float32), (ROT, B, NSQ))
    sgn = np.triu(np.ones((ROT, ROT), np.float32), 1) - np.tril(np.ones((ROT, ROT), np.float32), -1)
    row = np.arange(C).reshape(PN, PR).T
    ge = (row[:, :, None] >= np.arange(ROT)).astype(np.float32)
    return {"ident": ident, "neg_lo": neg_lo, "silu_fix": silu_fix, "tri": tri, "thr": thr, "sgn": sgn, "ge": ge}


def lay_out(v):
    import numpy as np

    f = {k: np.asarray(a) for k, a in v.items()}
    a = constants()
    a["x"] = f["x"].reshape(B * L, C)
    cond = np.zeros((145, 2), np.float32)
    cond[:C] = f["cond_1152"].T
    a["condA"], a["condB"] = cond[:128], cond[128:]

    def with_bias(w, b):
        return np.concatenate([w, b.reshape(1, -1)], 0)

    def cols_tail3(w):
        o = np.zeros((w.shape[0], 224), np.float32)
        o[:, :128] = w[:, :128]
        for k in range(3):
            o[:, 128 + 32 * k:144 + 32 * k] = w[:, 128:]
        return o

    def rows_tail3(w):
        o = np.zeros((96, w.shape[1]), np.float32)
        for k in range(3):
            o[32 * k:32 * k + 17] = w[128:145]
        return o

    def qkv(w):
        q, k, vv = (w[:, j * C:(j + 1) * C].reshape(-1, H, D) for j in range(3))
        oq = np.zeros((w.shape[0], H, 32), np.float32)
        ok = np.zeros((w.shape[0], H, 32), np.float32)
        for j in range(3):
            oq[:, :, j * D:(j + 1) * D] = q
            ok[:, :, j * D:(j + 1) * D] = k
        ok[C, :, 27:29] = 1
        ov = np.zeros((w.shape[0], H, D + 1), np.float32)
        ov[:, :, :D] = vv
        ov[C, :, D] = 1
        return [o.reshape(w.shape[0], -1) for o in (oq, ok, ov)]

    def fc2(ws, bs):
        o = np.zeros((128, len(ws), 5, C), np.float32)
        for e, (w, b) in enumerate(zip(ws, bs)):
            for m, (c0, n) in enumerate(MC):
                o[:n, e, m] = w[c0:c0 + n]
            o[64, e, 4] = b
        return o

    names = [("L0_cond_W_qkv", "L0_cond_b_qkv", "L0_cond_W_proj", "L0_cond_b_proj", "L0_cond_W_ada", "L0_cond_b_ada"),
             ("L1_cond_qkv_w", "L1_cond_qkv_b", "L1_cond_proj_w", "L1_cond_proj_b", "L1_cond_ada_w", "L1_cond_ada_b"),
             ("L3_cond_w_qkv", "L3_cond_b_qkv", "L3_cond_w_proj", "L3_cond_b_proj", "L3_cond_w_adaln", "L3_cond_b_adaln")]
    ffs = [([f["L0_cond_W_fc1"]], [f["L0_cond_b_fc1"]], [f["L0_cond_W_fc2"]], [f["L0_cond_b_fc2"]]),
           ([f["L1_cond_fc1_w"]], [f["L1_cond_fc1_b"]], [f["L1_cond_fc2_w"]], [f["L1_cond_fc2_b"]]),
           (f["L3_cond_w1"], f["L3_cond_b1"], f["L3_cond_w2"], f["L3_cond_b2"])]
    for n, ((wq, bq, wp, bp, wa, ba), (w1, b1, w2, b2)) in enumerate(zip(names, ffs)):
        w = with_bias(f[wq], f[bq])
        if n == 1:
            parts = [np.concatenate([w, np.zeros((145, PC - 3 * C), np.float32)], 1)]
        else:
            parts = qkv(w)
        parts.append(with_bias(f[wp], f[bp]))
        parts += [with_bias(w, b) for w, b in zip(w1, b1)]
        if n == NL - 1:
            parts.append(with_bias(f["L3_cond_w_gate"], np.zeros(E, np.float32)))
        w = np.concatenate(parts, 1)
        a[f"wa{n}"] = w[:128]
        a[f"wb{n}"] = rows_tail3(w)
        a[f"w2{n}"] = fc2(w2, b2)
        w = with_bias(f[wa], f[ba])
        six = [w[:, k * C:(k + 1) * C] for k in range(6)]
        a[f"ada{n}"] = np.concatenate([cols_tail3(six[k]) for k in (0, 1, 3, 4)] + [six[2], six[5]], 1)

    iu, ju = np.triu_indices(ROT, 1)
    sk = np.zeros((145, ROT, ROT), np.float32)
    w = with_bias(f["L2_cond_W"].T, f["L2_cond_b"])
    sk[:, ju, iu] = w
    sk[:, iu, ju] = w
    a["skew_w"] = sk.reshape(145, -1)
    aug = np.zeros((C, AUG), np.float32)
    aug[:, :ROT] = f["L2_cond_P"]
    aug[:, ROT:] = np.eye(C, dtype=np.float32)
    a["aug"] = aug.reshape(PN, PR, AUG).transpose(1, 0, 2)
    return {k: np.ascontiguousarray(z) for k, z in a.items()}


def kernel(**inputs):
    import concourse.bacc as bacc
    from concourse.bass_utils import run_bass_kernel_spmd

    arrays = lay_out(inputs)
    nc = bacc.Bacc("TRN2", target_bir_lowering=False, num_devices=1)
    t = {k: nc.dram_tensor(f"in_{k}", z.shape, F32, kind="ExternalInput").ap() for k, z in arrays.items()}
    out = nc.dram_tensor("x_out", (B * L, C), F32, kind="ExternalOutput").ap()
    build(nc, t, out)
    r = run_bass_kernel_spmd(nc, [{f"in_{k}": z for k, z in arrays.items()}], core_ids=[0])
    return r.results[0]["x_out"].reshape(B, L, C)
```

```python
from contextlib import ExitStack

import concourse.bass as bass
from concourse import mybir
from concourse.alu_op_type import AluOpType as ALU

F32 = mybir.dt.float32
F32R = mybir.dt.float32r
ACT = mybir.ActivationFunctionType
AX = mybir.AxisListType
RED = bass.bass_isa.ReduceOp

B, L, C = 2, 512, 144
T = B * L // 128
H, D = 16, 9
FF = 4 * C
E = 4
NL = 3
TAIL = C - 128
ROT = 64
GR = 4
NG = H // GR
EPS = 1e-6
MC = [(0, 128), (128, 128), (256, 128), (384, 128), (512, 64)]

QC, KC, VC, PC, W1C = 0, 512, 1024, 1184, 1328
COLS = [W1C + FF, W1C + FF, W1C + E * FF + E]
GC = W1C + E * FF
NSQ = 16
TAYLOR = 12
EXPM_BANK = 5
ROW_PERIOD, DOTS_AT, UPDATE_AT = 4, 1, 3
ROWS_IN_ATTENTION = 8 * 16 // ROW_PERIOD


def row_steps(n, m, at=0):
    return [m // ROW_PERIOD] if n == 0 and m % ROW_PERIOD == at else []


def build(nc, t, out):
    with ExitStack() as ctx:
        def sb(name, shape, dt=F32):
            return ctx.enter_context(nc.sbuf_tensor(name, shape, dt))

        def sem(name):
            return ctx.enter_context(nc.semaphore(name))

        psum = ctx.enter_context(nc.psum_tensor("psum", [128, 8, 512], F32))

        ident = sb("ident", [128, 128])
        neg_lo = sb("neg_lo", [128, 4])
        silu_fix = sb("silu_fix", [17, 2])
        tri = sb("tri", [128, E, E])
        x = sb("x", [128, T, C])
        xe = sb("xe", [128, T, 224])
        tA = sb("tA", [128, B * L])
        tB = sb("tB", [96, B * L], F32R)
        q1 = sb("q1", [128, B * NG, 512], F32R)
        kE = sb("kE", [128, B * NG, 512], F32R)
        kO = sb("kO", [128, B * NG, 512], F32R)
        hi_tmp = sb("hi_tmp", [128, 2, 512], F32R)
        k_tmp = sb("k_tmp", [128, 2, 512], F32R)
        q2 = sb("q2", [128, 2, 512], F32R)
        ws = sb("ws", [128, 8192])
        Vh = ws[:, 0:4096].rearrange("p (t h d) -> p t h d", t=T, h=H)
        Pb = ws[:, 4096:8192].rearrange("p (n s q) -> p n s q", n=4, s=2)
        raw = ws[:, 4096:8192]
        mt = sb("mt", [128, 2, 512])
        nmx = sb("nmx", [128, 2, 16])
        mhi = sb("mhi", [128, 2, 16], F32R)
        oT = sb("oT", [128, 2, 512])
        tBf = oT[:].rearrange("p s q -> p (s q)")
        rden = sb("rden", [128, 16])
        G = sb("G", [128, B, 5, 512])
        Gf = G[:].rearrange("p b m q -> p (b m q)")
        adaA = [Gf[:, 2368 * s:2368 * s + 1184] for s in range(2)]
        adaB = [Gf[0:17, 2368 * s + 1184:2368 * s + 2368] for s in range(2)]
        skA, skB = ws[:, 0:4096], ws[0:17, 4096:8192]
        hq = Gf[:, 0:T * 3 * C].rearrange("p (t c) -> p t c", t=T)
        prod = [ws[:, k * H * H * D:(k + 1) * H * H * D] for k in range(3)]
        hden = ws[:, 6912:6912 + T * H].rearrange("p (t h) -> p t h", t=T)
        hmax = ws[:, 7040:7040 + 2 * H].rearrange("p (t h) -> p t h", t=2)
        tmp = sb("tmp", [128, 4, 2 * C])
        acc = tmp[:].rearrange("p n c -> p (n c)").rearrange("p (t c) -> p t c", c=C)
        WA = sb("WA", [128, COLS[2]])
        WB = sb("WB", [96, COLS[2]], F32R)
        W2 = sb("W2", [128, E, 5, C])
        cA = sb("cA", [128, 4, B])
        cB = sb("cB", [17, 4, B])
        srepA = sb("srepA", [128, B, 128])
        srepB = sb("srepB", [17, B, 128])
        mod = sb("mod", [128, NL, 4, 2, B])
        gates = sb("gates", [128, NL, B, 2 * C])
        stats = sb("stats", [128, T, 6])
        mv = sb("mv", [128, T, 2])
        rstd = sb("rstd", [128, T])
        vare = sb("vare", [128, T])
        power = sb("power", [128, T + 1])
        sgn = sb("sgn", [ROT, ROT])
        thr = sb("thr", [128, NSQ])
        eye2 = sb("eye2", [128, 2 * ROT])
        skew = sb("skew", [128, ROT])
        skp = sb("skp", [128, 2, ROT])
        n1 = sb("n1", [128, 2])
        sq = sb("sq", [128, 3, NSQ])
        Rm = sb("Rm", [128, 2, ROT])
        Rk = sb("Rk", [128, 2, ROT])
        QA = sb("QA", [128, 2, C])
        vrow = sb("vrow", [128, C])
        vsq = sb("vsq", [128, C])
        qs = sb("qs", [128, 8])
        junk = sb("junk", [128, 2, C])
        dots = sb("dots", [128, 2])
        ucol = sb("ucol", [128, 2])
        UTx = sb("UTx", [128, 224])
        RU = sb("RU", [128, C])
        MA = sb("MA", [128, B, C])
        MB = sb("MB", [96, B, C], F32R)
        hS = tBf.rearrange("p (n h k) -> p n h k", n=4, h=H)
        hO = tmp[:].rearrange("p n c -> p (n c)").rearrange("p (t c) -> p t c", c=C)
        Rm_flat = Rm[:].rearrange("p s n -> p (s n)")
        Rk_flat = Rk[:].rearrange("p s n -> p (s n)")
        MBf = tmp[0:96, 0, :].rearrange("p (b c) -> p b c", b=B)
        lg = sb("lg", [128, T, E])
        m1 = sb("m1", [128, T])
        ahead, tied = (mt[:, k, 0:T * E * E].rearrange("p (t e f) -> p t e f", t=T, e=E) for k in range(2))
        cnt = sb("cnt", [128, 2, T, E])
        cw = sb("cw", [128, T, E])
        den = sb("den", [128, T])

        filled = [sem(f"bank{k}_filled") for k in range(8)]
        drained = [sem(f"bank{k}_drained") for k in range(8)]
        const_in = sem("const_in")
        ada_in = [sem(f"ada{n}_in") for n in range(NL)]
        wa_in = sem("wa_in")
        raw_in = sem("raw_in")
        skew_in = sem("skew_in")
        x_in = sem("x_in")
        preset = sem("preset")
        silu_exp = sem("silu_exp")
        silu_done = sem("silu_done")
        wb_done = sem("wb_done")
        xe_nat = sem("xe_nat")
        xe_dup = sem("xe_dup")
        tB_done = sem("tB_done")
        hi_done = sem("hi_done")
        k_done = sem("k_done")
        mt_done = sem("mt_done")
        x_done = sem("x_done")
        x_final = sem("x_final")
        norm_max = sem("norm_max")
        rm_init = sem("rm_init")
        rm_less_one = sem("rm_less_one")
        rowsum = sem("rowsum")
        vrow_ready = sem("vrow_ready")
        dots_done = sem("dots_done")
        reflector_done = sem("reflector_done")
        basis_updated = sem("basis_updated")
        var_done = sem("var_done")
        rstd_done = sem("rstd_done")
        kept_done = sem("kept_done")
        ut_done = sem("ut_done")
        m_done = sem("m_done")
        lg_exp = sem("lg_exp")
        hprod_done = sem("hprod_done")
        hs_done = sem("hs_done")
        hp_done = sem("hp_done")
        ho_done = sem("ho_done")
        head_norm = sem("head_norm")
        lg_ready = sem("lg_ready")
        stored = sem("stored")
        dve_step = sem("dve_step")
        pool_step = sem("pool_step")

        ada_h = [t[f"ada{n}"] for n in range(NL)]
        block = ctx.enter_context(nc.Block())

        use = {}
        uses = [0] * 8

        def full(eng, job):
            k, n = use[job]
            eng.wait_ge(filled[k], n)
            return psum[:, k, :]

        def empty(job):
            return drained[use[job][0]]

        def evacuated(eng, job):
            k, n = use[job]
            eng.wait_ge(drained[k], n)

        def by_quarters(ap, s):
            return ap.rearrange("p (v u a) -> p a u v", v=4, u=4) if s == 3 else ap

        def in_order(ap, s):
            return ap.rearrange("p (a u v) -> p a u v", u=4, v=4) if s == 3 else ap

        @block.tensor
        def _(pe):
            def claim(job, k):
                if uses[k]:
                    pe.wait_ge(drained[k], uses[k])
                uses[k] += 1
                use[job] = (k, uses[k])
                return psum[:, k, :]

            def tail_mm(o, lhsT, rhs, stop=True):
                return pe.matmul(o, lhsT, rhs, start=False, stop=stop)

            def ada_vectors(n):
                pe.wait_ge(ada_in[n], 32)
                o = claim(("ada", n), 7)
                for kind in range(4):
                    for ab, (c0, m) in enumerate(((0, 128), (128, 96))):
                        at = (kind * 2 + ab) * B
                        c = kind * 224 + c0
                        pe.matmul(o[0:m, at:at + B], adaA[n % 2][:, c:c + m], cA[:, 3, :], start=True, stop=False)
                        last = tail_mm(o[0:m, at:at + B], adaB[n % 2][:, c:c + m], cB[:, 3, :])
                last.then_inc(filled[7], 1)
                for b in range(B):
                    o = claim(("gate", n, b), 7)
                    pe.matmul(o[:, 0:2 * C], srepA[:, b, :], adaA[n % 2][:, 896:1184], start=True, stop=False)
                    tail_mm(o[:, 0:2 * C], srepB[:, b, :], adaB[n % 2][:, 896:1184]).then_inc(filled[7], 1)

            def generators():
                pe.wait_ge(skew_in, 32)
                o = claim("skew", 3)
                for j in range(ROT):
                    pe.matmul(o[0:ROT, 2 * j:2 * j + 2], skA[:, j * ROT:(j + 1) * ROT], cA[:, 3, :], start=True, stop=False)
                    last = tail_mm(o[0:ROT, 2 * j:2 * j + 2], skB[:, j * ROT:(j + 1) * ROT], cB[:, 3, :])
                last.then_inc(filled[3], 1)

            def exponential(k):
                if k == 0:
                    pe.wait_ge(rm_init, 1)
                o = claim(("expm", k), EXPM_BANK)
                if k:
                    evacuated(pe, ("expm", k - 1))
                for b in range(B):
                    rows = slice(64 * b, 64 * b + 64)
                    for s in range(2):
                        left = skp[rows, s, :] if k < TAYLOR else Rm[rows, 1 - s, :]
                        last = pe.matmul(o[rows, s * ROT:(s + 1) * ROT], left, Rm[rows, s, :], start=True, stop=True)
                last.then_inc(filled[EXPM_BANK], 1)

            def reflect_row(i):
                if i:
                    pe.wait_ge(basis_updated, i)
                o = claim(("house", i), 7)
                pe.matmul(o[:, 0:C - i], ident[0:ROT, i:i + 1].broadcast_to([ROT, 128]), QA[0:ROT, 0, i:C],
                          start=True, stop=True).then_inc(filled[7], 1)

            def subspace_map():
                pe.wait_ge(basis_updated, ROT)
                o = claim("UT", 6)
                pe.transpose(o[0:ROT, 0:64], QA[64:128, 0, 0:ROT], ident[64:128, 64:128])
                pe.transpose(o[0:ROT, 64:C], QA[0:80, 1, 0:ROT], ident[0:80, 0:80]).then_inc(filled[6], 1)
                pe.wait_ge(ut_done, 1)
                pe.wait_ge(rm_less_one, 1)
                o = claim("RU", 6)
                for b in range(B):
                    rows = slice(64 * b, 64 * b + 64)
                    last = pe.matmul(o[rows, 0:C], Rm[rows, 1, :], UTx[rows, 0:C], start=True, stop=True)
                last.then_inc(filled[6], 1)
                evacuated(pe, "RU")
                for b in range(B):
                    o = claim(("MA", b), 6)
                    rows = slice(64 * b, 64 * b + 64)
                    pe.matmul(o[:, 0:C], UTx[rows, 0:128], RU[rows, :], start=True, stop=True)
                    pe.matmul(o[0:96, C:2 * C], UTx[rows, 128:224], RU[rows, :], start=True, stop=True).then_inc(filled[6], 1)

            pe.wait_ge(const_in, 16 * 7)
            pe.wait_ge(silu_done, 1)
            ada_vectors(0)
            generators()
            ada_vectors(1)
            ada_vectors(2)
            pe.wait_ge(x_in, 64)

            def to_features(s):
                for half in range(2):
                    pe.wait_ge(xe_dup, 2 * (2 * s + half + 1))
                    o = claim(("tA", s, half), 2 * half)
                    for j in range(4):
                        last = pe.transpose(o[:, j * 128:(j + 1) * 128], xe[:, 4 * half + j, 0:128], ident[:])
                    last.then_inc(filled[2 * half], 1)
                    o = claim(("tB", s, half), 2 * half + 1)
                    for j in range(4):
                        last = pe.transpose(o[0:96, j * 128:(j + 1) * 128], xe[:, 4 * half + j, 128:224], ident[:])
                    last.then_inc(filled[2 * half + 1], 1)

            def ready(s, half):
                evacuated(pe, ("tA", s, half))
                pe.wait_ge(tB_done, 2 * s + half + 1)

            def token_major(name, s, wa, wb, width, banks):
                for pair in range(T // 2):
                    if pair % 2 == 0:
                        ready(s, pair // 2)
                    k = banks[pair % len(banks)]
                    o = claim((*name, pair), k)
                    for j in range(2):
                        tok = slice((2 * pair + j) * 128, (2 * pair + j + 1) * 128)
                        pe.matmul(o[:, j * width:(j + 1) * width], tA[:, tok], wa(pair // 2), start=True, stop=False)
                        last = tail_mm(o[:, j * width:(j + 1) * width], tB[:, tok], wb(pair // 2))
                    last.then_inc(filled[k], 1)

            def st_mm(n, i, kb):
                if kb == 0:
                    evacuated(pe, ("mt", n, i))
                for pr, kx in ((0, kE), (1, kO)):
                    claim(("st", n, i, kb, pr), 2 * pr)
                    for s in range(2):
                        rows = slice(64 * s, 64 * s + 64)
                        last = pe.matmul(psum[:, 2 * pr + s, :], kx[rows, i, kb * 128:(kb + 1) * 128],
                                         q2[rows, i % 2, :], start=True, stop=True)
                    last.then_inc(filled[2 * pr], 1)

            def pv_mm(n, i, kb):
                if kb == 0:
                    claim(("pv", n, i), 6)
                unit = ((n // 2 * 8 + i) * 4 + kb) * 2
                for pr in range(2):
                    evacuated(pe, ("st", n, i, kb, pr))
                for c in range(GR):
                    pr, s = c % 2, c // 2
                    last = pe.matmul(psum[32 * c:32 * c + 32, 6, :], Vh[:, (i // NG) * 4 + kb, (i % NG) * GR + c, :],
                                     Pb[:, (unit + pr) % 4, s, :], start=(kb == 0), stop=(kb == 3))
                if kb == 3:
                    last.then_inc(filled[6], 1)

            def mx_mm(n, i, qt):
                for j, c in enumerate((0, 2, 1, 3)):
                    kx = kE if c % 2 == 0 else kO
                    rows = slice(64 * (c // 2), 64 * (c // 2) + 64)
                    k = 4 + j % 2
                    o = claim(("mx", n, i, qt, c), k)
                    pe.matmul(o, q1[rows, i, qt * 128:(qt + 1) * 128], kx[rows, i, :],
                              start=True, stop=True).then_inc(filled[k], 1)
                    for step in row_steps(n, (i * 4 + qt) * 4 + j):
                        reflect_row(step)

            def mt_mm(n, i):
                pe.wait_ge(mt_done, 2 * (n // 2 * 8 + i + 1))
                o = claim(("mt", n, i), 7)
                for qt in range(4):
                    last = pe.transpose(o[:, qt * 128:(qt + 1) * 128], mt[:, i % 2, qt * 128:(qt + 1) * 128], ident[:])
                last.then_inc(filled[7], 1)

            def ot_mm(n, i):
                evacuated(pe, ("pv", n, i))
                o = claim(("ot", n, i), 7)
                for qt in range(4):
                    last = pe.transpose(o[:, qt * 128:(qt + 1) * 128], oT[:, i % 2, qt * 128:(qt + 1) * 128], ident[:])
                last.then_inc(filled[7], 1)

            def hidden(n, e, b, s):
                ready(s, b)
                for m, (c0, w) in enumerate(MC):
                    k = m % 4
                    o = claim(("f1", n, e, b, m), k)
                    c = W1C + e * FF + c0
                    pe.matmul(o[0:w, :], WA[:, c:c + w], tA[:, b * L:(b + 1) * L], start=True, stop=False)
                    tail_mm(o[0:w, :], WB[:, c:c + w], tB[:, b * L:(b + 1) * L]).then_inc(filled[k], 1)

            def back(n, e, b):
                for m in range(1, 5):
                    evacuated(pe, ("f1", n, e, b, m))
                for pair in range(2):
                    k = 4 + (2 * b + pair) % 4
                    o = claim(("f2", n, e, 2 * b + pair), k)
                    for j in range(2):
                        tok = slice((2 * pair + j) * 128, (2 * pair + j + 1) * 128)
                        for m, (c0, w) in enumerate(MC):
                            w += m == 4
                            last = pe.matmul(o[:, j * C:(j + 1) * C], G[0:w, b, m, tok], W2[0:w, e, m, :],
                                             start=(m == 0), stop=(m == 4))
                    last.then_inc(filled[k], 1)

            def attention_mm(n, s):
                token_major(("v", n), s, lambda b: WA[:, VC:VC + 160], lambda b: WB[:, VC:VC + 160], 160, [4, 5, 6, 7])
                for i in range(B * NG):
                    b, g = divmod(i, NG)
                    for part, c0 in ((0, QC), (1, KC)):
                        k = (2 * i + part) % 8
                        o = claim(("qk", n, i, part), k)
                        c = c0 + g * 128
                        pe.matmul(o, WA[:, c:c + 128], tA[:, b * L:(b + 1) * L], start=True, stop=False)
                        tail_mm(o, WB[:, c:c + 128], tB[:, b * L:(b + 1) * L]).then_inc(filled[k], 1)
                for pair in range(T // 2):
                    evacuated(pe, ("v", n, pair))
                if n == 2:
                    pe.wait_ge(preset, 12)
                for i in range(-1, B * NG):
                    if i + 1 < B * NG:
                        evacuated(pe, ("qk", n, i + 1, 0))
                        pe.wait_ge(k_done, 2 * (n // 2 * 8 + i + 2))
                    for kb in range(4):
                        if i >= 0:
                            st_mm(n, i, kb)
                        if i + 1 < B * NG:
                            mx_mm(n, i + 1, kb)
                        if i >= 0 and kb >= 1:
                            pv_mm(n, i, kb - 1)
                        if i >= 1 and kb == 0:
                            pv_mm(n, i - 1, 3)
                        if i >= 1 and kb == 1:
                            ot_mm(n, i - 1)
                    if i + 1 < B * NG:
                        mt_mm(n, i + 1)
                pv_mm(n, B * NG - 1, 3)
                ot_mm(n, B * NG - 1)

            for n in range(NL):
                s = [0, 3, 7][n]
                to_features(s)
                pe.wait_ge(wa_in, 32 * (n + 1))
                pe.wait_ge(wb_done, n + 1)
                if n == 1:
                    for j in range(T):
                        b, v = divmod(j, 4)
                        if v == 0:
                            ready(s, b)
                        o = claim(("hqkv", j), j)
                        tok = slice(j * 128, (j + 1) * 128)
                        pe.matmul(o[:, 0:3 * C], tA[:, tok], WA[:, 0:3 * C], start=True, stop=False)
                        tail_mm(o[:, 0:3 * C], tB[:, tok], WB[:, 0:3 * C]).then_inc(filled[j], 1)
                    for k in range(TAYLOR + NSQ):
                        exponential(k)
                else:
                    attention_mm(n, s)
                to_features(s + 1)
                token_major(("proj", n), s + 1, lambda b: WA[:, PC:PC + C], lambda b: WB[:, PC:PC + C], C, [4, 5, 6, 7])
                to_features(s + 2)
                if n == 0:
                    for i in range(ROWS_IN_ATTENTION, ROT):
                        reflect_row(i)
                if n == NL - 1:
                    o = claim("logits", 7)
                    for tt in range(T):
                        ready(s + 2, tt // 4)
                        tok = slice(tt * 128, (tt + 1) * 128)
                        pe.matmul(o[:, tt * E:(tt + 1) * E], tA[:, tok], WA[:, GC:GC + E], start=True, stop=False)
                        last = tail_mm(o[:, tt * E:(tt + 1) * E], tB[:, tok], WB[:, GC:GC + E])
                    last.then_inc(filled[7], 1)
                if n == 1:
                    pe.wait_ge(preset, 11)
                for e in range(E if n == NL - 1 else 1):
                    for b in range(B):
                        hidden(n, e, b, s + 2)
                        if b == 1:
                            back(n, e, 0)
                    back(n, e, 1)
                if n == 1:
                    to_features(6)
                    subspace_map()
                    pe.wait_ge(m_done, 2)
                    token_major(("rot",), 6, lambda b: MA[:, b, :], lambda b: MB[:, b, :], C, [4, 5, 6, 7])

        @block.sync
        def _(sp):
            for name, dst in (("ident", ident[:]), ("neg_lo", neg_lo[:]), ("silu_fix", silu_fix[:]), ("tri", tri[:]),
                              ("condA", cA[:, 0, :]), ("condB", cB[:, 0, :]), ("thr", thr[:])):
                sp.dma_start(dst, t[name]).then_inc(const_in, 16)
            for n in range(NL):
                if n == 2:
                    for b in range(B):
                        evacuated(sp, ("gate", 0, b))
                sp.dma_start(adaA[n % 2], ada_h[n][0:128, :]).then_inc(ada_in[n], 16)
                sp.dma_start(adaB[n % 2], ada_h[n][128:145, :]).then_inc(ada_in[n], 16)
                if n == 0:
                    sp.dma_start(skA, t["skew_w"][0:128, :]).then_inc(skew_in, 16)
                    sp.dma_start(skB, t["skew_w"][128:145, :]).then_inc(skew_in, 16)
                    for name, dst in (("sgn", sgn[:]), ("aug", QA[:]), ("eye2", eye2[:]),
                                      ("x", x[:])):
                        src = t[name].rearrange("(t p) c -> p t c", p=128) if name == "x" else t[name]
                        sp.dma_start(dst, src).then_inc(x_in, 16)
            evacuated(sp, "skew")
            for n in range(NL):
                if n:
                    sp.wait_ge(x_done, 8 * n)
                sp.dma_start(raw[0:96, 0:COLS[n]], t[f"wb{n}"]).then_inc(raw_in, 16)
                sp.dma_start(WA[:, 0:COLS[n]], t[f"wa{n}"]).then_inc(wa_in, 16)
                ne = E if n == NL - 1 else 1
                sp.dma_start(W2[:, 0:ne, :, :], t[f"w2{n}"]).then_inc(wa_in, 16)
            for pair in range(T // 2):
                sp.wait_ge(x_final, pair + 1)
                sp.dma_start(out.rearrange("(t p) c -> p t c", p=128)[:, 2 * pair:2 * pair + 2, :],
                             x[:, 2 * pair:2 * pair + 2, :]).then_inc(stored, 16)
            sp.wait_ge(stored, 16 * (T // 2))

        @block.vector
        def _(dve):
            steps = [0]

            def then(ins):
                steps[0] += 1
                ins.then_inc(dve_step, 1)
                dve.wait_ge(dve_step, steps[0])

            dve.memset(mt[:], 0.0).then_inc(preset, 1)
            dve.memset(xe[:], 0.0).then_inc(preset, 1)
            dve.wait_ge(preset, 2)
            for k in range(3):
                at = 128 + 32 * k + TAIL
                dve.memset(xe[:, :, at:at + 1], 1.0).then_inc(preset, 1)
            dve.memset(UTx[:], 0.0).then_inc(preset, 1)
            dve.memset(power[:, 0:T], -0.5).then_inc(preset, 1)
            dve.memset(power[:, T:T + 1], 0.5).then_inc(preset, 1)
            dve.wait_ge(preset, 8)

            dve.wait_ge(silu_exp, 2)
            dve.tensor_scalar(cA[:, 2, :], cA[:, 1, :], 1.0, None, ALU.add)
            then(dve.tensor_scalar(cB[:, 2, :], cB[:, 1, :], 1.0, None, ALU.add))
            dve.reciprocal(cA[:, 2, :], cA[:, 2, :])
            then(dve.reciprocal(cB[:, 2, :], cB[:, 2, :]))
            dve.tensor_tensor(cA[:, 3, :], cA[:, 0, :], cA[:, 2, :], ALU.mult)
            then(dve.tensor_tensor(cB[:, 2, :], cB[:, 0, :], cB[:, 2, :], ALU.mult))
            then(dve.tensor_scalar(cB[:, 3, :], cB[:, 2, :], silu_fix[:, 0:1], silu_fix[:, 1:2], ALU.mult, ALU.add))
            dve.tensor_copy(srepA[:], cA[:, 3, :].unsqueeze(2).broadcast_to([128, B, 128]))
            dve.tensor_copy(srepB[:], cB[:, 3, :].unsqueeze(2).broadcast_to([17, B, 128])).then_inc(silu_done, 1)

            def ada_vectors(n):
                v = full(dve, ("ada", n))[:, 0:16].rearrange("p (k a b) -> p k a b", k=4, a=2)
                for kind in range(4):
                    dve.tensor_scalar(mod[:, n, kind, 0, :], v[:, kind, 0, :], float(kind % 2), None, ALU.add)
                    ins = dve.tensor_scalar(mod[0:96, n, kind, 1, :], v[0:96, kind, 1, :], float(kind % 2), None, ALU.add)
                ins.then_inc(empty(("ada", n)), 1)
                for b in range(B):
                    o = full(dve, ("gate", n, b))
                    dve.tensor_copy(gates[:, n, b, :], o[:, 0:2 * C]).then_inc(empty(("gate", n, b)), 1)

            def generators():
                dve.wait_ge(x_in, 64)
                o = full(dve, "skew")
                for b in range(B):
                    ins = dve.tensor_tensor(skew[64 * b:64 * b + 64, :], o[0:ROT, b:2 * ROT:2], sgn[:], ALU.mult)
                ins.then_inc(empty("skew"), 1)
                evacuated(dve, "skew")
                dve.tensor_reduce(n1[:, 0:1], skew[:], AX.X, ALU.add, apply_absolute_value=True).then_inc(rowsum, 1)

            def exponential_start():
                dve.wait_ge(norm_max, 1)
                then(dve.tensor_tensor(sq[:, 0], n1[:, 1:2].broadcast_to([128, NSQ]), thr[:], ALU.is_gt))
                dve.tensor_scalar(sq[:, 1], sq[:, 0], -1.0, 1.0, ALU.mult, ALU.add)
                then(dve.tensor_scalar(sq[:, 2], sq[:, 0], -0.5, 1.0, ALU.mult, ALU.add))
                w = NSQ
                while w > 1:
                    w //= 2
                    then(dve.tensor_tensor(sq[:, 2, 0:w], sq[:, 2, 0:w], sq[:, 2, w:2 * w], ALU.mult))
                then(dve.tensor_scalar(skp[:, 1, :], skew[:], sq[:, 2, 0:1], None, ALU.mult))
                dve.tensor_scalar(skp[:, 0, :], skp[:, 1, :], -1.0, None, ALU.mult)
                dve.tensor_copy(Rm_flat, eye2[:]).then_inc(rm_init, 1)

            def exponential(k):
                job = ("expm", k)
                if k >= TAYLOR:
                    sk = k - TAYLOR
                    if k == TAYLOR:
                        evacuated(dve, ("expm", k - 1))
                    dve.tensor_scalar(Rk_flat, Rm_flat, sq[:, 1, sk:sk + 1], None, ALU.mult).then_inc(kept_done, 1)
                o = full(dve, job)[:, 0:2 * ROT]
                if k < TAYLOR:
                    dve.scalar_tensor_tensor(Rm_flat, o, 1.0 / (TAYLOR - k), eye2[:], ALU.mult, ALU.add).then_inc(empty(job), 1)
                else:
                    dve.wait_ge(kept_done, sk + 1)
                    dve.scalar_tensor_tensor(Rm_flat, o, sq[:, 0, sk:sk + 1], Rk_flat, ALU.mult, ALU.add).then_inc(empty(job), 1)
                if k >= TAYLOR:
                    evacuated(dve, job)

            def exponential_end():
                dve.tensor_tensor(Rm_flat, Rm_flat, eye2[:], ALU.subtract).then_inc(rm_less_one, 1)

            def reflect_dots(i):
                dve.wait_ge(vrow_ready, i + 1)
                if i:
                    dve.wait_ge(basis_updated, i)
                for c in range(2):
                    ins = dve.tensor_tensor_reduce(out=junk[:, c, i:C], in0=QA[:, c, i:C], in1=vrow[:, i:C], scale=1.0,
                                                   scalar=0.0, op0=ALU.mult, op1=ALU.add, accum_out=dots[:, c:c + 1])
                ins.then_inc(dots_done, 1)

            def reflect_update(i):
                dve.wait_ge(reflector_done, i + 1)
                then(dve.reciprocal(qs[:, 4:5], qs[:, 4:5]))
                then(dve.tensor_scalar(ucol[:], ucol[:], qs[:, 4:5], None, ALU.mult))
                for c in range(2):
                    ins = dve.scalar_tensor_tensor(QA[:, c, i:C], vrow[:, i:C], ucol[:, c:c + 1], QA[:, c, i:C], ALU.mult, ALU.add)
                ins.then_inc(basis_updated, 1)

            def subspace_map():
                o = full(dve, "UT")
                dve.tensor_copy(UTx[0:64, 0:C], o[0:ROT, 0:C])
                dve.tensor_copy(UTx[64:128, 0:C], o[0:ROT, 0:C]).then_inc(empty("UT"), 1)
                evacuated(dve, "UT")
                for k in range(1, 3):
                    ins = dve.tensor_copy(UTx[:, 128 + 32 * k:128 + 32 * k + TAIL], UTx[:, 128:C])
                ins.then_inc(ut_done, 1)
                o = full(dve, "RU")
                dve.tensor_copy(RU[:], o[:, 0:C]).then_inc(empty("RU"), 1)
                for b in range(B):
                    job = ("MA", b)
                    o = full(dve, job)
                    dve.tensor_copy(MA[:, b, :], o[:, 0:C])
                    dve.tensor_copy(MB[:, b, :], o[0:96, C:2 * C])
                    dve.tensor_copy(MBf[:, b, :], o[0:96, C:2 * C]).then_inc(empty(job), 1)
                    evacuated(dve, job)
                    dve.tensor_tensor(MB[64:96, b, :], MBf[64:96, b, :], MB[64:96, b, :].bitcast(F32), ALU.subtract).then_inc(m_done, 1)

            ada_vectors(0)
            generators()
            ada_vectors(1)
            ada_vectors(2)
            dve.memset(ws[:, 0:4096], 0.0).then_inc(preset, 1)
            dve.memset(G[64:65, :, 4, :], 1.0).then_inc(preset, 1)

            norms = [0]

            def layernorm(s):
                for tt in range(T):
                    ins = dve.bn_stats(stats[:, tt, :], x[:, tt, :])
                then(ins)
                for tt in range(T):
                    ins = dve.bn_aggr(mv[:, tt, :], stats[:, tt, :])
                then(ins)
                dve.tensor_scalar(vare[:], mv[:, :, 1], EPS, None, ALU.add).then_inc(var_done, 1)
                norms[0] += 1
                dve.wait_ge(rstd_done, norms[0])
                for tt in range(T):
                    dve.tensor_scalar(xe[:, tt, 0:C], x[:, tt, :], mv[:, tt, 0:1], rstd[:, tt:tt + 1],
                                      ALU.subtract, ALU.mult).then_inc(xe_nat, 1)

            def mains(s, n, kind):
                for half in range(2):
                    job = ("tA", s, half)
                    o = full(dve, job)
                    dst, o = by_quarters(tA[:, half * L:(half + 1) * L], s), in_order(o, s)
                    if kind is None:
                        ins = dve.tensor_copy(dst, o)
                    else:
                        ins = dve.tensor_scalar(dst, o, mod[:, n, kind + 1, 0, half:half + 1],
                                                mod[:, n, kind, 0, half:half + 1], ALU.mult, ALU.add)
                    ins.then_inc(empty(job), 1)

            sent = [0]

            def gated(name, n, which):
                for pair in range(T // 2):
                    job = (*name, pair)
                    o = full(dve, job)
                    if sent[0] >= 4:
                        dve.wait_ge(x_done, sent[0] - 3)
                    gt = gates[:, n, pair // 2, which * C:(which + 1) * C].unsqueeze(1).broadcast_to([128, 2, C])
                    dve.tensor_tensor(tmp[:, sent[0] % 4, :].rearrange("p (j c) -> p j c", j=2),
                                      o[:, 0:2 * C].rearrange("p (j c) -> p j c", j=2), gt, ALU.mult).then_inc(empty(job), 1)
                    sent[0] += 1

            def normalised(n, i):
                b, g = divmod(i, NG)
                job = ("ot", n, i)
                o = full(dve, job)
                then(dve.reciprocal(rden[:], o[:, D::32]))
                heads = o.rearrange("p (q c d) -> p q c d", q=4, c=GR)
                dst = xe[:, 4 * b:4 * b + 4, g * GR * D:(g + 1) * GR * D].rearrange("p q (c d) -> p q c d", c=GR)
                rd = rden[:].rearrange("p (q c) -> p q c", q=4)
                for qt in range(4):
                    ins = dve.tensor_tensor(dst[:, qt], heads[:, qt, :, 0:D], rd[:, qt].unsqueeze(2).broadcast_to([128, GR, D]), ALU.mult)
                ins.then_inc(empty(job), 1)

            def attention(n):
                for i in range(B * NG):
                    for part, dst in ((0, q1[:, i, :]), (1, k_tmp[:, i % 2, :])):
                        job = ("qk", n, i, part)
                        o = full(dve, job)
                        dve.wait_ge(hi_done, n // 2 * 16 + 2 * i + part + 1)
                        if part == 1 and n // 2 * 8 + i >= 2:
                            dve.wait_ge(k_done, 2 * (n // 2 * 8 + i - 1))
                        dve.scalar_tensor_tensor(dst, hi_tmp[:, part, :].bitcast(F32), neg_lo[:, part:part + 1], o,
                                                 ALU.mult, ALU.add).then_inc(empty(job), 1)
                for i in range(-1, B * NG):
                    for kb in range(4):
                        if i + 1 < B * NG:
                            for c in (0, 2, 1, 3):
                                job = ("mx", n, i + 1, kb, c)
                                o = full(dve, job)
                                dve.tensor_reduce(nmx[:, (i + 1) % 2, kb * 4 + c:kb * 4 + c + 1], o, AX.X, ALU.max,
                                                  negate=True).then_inc(empty(job), 1)
                                m = ((i + 1) * 4 + kb) * 4 + (0, 2, 1, 3).index(c)
                                if i >= 1 and kb == 2 and c == 0:
                                    normalised(n, i - 1)
                                for step in row_steps(n, m, DOTS_AT):
                                    reflect_dots(step)
                                for step in row_steps(n, m, UPDATE_AT):
                                    reflect_update(step)
                    if i + 1 < B * NG:
                        job = ("mt", n, i + 1)
                        o = full(dve, job)
                        dve.tensor_tensor(q2[:, (i + 1) % 2, :], q1[:, i + 1, :].bitcast(F32), o, ALU.add).then_inc(empty(job), 1)
                for i in range(B * NG - 2, B * NG):
                    normalised(n, i)
                dve.wait_ge(empty(("ot", n, B * NG - 1)), use[("ot", n, B * NG - 1)][1])

            def heads():
                exponential_start()
                for j in range(T + 1):
                    for k in range(3 * j, min(3 * j + 3, TAYLOR + NSQ)):
                        exponential(k)
                    if j < T:
                        S = hS[:, j % 4]
                        dve.wait_ge(hprod_done, j + 1)
                        if j >= 4:
                            dve.wait_ge(ho_done, j - 3)
                        then(dve.tensor_reduce(S, prod[j % 2].rearrange("p (h k d) -> p h k d", h=H, k=H), AX.X, ALU.add))
                        then(dve.tensor_reduce(hmax[:, j % 2], S, AX.X, ALU.max))
                        dve.tensor_tensor(S, S, hmax[:, j % 2].unsqueeze(2).broadcast_to([128, H, H]), ALU.subtract).then_inc(hs_done, 1)
                    if j >= 1:
                        t1 = j - 1
                        S = hS[:, t1 % 4]
                        dve.wait_ge(hp_done, t1 + 1)
                        dve.tensor_reduce(hden[:, t1], S, AX.X, ALU.add)
                        pv = prod[2].rearrange("p (h d k) -> p h d k", h=H, d=D)
                        vv = hq[:, t1, 2 * C:3 * C].rearrange("p (k d) -> p d k", k=H)
                        if t1:
                            dve.wait_ge(ho_done, t1)
                        then(dve.tensor_tensor(pv, S.unsqueeze(2).broadcast_to([128, H, D, H]),
                                               vv.unsqueeze(1).broadcast_to([128, H, D, H]), ALU.mult))
                        dve.reciprocal(hden[:, t1], hden[:, t1])
                        dve.tensor_reduce(hO[:, t1, :].rearrange("p (h d) -> p h d", h=H), pv, AX.X, ALU.add).then_inc(ho_done, 1)
                for k in range(3 * T + 3, TAYLOR + NSQ):
                    exponential(k)
                exponential_end()
                dve.wait_ge(ho_done, T)
                for b in range(B):
                    dst = xe[:, 4 * b:4 * b + 4, 0:C]
                    for u in range(4):
                        for hh in range(4):
                            fr, to = slice(32 * u, 32 * u + 32), slice(32 * hh, 32 * hh + 32)
                            src = hO[fr, 4 * b:4 * b + 4, :].rearrange("p v (g h d) -> p h g v d", h=4, d=D)[:, hh]
                            rd = hden[fr, 4 * b:4 * b + 4, :].rearrange("p v (g h) -> p h g v", h=4)[:, hh]
                            d = dst[to, :, 4 * u * D:4 * (u + 1) * D].rearrange("p g (v d) -> p g v d", v=4)
                            ins = dve.tensor_tensor(d, src, rd.unsqueeze(3).broadcast_to([32, 4, 4, D]), ALU.mult)
                    ins.then_inc(head_norm, 1)
                dve.wait_ge(head_norm, B)
                dve.memset(G[64:65, :, 4, :], 1.0).then_inc(preset, 1)
                dve.memset(ws[:, 0:4096], 0.0).then_inc(preset, 1)

            for n in range(NL):
                s = [0, 3, 7][n]
                if n == 1:
                    dve.wait_ge(x_done, 8)
                layernorm(s)
                mains(s, n, 0)
                if n == 1:
                    heads()
                else:
                    attention(n)
                mains(s + 1, n, None)
                gated(("proj", n), n, 0)
                dve.wait_ge(x_done, sent[0])
                layernorm(s + 2)
                mains(s + 2, n, 2)
                if n == 0:
                    for i in range(ROWS_IN_ATTENTION, ROT):
                        reflect_dots(i)
                        reflect_update(i)
                if n < NL - 1:
                    gated(("f2", n, 0), n, 1)
                    dve.wait_ge(x_done, sent[0])
                else:
                    o = full(dve, "logits")
                    dve.tensor_copy(lg[:].rearrange("p t e -> p (t e)"), o[:, 0:T * E]).then_inc(empty("logits"), 1)
                    evacuated(dve, "logits")
                    then(dve.tensor_reduce(m1[:], lg[:], AX.X, ALU.max))
                    other = lg[:].unsqueeze(2).broadcast_to([128, T, E, E])
                    own = lg[:].unsqueeze(3).broadcast_to([128, T, E, E])
                    dve.tensor_tensor(ahead, other, own, ALU.is_gt)
                    then(dve.tensor_tensor(tied, other, own, ALU.is_equal))
                    then(dve.tensor_tensor(tied, tied, tri[:].unsqueeze(1).broadcast_to([128, T, E, E]), ALU.mult))
                    then(dve.tensor_tensor(ahead, ahead, tied, ALU.add))
                    then(dve.tensor_reduce(cnt[:, 0], ahead, AX.X, ALU.add))
                    then(dve.tensor_scalar(cnt[:, 0], cnt[:, 0], 1.5, None, ALU.is_lt))
                    dve.tensor_tensor(cw[:], lg[:], m1[:].unsqueeze(2).broadcast_to([128, T, E]), ALU.subtract).then_inc(lg_ready, 1)
                    dve.wait_ge(lg_exp, 1)
                    then(dve.tensor_tensor(cw[:], cnt[:, 1], cnt[:, 0], ALU.mult))
                    then(dve.tensor_reduce(den[:], cw[:], AX.X, ALU.add))
                    then(dve.reciprocal(den[:], den[:]))
                    then(dve.tensor_tensor(cw[:], cw[:], den[:].unsqueeze(2).broadcast_to([128, T, E]), ALU.mult))
                    for e in range(E):
                        for pair in range(T // 2):
                            job = ("f2", n, e, pair)
                            o = full(dve, job)
                            for j in range(2):
                                tt = 2 * pair + j
                                if e == 0:
                                    ins = dve.tensor_scalar(acc[:, tt, :], o[:, j * C:(j + 1) * C], cw[:, tt, e:e + 1], None, ALU.mult)
                                else:
                                    ins = dve.scalar_tensor_tensor(acc[:, tt, :], o[:, j * C:(j + 1) * C], cw[:, tt, e:e + 1],
                                                                   acc[:, tt, :], ALU.mult, ALU.add)
                            ins.then_inc(empty(job), 1)
                            evacuated(dve, job)
                            if e == E - 1:
                                gt = gates[:, n, pair // 2, C:2 * C].unsqueeze(1).broadcast_to([128, 2, C])
                                xs, ac = x[:, 2 * pair:2 * pair + 2, :], acc[:, 2 * pair:2 * pair + 2, :]
                                then(dve.tensor_tensor(ac, ac, gt, ALU.mult))
                                dve.tensor_tensor(xs, xs, ac, ALU.add).then_inc(x_final, 1)
                if n == 1:
                    for tt in range(T):
                        dve.tensor_copy(xe[:, tt, 0:C], x[:, tt, :]).then_inc(xe_nat, 1)
                    mains(6, n, None)
                    subspace_map()
                    for pair in range(T // 2):
                        job = ("rot", pair)
                        o = full(dve, job)
                        xs = x[:, 2 * pair:2 * pair + 2, :].rearrange("p t c -> p (t c)")
                        ins = dve.tensor_tensor(xs, xs, o[:, 0:2 * C], ALU.add).then_inc(empty(job), 1)
                    evacuated(dve, job)

        @block.scalar
        def _(act):
            act.wait_ge(const_in, 16 * 7)
            act.activation(cA[:, 1, :], cA[:, 0, :], ACT.Exp, scale=-1.0).then_inc(silu_exp, 1)
            act.activation(cB[:, 1, :], cB[:, 0, :], ACT.Exp, scale=-1.0).then_inc(silu_exp, 1)
            def reflect_row(i):
                job = ("house", i)
                o = full(act, job)
                if i:
                    act.wait_ge(basis_updated, i)
                act.activation(vrow[:, i:C], o[:, 0:C - i], ACT.Copy).then_inc(vrow_ready, 1)
                act.activation(vsq[:, i:C], o[:, 0:C - i], ACT.Square, accum_out=qs[:, 0:1]).then_inc(empty(job), 1)

            def tails(s, n, kind):
                for half in range(2):
                    job = ("tB", s, half)
                    o = full(act, job)
                    for dst, rows in ((tB, slice(0, 96)), (tBf, slice(32, 64))):
                        d, r = by_quarters(dst[rows, half * L:(half + 1) * L], s), in_order(o[rows, :], s)
                        if kind is None:
                            ins = act.activation(d, r, ACT.Copy)
                        else:
                            ins = act.activation(d, r, ACT.Identity, scale=mod[rows, n, kind + 1, 1, half:half + 1],
                                                 bias=mod[rows, n, kind, 1, half:half + 1])
                    ins.then_inc(empty(job), 1)

            def out_copy(n, i):
                job = ("pv", n, i)
                act.activation(oT[:, i % 2, :], full(act, job), ACT.Copy).then_inc(empty(job), 1)

            def attention(n):
                for pair in range(T // 2):
                    job = ("v", n, pair)
                    o = full(act, job)
                    act.activation(Vh[:, 2 * pair:2 * pair + 2, :, 0:10].rearrange("p t h d -> p (t h) d"),
                                   o[:, 0:320].rearrange("p (h d) -> p h d", d=10), ACT.Copy).then_inc(empty(job), 1)
                for i in range(B * NG):
                    for part in range(2):
                        job = ("qk", n, i, part)
                        o = full(act, job)
                        if i:
                            evacuated(act, ("qk", n, i - 1, part))
                        act.activation(hi_tmp[:, part, :], o, ACT.Copy).then_inc(hi_done, 1)
                for m in range(16):
                    for step in row_steps(n, m):
                        reflect_row(step)
                for i in range(B * NG):
                    for kb in range(4):
                        for pr in range(2):
                            job = ("st", n, i, kb, pr)
                            full(act, job)
                            unit = ((n // 2 * 8 + i) * 4 + kb) * 2 + pr
                            act.activation(Pb[:, unit % 4], psum[:, 2 * pr:2 * pr + 2, :], ACT.Exp,
                                           scale=float(D) ** -0.5).then_inc(empty(job), 1)
                            for m in range(2):
                                for step in row_steps(n if i + 1 < B * NG else NL, ((i + 1) * 4 + kb) * 4 + 2 * pr + m):
                                    reflect_row(step)
                        if i >= 1 and kb == 0:
                            out_copy(n, i - 1)
                out_copy(n, B * NG - 1)

            def heads():
                for j in range(T):
                    job = ("hqkv", j)
                    act.activation(hq[:, j, :], full(act, job)[:, 0:3 * C], ACT.Copy).then_inc(empty(job), 1)
                for j in range(T):
                    act.wait_ge(hs_done, j + 1)
                    act.activation(hS[:, j % 4], hS[:, j % 4], ACT.Exp, scale=float(D) ** -0.5).then_inc(hp_done, 1)

            act.wait_ge(preset, 10)
            for n in range(NL):
                s = [0, 3, 7][n]
                evacuated(act, ("ada", n))
                tails(s, n, 0)
                if n == 1:
                    heads()
                else:
                    attention(n)
                tails(s + 1, n, None)
                tails(s + 2, n, 2)
                if n == 0:
                    for i in range(ROWS_IN_ATTENTION, ROT):
                        reflect_row(i)
                if n == NL - 1:
                    act.wait_ge(lg_ready, 1)
                    act.activation(cnt[:, 1], cw[:], ACT.Exp).then_inc(lg_exp, 1)
                func = ACT.Gelu if n == 1 else ACT.Gelu_apprx_tanh
                for e in range(E if n == NL - 1 else 1):
                    for b in range(B):
                        for m, (c0, w) in enumerate(MC):
                            job = ("f1", n, e, b, m)
                            o = full(act, job)
                            act.activation(G[0:w, b, m, :], o[0:w, :], func).then_inc(empty(job), 1)
                if n == 1:
                    tails(6, n, None)

        @block.gpsimd
        def _(pool):

            raised = {}

            def signal(ins, s):
                raised[s.name] = raised.get(s.name, 0) + 1
                ins.then_inc(s, 1)
                pool.wait_ge(s, raised[s.name])

            halves = [0]

            def tail_copies(half, job=None):
                if job == "heads":
                    pool.wait_ge(head_norm, half + 1)
                elif job:
                    evacuated(pool, job)
                else:
                    halves[0] += 1
                    pool.wait_ge(xe_nat, 4 * halves[0])
                rows = xe[:, 4 * half:4 * half + 4, :]
                for k in range(1, 3):
                    at = 128 + 32 * k
                    signal(pool.tensor_copy(rows[:, :, at:at + TAIL], rows[:, :, 128:C]), xe_dup)

            def tail_lows(s):
                for half in range(2):
                    evacuated(pool, ("tB", s, half))
                    cols = slice(half * L, (half + 1) * L)
                    signal(pool.tensor_tensor(tB[32:64, cols], tBf[32:64, cols], tB[32:64, cols].bitcast(F32),
                                       ALU.subtract), tB_done)

            def add_to_x(name):
                for pair in range(T // 2):
                    evacuated(pool, (*name, pair))
                    xs = x[:, 2 * pair:2 * pair + 2, :].rearrange("p t c -> p (t c)")
                    signal(pool.tensor_tensor(xs, xs, tmp[:, pair % 4, :], ALU.add), x_done)

            def max_rows(n, i):
                for c in (1, 3):
                    evacuated(pool, ("mx", n, i, 3, c))
                m = nmx[:, i % 2, :]
                signal(pool.tensor_copy(mhi[:, i % 2, :], m), pool_step)
                signal(pool.tensor_copy(mt[:, i % 2, 27::32], mhi[:, i % 2, :].bitcast(F32)), mt_done)
                signal(pool.tensor_tensor(mt[:, i % 2, 28::32], m, mhi[:, i % 2, :].bitcast(F32), ALU.subtract), mt_done)

            norms = [0]

            def rstds():
                norms[0] += 1
                pool.wait_ge(var_done, norms[0])
                signal(pool.tensor_tensor(rstd[:], vare[:], power[:, 0:T], ALU.pow), rstd_done)

            def attention(n):
                for i in range(B * NG):
                    evacuated(pool, ("qk", n, i, 1))
                    for dst, col in ((kE, 2), (kO, 3)):
                        signal(pool.tensor_scalar(dst[:, i, :], k_tmp[:, i % 2, :].bitcast(F32), neg_lo[:, col:col + 1], None,
                                           ALU.mult), k_done)
                for i in range(B * NG):
                    for m in range(16):
                        for step in row_steps(n, i * 16 + m, DOTS_AT):
                            reflector(step)
                    max_rows(n, i)
                    if i == 5:
                        tail_copies(0, ("ot", n, 3))
                tail_copies(1, ("ot", n, 7))

            def heads():
                for j in range(T):
                    evacuated(pool, ("hqkv", j))
                    if j >= 2:
                        pool.wait_ge(hs_done, j - 1)
                    q, k = (hq[:, j, p * C:(p + 1) * C].rearrange("p (h d) -> p h d", h=H) for p in range(2))
                    pj = prod[j % 2].rearrange("p (h k d) -> p h k d", h=H, k=H)
                    signal(pool.tensor_tensor(pj, q.unsqueeze(2).broadcast_to([128, H, H, D]),
                                              k.unsqueeze(1).broadcast_to([128, H, H, D]), ALU.mult), hprod_done)
                for half in range(2):
                    tail_copies(half, "heads")

            pool.wait_ge(rowsum, 1)
            signal(pool.partition_all_reduce(n1[:, 1:2], n1[:, 0:1], 128, RED.max), norm_max)

            def reflector(i):
                sigma, root, sign2, beta, den = (qs[:, c:c + 1] for c in range(5))
                alpha = vrow[:, i:i + 1]
                evacuated(pool, ("house", i))
                if i:
                    pool.wait_ge(basis_updated, i)
                signal(pool.tensor_tensor(root, sigma, power[:, T:T + 1], ALU.pow), pool_step)
                signal(pool.tensor_scalar(sign2, alpha, 0.0, -2.0, ALU.is_ge, ALU.mult), pool_step)
                signal(pool.tensor_scalar(beta, sign2, 1.0, root, ALU.add, ALU.mult), pool_step)
                signal(pool.tensor_scalar(den, alpha, beta, sigma, ALU.mult, ALU.subtract), pool_step)
                signal(pool.tensor_scalar(den, den, -1.0, 1e-30, ALU.mult, ALU.max), pool_step)
                signal(pool.tensor_scalar(ucol[:], QA[:, :, i], beta, None, ALU.mult), pool_step)
                pool.wait_ge(dots_done, i + 1)
                signal(pool.tensor_tensor(ucol[:], ucol[:], dots[:], ALU.subtract), pool_step)
                signal(pool.tensor_scalar(alpha, alpha, beta, None, ALU.subtract), reflector_done)

            for n in range(NL):
                s = [0, 3, 7][n]
                pool.wait_ge(raw_in, 16 * (n + 1))
                signal(pool.tensor_copy(WB[:, 0:COLS[n]], raw[0:96, 0:COLS[n]]), pool_step)
                signal(pool.tensor_tensor(WB[64:96, 0:COLS[n]], raw[64:96, 0:COLS[n]], WB[64:96, 0:COLS[n]].bitcast(F32),
                                   ALU.subtract), wb_done)
                rstds()
                for half in range(2):
                    tail_copies(half)
                tail_lows(s)
                if n == 1:
                    heads()
                else:
                    attention(n)
                tail_lows(s + 1)
                add_to_x(("proj", n))
                rstds()
                for half in range(2):
                    tail_copies(half)
                tail_lows(s + 2)
                if n == 0:
                    for i in range(ROWS_IN_ATTENTION, ROT):
                        reflector(i)
                if n < NL - 1:
                    add_to_x(("f2", n, 0))
                if n == 1:
                    for half in range(2):
                        tail_copies(half)
                    tail_lows(6)


def constants():
    import numpy as np

    ident = np.eye(128, dtype=np.float32)
    r = np.arange(128) % 32
    neg_lo = np.zeros((128, 4), np.float32)
    neg_lo[:, 0] = np.where((r >= D) & (r < 2 * D), -1, 0)
    neg_lo[:, 1] = np.where((r >= 2 * D) & (r < 3 * D), -1, 0)
    neg_lo[:, 2] = np.arange(128) // 32 % 2 == 0
    neg_lo[:, 3] = np.arange(128) // 32 % 2 == 1
    silu_fix = np.zeros((17, 2), np.float32)
    silu_fix[:16, 0] = 1
    silu_fix[16, 1] = 1
    tri = np.broadcast_to(np.tril(np.ones((E, E), np.float32), -1), (128, E, E))
    thr = np.broadcast_to(2.0 ** np.arange(NSQ, dtype=np.float32), (128, NSQ))
    sgn = np.triu(np.ones((ROT, ROT), np.float32), 1) - np.tril(np.ones((ROT, ROT), np.float32), -1)
    eye2 = np.tile(np.eye(ROT, dtype=np.float32), (2, 2))
    return {"ident": ident, "neg_lo": neg_lo, "silu_fix": silu_fix, "tri": tri, "thr": thr, "sgn": sgn, "eye2": eye2}


def lay_out(v):
    import numpy as np

    f = {k: np.asarray(a) for k, a in v.items()}
    a = constants()
    a["x"] = f["x"].reshape(B * L, C)
    cond = np.zeros((145, 2), np.float32)
    cond[:C] = f["cond_1152"].T
    a["condA"], a["condB"] = cond[:128], cond[128:]

    def with_bias(w, b):
        return np.concatenate([w, b.reshape(1, -1)], 0)

    def cols_tail3(w):
        o = np.zeros((w.shape[0], 224), np.float32)
        o[:, :128] = w[:, :128]
        for k in range(3):
            o[:, 128 + 32 * k:144 + 32 * k] = w[:, 128:]
        return o

    def rows_tail3(w):
        o = np.zeros((96, w.shape[1]), np.float32)
        for k in range(3):
            o[32 * k:32 * k + 17] = w[128:145]
        return o

    def qkv(w):
        q, k, vv = (w[:, j * C:(j + 1) * C].reshape(-1, H, D) for j in range(3))
        oq = np.zeros((w.shape[0], H, 32), np.float32)
        ok = np.zeros((w.shape[0], H, 32), np.float32)
        for j in range(3):
            oq[:, :, j * D:(j + 1) * D] = q
            ok[:, :, j * D:(j + 1) * D] = k
        ok[C, :, 27:29] = 1
        ov = np.zeros((w.shape[0], H, D + 1), np.float32)
        ov[:, :, :D] = vv
        ov[C, :, D] = 1
        return [o.reshape(w.shape[0], -1) for o in (oq, ok, ov)]

    def fc2(ws, bs):
        o = np.zeros((128, len(ws), 5, C), np.float32)
        for e, (w, b) in enumerate(zip(ws, bs)):
            for m, (c0, n) in enumerate(MC):
                o[:n, e, m] = w[c0:c0 + n]
            o[64, e, 4] = b
        return o

    names = [("L0_cond_W_qkv", "L0_cond_b_qkv", "L0_cond_W_proj", "L0_cond_b_proj", "L0_cond_W_ada", "L0_cond_b_ada"),
             ("L1_cond_qkv_w", "L1_cond_qkv_b", "L1_cond_proj_w", "L1_cond_proj_b", "L1_cond_ada_w", "L1_cond_ada_b"),
             ("L3_cond_w_qkv", "L3_cond_b_qkv", "L3_cond_w_proj", "L3_cond_b_proj", "L3_cond_w_adaln", "L3_cond_b_adaln")]
    ffs = [([f["L0_cond_W_fc1"]], [f["L0_cond_b_fc1"]], [f["L0_cond_W_fc2"]], [f["L0_cond_b_fc2"]]),
           ([f["L1_cond_fc1_w"]], [f["L1_cond_fc1_b"]], [f["L1_cond_fc2_w"]], [f["L1_cond_fc2_b"]]),
           (f["L3_cond_w1"], f["L3_cond_b1"], f["L3_cond_w2"], f["L3_cond_b2"])]
    for n, ((wq, bq, wp, bp, wa, ba), (w1, b1, w2, b2)) in enumerate(zip(names, ffs)):
        w = with_bias(f[wq], f[bq])
        if n == 1:
            parts = [np.concatenate([w, np.zeros((145, PC - 3 * C), np.float32)], 1)]
        else:
            parts = qkv(w)
        parts.append(with_bias(f[wp], f[bp]))
        parts += [with_bias(w, b) for w, b in zip(w1, b1)]
        if n == NL - 1:
            parts.append(with_bias(f["L3_cond_w_gate"], np.zeros(E, np.float32)))
        w = np.concatenate(parts, 1)
        a[f"wa{n}"] = w[:128]
        a[f"wb{n}"] = rows_tail3(w)
        a[f"w2{n}"] = fc2(w2, b2)
        w = with_bias(f[wa], f[ba])
        six = [w[:, k * C:(k + 1) * C] for k in range(6)]
        a[f"ada{n}"] = np.concatenate([cols_tail3(six[k]) for k in (0, 1, 3, 4)] + [six[2], six[5]], 1)

    iu, ju = np.triu_indices(ROT, 1)
    sk = np.zeros((145, ROT, ROT), np.float32)
    w = with_bias(f["L2_cond_W"].T, f["L2_cond_b"])
    sk[:, ju, iu] = w
    sk[:, iu, ju] = w
    a["skew_w"] = sk.reshape(145, -1)
    aug = np.zeros((256, C), np.float32)
    aug[:ROT] = f["L2_cond_P"].T
    aug[ROT:ROT + C] = np.eye(C, dtype=np.float32)
    a["aug"] = aug.reshape(2, 128, C).transpose(1, 0, 2)
    return {k: np.ascontiguousarray(z) for k, z in a.items()}


def kernel(**inputs):
    import concourse.bacc as bacc
    from concourse.bass_utils import run_bass_kernel_spmd

    arrays = lay_out(inputs)
    nc = bacc.Bacc("TRN2", target_bir_lowering=False, num_devices=1)
    t = {k: nc.dram_tensor(f"in_{k}", z.shape, F32, kind="ExternalInput").ap() for k, z in arrays.items()}
    out = nc.dram_tensor("x_out", (B * L, C), F32, kind="ExternalOutput").ap()
    build(nc, t, out)
    r = run_bass_kernel_spmd(nc, [{f"in_{k}": z for k, z in arrays.items()}], core_ids=[0])
    return r.results[0]["x_out"].reshape(B, L, C)
```

```python
from contextlib import ExitStack

import concourse.bass as bass
from concourse import mybir
from concourse.alu_op_type import AluOpType as ALU

F32 = mybir.dt.float32
F32R = mybir.dt.float32r
ACT = mybir.ActivationFunctionType
AX = mybir.AxisListType
RED = bass.bass_isa.ReduceOp

B, L, C = 2, 512, 144
T = B * L // 128
H, D = 16, 9
FF = 4 * C
E = 4
NL = 3
TAIL = C - 128
ROT = 64
GR = 4
NG = H // GR
EPS = 1e-6
MC = [(0, 128), (128, 128), (256, 128), (384, 128), (512, 64)]

QC, KC, VC, PC, W1C = 0, 512, 1024, 1184, 1328
COLS = [W1C + FF, W1C + FF, W1C + E * FF + E]
GC = W1C + E * FF
NSQ = 16
TAYLOR = 12
EXPM_BANK = 5
MASKS_ON_ACT = 2
SCORES_AFTER = 6
UNITS = 4 * B * NG


def unit_of(v):
    return divmod(v, 4) if 0 <= v < UNITS else None


ROW_PERIOD, ROW_AT, DOTS_AT, UPDATE_AT = 6, 0, 1, 4
ROWS_IN_ATTENTION = (8 * 16 - UPDATE_AT - 1) // ROW_PERIOD + 1


ROWS_IN_MLP = 6
HEADS_ROW = ROT - 2 * T - ROWS_IN_MLP
HEADS_END = HEADS_ROW + 2 * T
FIRST_ROWS = HEADS_ROW - ROWS_IN_ATTENTION - ROWS_IN_MLP


def row_steps(n, m, at=ROW_AT):
    step, off = divmod(m - at, ROW_PERIOD)
    return [FIRST_ROWS + step] if n == 0 and off == 0 and 0 <= step < ROWS_IN_ATTENTION else []


def mlp_step(n, b, m):
    first = [HEADS_ROW - ROWS_IN_MLP, HEADS_END, None][n]
    place = {(0, 2): 0, (0, 4): 1, (1, 2): 2, (1, 4): 3, (2, 0): 4, (2, 1): 5}.get((b, m))
    return [] if first is None or place is None else [first + place]


def expm_steps(j):
    return [10 + j] if j < T else []


def mlp_expm(n, b, m):
    return [] if n == 2 else [(0, 10 + T)[n] + 5 * b + m]


assert TAYLOR + NSQ == 2 * 5 * B + T


def build(nc, t, out):
    with ExitStack() as ctx:
        def sb(name, shape, dt=F32):
            return ctx.enter_context(nc.sbuf_tensor(name, shape, dt))

        def sem(name):
            return ctx.enter_context(nc.semaphore(name))

        psum = ctx.enter_context(nc.psum_tensor("psum", [128, 8, 512], F32))

        ident = sb("ident", [128, 128])
        neg_lo = sb("neg_lo", [128, 2 + GR])
        silu_fix = sb("silu_fix", [17, 2])
        tri = sb("tri", [128, E, E])
        x = sb("x", [128, T, C])
        xe = sb("xe", [128, T, 224])
        tA = sb("tA", [128, B * L])
        tB = sb("tB", [96, B * L], F32R)
        q1 = sb("q1", [128, 2, 512], F32R)
        km = sb("km", [128, 3, GR, 512], F32R)
        hi_tmp = sb("hi_tmp", [128, 2, 512], F32R)
        k_tmp = sb("k_tmp", [128, 512])
        q2 = sb("q2", [128, 2, 512], F32R)
        ws = sb("ws", [128, 8192])
        Vh = ws[:, 0:4096].rearrange("p (t h d) -> p t h d", t=T, h=H)
        Pb = ws[:, 4096:8192].rearrange("p (n s q) -> p n s q", n=4, s=2)
        mt = sb("mt", [128, 2, 512])
        nmx = sb("nmx", [128, 2, 16])
        mhi = sb("mhi", [128, 2, 16], F32R)
        oT = sb("oT", [128, 2, 512])
        tBf = oT[:].rearrange("p s q -> p (s q)")
        rden = sb("rden", [128, 16])
        G = sb("G", [128, B, 5, 512])
        Gf = G[:].rearrange("p b m q -> p (b m q)")
        adaA = [Gf[:, 2368 * s:2368 * s + 1184] for s in range(2)]
        adaB = [Gf[0:17, 2368 * s + 1184:2368 * s + 2368] for s in range(2)]
        skA, skB = ws[:, 0:4096], ws[0:17, 4096:8192]
        hq = Gf[:, 0:T * 3 * C].rearrange("p (t c) -> p t c", t=T)
        prod = [ws[:, k * H * H * D:(k + 1) * H * H * D] for k in range(3)]
        hden = ws[:, 6912:6912 + T * H].rearrange("p (t h) -> p t h", t=T)
        hmax = ws[:, 7040:7040 + 2 * H].rearrange("p (t h) -> p t h", t=2)
        tmp = sb("tmp", [128, 4, 2 * C])
        acc = tmp[:].rearrange("p n c -> p (n c)").rearrange("p (t c) -> p t c", c=C)
        WA = sb("WA", [128, COLS[2]])
        WB = sb("WB", [96, COLS[2]], F32R)
        W2 = sb("W2", [128, E, 5, C])
        WAs = [WA, sb("WA1", [128, COLS[1]]), WA]
        WBs = [WB, sb("WB1", [96, COLS[1]], F32R), WB]
        W2s = [W2, sb("W21", [128, 1, 5, C]), W2]
        spare = W2[:, 1:E].rearrange("p e m c -> p (e m c)")
        raws = [spare, spare, ws[:, 4096:8192]]
        cA = sb("cA", [128, 4, B])
        cB = sb("cB", [17, 4, B])
        srepA = sb("srepA", [128, B, 128])
        srepB = sb("srepB", [17, B, 128])
        mod = sb("mod", [128, NL, 4, 2, B])
        gates = sb("gates", [128, NL, B, 2 * C])
        stats = sb("stats", [128, T, 6])
        mv = sb("mv", [128, T, 2])
        rstd = sb("rstd", [128, T])
        vare = sb("vare", [128, T])
        power = sb("power", [128, T + 1])
        sgn = sb("sgn", [ROT, ROT])
        thr = sb("thr", [128, NSQ])
        eye2 = sb("eye2", [128, 2 * ROT])
        skew = sb("skew", [128, ROT])
        skp = sb("skp", [128, 2, ROT])
        n1 = sb("n1", [128, 2])
        sq = sb("sq", [128, 3, NSQ])
        Rm = sb("Rm", [128, 2, ROT])
        Rk = sb("Rk", [128, 2, ROT])
        QA = sb("QA", [128, 2, C])
        vrow = sb("vrow", [128, C])
        vsq = sb("vsq", [128, C])
        qs = sb("qs", [128, 8])
        junk = sb("junk", [128, 2, C])
        tiny = sb("tiny", [128, 1])
        dots = sb("dots", [128, 2])
        ucol = sb("ucol", [128, 2])
        UTx = sb("UTx", [128, 224])
        RU = sb("RU", [128, C])
        MA = sb("MA", [128, B, C])
        MB = sb("MB", [96, B, C], F32R)
        hS = tBf.rearrange("p (n h k) -> p n h k", n=4, h=H)
        hO = tmp[:].rearrange("p n c -> p (n c)").rearrange("p (t c) -> p t c", c=C)
        Rm_flat = Rm[:].rearrange("p s n -> p (s n)")
        Rk_flat = Rk[:].rearrange("p s n -> p (s n)")
        MBf = tmp[0:96, 0, :].rearrange("p (b c) -> p b c", b=B)
        lg = sb("lg", [128, T, E])
        m1 = sb("m1", [128, T])
        ahead, tied = (mt[:, k, 0:T * E * E].rearrange("p (t e f) -> p t e f", t=T, e=E) for k in range(2))
        cnt = sb("cnt", [128, 2, T, E])
        cw = sb("cw", [128, T, E])
        den = sb("den", [128, T])

        filled = [sem(f"bank{k}_filled") for k in range(8)]
        drained = [sem(f"bank{k}_drained") for k in range(8)]
        const_in = sem("const_in")
        tables_in = sem("tables_in")
        ada_in = [sem(f"ada{n}_in") for n in range(NL)]
        wa_in = [sem(f"weights{n}_in") for n in range(NL)]
        raw_in = [sem(f"tail_weights{n}_in") for n in range(NL)]
        wb_high = sem("wb_high")
        skew_in = sem("skew_in")
        x_in = sem("x_in")
        sgn_in = sem("sgn_in")
        basis_in = sem("basis_in")
        preset = sem("preset")
        silu_exp = sem("silu_exp")
        silu_done = sem("silu_done")
        wb_done = sem("wb_done")
        xe_nat = sem("xe_nat")
        xe_dup = sem("xe_dup")
        tB_done = sem("tB_done")
        hi_done = sem("hi_done")
        km_act = sem("km_act")
        km_pool = sem("km_pool")
        mt_done = sem("mt_done")
        x_done = sem("x_done")
        x_final = sem("x_final")
        norm_max = sem("norm_max")
        rm_init = sem("rm_init")
        rm_less_one = sem("rm_less_one")
        rowsum = sem("rowsum")
        vrow_ready = sem("vrow_ready")
        dots_done = sem("dots_done")
        reflector_done = sem("reflector_done")
        row_updated = sem("row_updated")
        basis_updated = sem("basis_updated")
        var_done = sem("var_done")
        rstd_done = sem("rstd_done")
        kept_done = sem("kept_done")
        ut_done = sem("ut_done")
        m_done = sem("m_done")
        lg_exp = sem("lg_exp")
        hprod_done = sem("hprod_done")
        hsum_done = sem("hsum_done")
        hs_done = sem("hs_done")
        hp_done = sem("hp_done")
        ho_done = sem("ho_done")
        head_norm = sem("head_norm")
        head_rows = [sem(f"head_rows{b}") for b in range(B)]
        values_done = sem("values_done")
        ones_set = sem("ones_set")
        pads_set = sem("pads_set")
        lg_ready = sem("lg_ready")
        stored = sem("stored")
        dve_step = sem("dve_step")
        pool_step = sem("pool_step")

        ada_h = [t[f"ada{n}"] for n in range(NL)]
        block = ctx.enter_context(nc.Block())

        use = {}
        uses = [0] * 8

        def full(eng, job):
            k, n = use[job]
            eng.wait_ge(filled[k], n)
            return psum[:, k, :]

        def empty(job):
            return drained[use[job][0]]

        def evacuated(eng, job):
            k, n = use[job]
            eng.wait_ge(drained[k], n)

        def by_quarters(ap, s):
            return ap.rearrange("p (v u a) -> p a u v", v=4, u=4) if s == 3 else ap

        def in_order(ap, s):
            return ap.rearrange("p (a u v) -> p a u v", u=4, v=4) if s == 3 else ap

        def head_block(b, u, hh):
            src = hO[32 * u:32 * u + 32, 4 * b:4 * b + 4, :].rearrange("p v (g h d) -> p h g v d", h=4, d=D)[:, hh]
            dst = xe[32 * hh:32 * hh + 32, 4 * b:4 * b + 4, 4 * u * D:4 * (u + 1) * D]
            return dst.rearrange("p g (v d) -> p g v d", v=4), src

        @block.tensor
        def _(pe):
            def claim(job, k):
                if uses[k]:
                    pe.wait_ge(drained[k], uses[k])
                uses[k] += 1
                use[job] = (k, uses[k])
                return psum[:, k, :]

            def tail_mm(o, lhsT, rhs, stop=True):
                return pe.matmul(o, lhsT, rhs, start=False, stop=stop)

            def ada_vectors(n, part):
                if part == 0:
                    pe.wait_ge(ada_in[n], 32)
                    claim(("ada", n), 6)
                o = psum[:, 6, :]
                for kind in (2 * part, 2 * part + 1):
                    for ab, (c0, m) in enumerate(((0, 128), (128, 96))):
                        at = (kind * 2 + ab) * B
                        c = kind * 224 + c0
                        pe.matmul(o[0:m, at:at + B], adaA[n % 2][:, c:c + m], cA[:, 3, :], start=True, stop=False)
                        last = tail_mm(o[0:m, at:at + B], adaB[n % 2][:, c:c + m], cB[:, 3, :])
                if part == 1:
                    last.then_inc(filled[6], 1)

            def gate_vectors(n):
                for b in range(B):
                    k = 6 - 2 * b
                    o = claim(("gate", n, b), k)
                    pe.matmul(o[:, 0:2 * C], srepA[:, b, :], adaA[n % 2][:, 896:1184], start=True, stop=False)
                    tail_mm(o[:, 0:2 * C], srepB[:, b, :], adaB[n % 2][:, 896:1184]).then_inc(filled[k], 1)

            def generators(part):
                if part == 0:
                    pe.wait_ge(skew_in, 32)
                    claim("skew", 5)
                o = psum[:, 5, :]
                for j in range(ROT // 8 * part, ROT // 8 * (part + 1)):
                    pe.matmul(o[0:ROT, 2 * j:2 * j + 2], skA[:, j * ROT:(j + 1) * ROT], cA[:, 3, :], start=True, stop=False)
                    last = tail_mm(o[0:ROT, 2 * j:2 * j + 2], skB[:, j * ROT:(j + 1) * ROT], cB[:, 3, :])
                if part == 7:
                    last.then_inc(filled[5], 1)

            def exponential(k):
                if k == 0:
                    pe.wait_ge(rm_init, 1)
                o = claim(("expm", k), EXPM_BANK)
                if k:
                    evacuated(pe, ("expm", k - 1))
                for b in range(B):
                    rows = slice(64 * b, 64 * b + 64)
                    for s in range(2):
                        left = skp[rows, s, :] if k < TAYLOR else Rm[rows, 1 - s, :]
                        last = pe.matmul(o[rows, s * ROT:(s + 1) * ROT], left, Rm[rows, s, :], start=True, stop=True)
                last.then_inc(filled[EXPM_BANK], 1)

            def reflect_row(i):
                if i:
                    pe.wait_ge(row_updated, i)
                o = claim(("house", i), 7)
                pe.matmul(o[:, 0:C - i], ident[0:ROT, i:i + 1].broadcast_to([ROT, 128]), QA[0:ROT, 0, i:C],
                          start=True, stop=True).then_inc(filled[7], 1)

            def subspace_map():
                pe.wait_ge(basis_updated, ROT)
                o = claim("UT", 6)
                pe.transpose(o[0:ROT, 0:64], QA[64:128, 0, 0:ROT], ident[64:128, 64:128])
                pe.transpose(o[0:ROT, 64:C], QA[0:80, 1, 0:ROT], ident[0:80, 0:80]).then_inc(filled[6], 1)
                pe.wait_ge(ut_done, 1)
                pe.wait_ge(rm_less_one, 1)
                o = claim("RU", 6)
                for b in range(B):
                    rows = slice(64 * b, 64 * b + 64)
                    last = pe.matmul(o[rows, 0:C], Rm[rows, 1, :], UTx[rows, 0:C], start=True, stop=True)
                last.then_inc(filled[6], 1)
                evacuated(pe, "RU")
                for b in range(B):
                    o = claim(("MA", b), 6)
                    rows = slice(64 * b, 64 * b + 64)
                    pe.matmul(o[:, 0:C], UTx[rows, 0:128], RU[rows, :], start=True, stop=True)
                    pe.matmul(o[0:96, C:2 * C], UTx[rows, 128:224], RU[rows, :], start=True, stop=True).then_inc(filled[6], 1)

            pe.wait_ge(const_in, 16 * 4)
            pe.wait_ge(silu_done, 1)
            def to_features(s):
                for half in range(2):
                    pe.wait_ge(xe_dup, 2 * (2 * s + half + 1))
                    o = claim(("tA", s, half), 2 * half)
                    for j in range(4):
                        last = pe.transpose(o[:, j * 128:(j + 1) * 128], xe[:, 4 * half + j, 0:128], ident[:])
                    last.then_inc(filled[2 * half], 1)
                    o = claim(("tB", s, half), 2 * half + 1)
                    for j in range(4):
                        last = pe.transpose(o[0:96, j * 128:(j + 1) * 128], xe[:, 4 * half + j, 128:224], ident[:])
                    last.then_inc(filled[2 * half + 1], 1)

            for i in range(FIRST_ROWS):
                if i == 0:
                    pe.wait_ge(basis_in, 16)
                    pe.wait_ge(const_in, 16 * 4)
                reflect_row(i)
                if i == 0:
                    pe.wait_ge(silu_done, 1)
                if i < 2:
                    ada_vectors(0, i)
                if i == 2:
                    gate_vectors(0)
                if i == 3:
                    to_features(0)
                if 3 <= i < 11:
                    generators(i - 3)
                for n in (1, 2):
                    if i == 9 + 2 * n:
                        ada_vectors(n, 0)
                        ada_vectors(n, 1)
                    if i == 10 + 2 * n:
                        gate_vectors(n)

            def ready(s, half):
                evacuated(pe, ("tA", s, half))
                pe.wait_ge(tB_done, 2 * s + half + 1)

            def token_major(name, s, wa, wb, width, banks):
                for pair in range(T // 2):
                    if pair % 2 == 0:
                        ready(s, pair // 2)
                    k = banks[pair % len(banks)]
                    o = claim((*name, pair), k)
                    for j in range(2):
                        tok = slice((2 * pair + j) * 128, (2 * pair + j + 1) * 128)
                        pe.matmul(o[:, j * width:(j + 1) * width], tA[:, tok], wa(pair // 2), start=True, stop=False)
                        last = tail_mm(o[:, j * width:(j + 1) * width], tB[:, tok], wb(pair // 2))
                    last.then_inc(filled[k], 1)

            def st_mm(n, i, kb, half):
                if kb == 0 and half == 0:
                    evacuated(pe, ("mt", n, i))
                claim(("st", n, i, kb, half), 2 * half)
                for s in range(2):
                    last = pe.matmul(psum[:, 2 * half + s, :], km[:, i % 3, 2 * s + half, kb * 128:(kb + 1) * 128],
                                     q2[:, i % 2, :], start=True, stop=True)
                last.then_inc(filled[2 * half], 1)

            def pv_mm(n, i, kb):
                if kb == 0:
                    claim(("pv", n, i), 6)
                unit = ((n // 2 * 8 + i) * 4 + kb) * 2
                for pr in range(2):
                    evacuated(pe, ("st", n, i, kb, pr))
                for c in range(GR):
                    pr, s = c % 2, c // 2
                    last = pe.matmul(psum[32 * c:32 * c + 32, 6, :], Vh[:, (i // NG) * 4 + kb, (i % NG) * GR + c, :],
                                     Pb[:, (unit + pr) % 4, s, :], start=(kb == 0), stop=(kb == 3))
                if kb == 3:
                    last.then_inc(filled[6], 1)

            def mx_mm(n, i, qt, j):
                for c in ((0, 2, 1, 3)[j],):
                    k = 4 + j % 2
                    o = claim(("mx", n, i, qt, c), k)
                    pe.matmul(o, q1[:, i % 2, qt * 128:(qt + 1) * 128], km[:, i % 3, c, :],
                              start=True, stop=True).then_inc(filled[k], 1)
                    for step in row_steps(n, (i * 4 + qt) * 4 + j):
                        reflect_row(step)

            def mt_mm(n, i):
                pe.wait_ge(mt_done, 2 * (n // 2 * 8 + i + 1))
                o = claim(("mt", n, i), 7)
                for qt in range(4):
                    last = pe.transpose(o[:, qt * 128:(qt + 1) * 128], mt[:, i % 2, qt * 128:(qt + 1) * 128], ident[:])
                last.then_inc(filled[7], 1)

            def ot_mm(n, i):
                evacuated(pe, ("pv", n, i))
                o = claim(("ot", n, i), 7)
                for qt in range(4):
                    last = pe.transpose(o[:, qt * 128:(qt + 1) * 128], oT[:, i % 2, qt * 128:(qt + 1) * 128], ident[:])
                last.then_inc(filled[7], 1)

            def hidden(n, e, b, s):
                ready(s, b)
                for m, (c0, w) in enumerate(MC):
                    k = m % 4
                    o = claim(("f1", n, e, b, m), k)
                    c = W1C + e * FF + c0
                    pe.matmul(o[0:w, :], WAs[n][:, c:c + w], tA[:, b * L:(b + 1) * L], start=True, stop=False)
                    tail_mm(o[0:w, :], WBs[n][:, c:c + w], tB[:, b * L:(b + 1) * L]).then_inc(filled[k], 1)
                    for step in mlp_step(n, b, m):
                        reflect_row(step)
                    for step in mlp_expm(n, b, m):
                        exponential(step)

            def back(n, e, b):
                for m in range(1, 5):
                    evacuated(pe, ("f1", n, e, b, m))
                for pair in range(2):
                    k = 4 + (2 * b + pair) % 4
                    o = claim(("f2", n, e, 2 * b + pair), k)
                    for j in range(2):
                        tok = slice((2 * pair + j) * 128, (2 * pair + j + 1) * 128)
                        for m, (c0, w) in enumerate(MC):
                            w += m == 4
                            last = pe.matmul(o[:, j * C:(j + 1) * C], G[0:w, b, m, tok], W2s[n][0:w, e, m, :],
                                             start=(m == 0), stop=(m == 4))
                    last.then_inc(filled[k], 1)
                    for step in mlp_step(n, 2, 2 * b + pair):
                        reflect_row(step)

            def qk_mm(n, s, i, part):
                b, g = divmod(i, NG)
                o = claim(("qk", n, i, part), 7)
                c = (QC, KC)[part] + g * 128
                pe.matmul(o, WAs[n][:, c:c + 128], tA[:, b * L:(b + 1) * L], start=True, stop=False)
                tail_mm(o, WBs[n][:, c:c + 128], tB[:, b * L:(b + 1) * L]).then_inc(filled[7], 1)

            def attention_mm(n, s):
                token_major(("v", n), s, lambda b, n=n: WAs[n][:, VC:VC + 160], lambda b, n=n: WBs[n][:, VC:VC + 160], 160, [4, 5, 6, 7])
                qk_mm(n, s, 0, 1)
                qk_mm(n, s, 0, 0)
                for pair in range(T // 2):
                    evacuated(pe, ("v", n, pair))
                if n == 2:
                    pe.wait_ge(pads_set, 1)
                for u in range(UNITS + SCORES_AFTER + 2):
                    g, part = divmod(u, 4)
                    maxima, scores, values = unit_of(u), unit_of(u - SCORES_AFTER), unit_of(u - SCORES_AFTER - 1)
                    if maxima and part == 0:
                        evacuated(pe, ("qk", n, g, 0))
                        pe.wait_ge(km_act, MASKS_ON_ACT * (n // 2 * 8 + g + 1))
                        pe.wait_ge(km_pool, (GR - MASKS_ON_ACT) * (n // 2 * 8 + g + 1))
                    for half in range(2):
                        if scores:
                            st_mm(n, *scores, half)
                        if maxima:
                            mx_mm(n, *maxima, 2 * half)
                        if half == 0:
                            if values:
                                pv_mm(n, *values)
                            if part == 0 and 0 <= g - 3 < B * NG:
                                ot_mm(n, g - 3)
                        elif part == 0 and 0 <= g - 1 < B * NG:
                            mt_mm(n, g - 1)
                        elif part in (1, 2) and g + 1 < B * NG:
                            qk_mm(n, s, g + 1, part == 1)
                        if maxima:
                            mx_mm(n, *maxima, 2 * half + 1)
                ot_mm(n, B * NG - 1)

            for n in range(NL):
                s = [0, 3, 7][n]
                if n:
                    to_features(s)
                pe.wait_ge(wa_in[n], 32)
                pe.wait_ge(wb_done, n + 1)
                if n == 1:
                    for j in range(T):
                        b, v = divmod(j, 4)
                        if v == 0:
                            ready(s, b)
                        o = claim(("hqkv", j), j)
                        tok = slice(j * 128, (j + 1) * 128)
                        pe.matmul(o[:, 0:3 * C], tA[:, tok], WAs[n][:, 0:3 * C], start=True, stop=False)
                        tail_mm(o[:, 0:3 * C], tB[:, tok], WBs[n][:, 0:3 * C]).then_inc(filled[j], 1)
                    reflect_row(HEADS_ROW)
                    for j in range(T + 1):
                        for part in range(3):
                            for k in expm_steps(j)[part:part + 1]:
                                exponential(k)
                            i = HEADS_ROW + 2 * j + 1 + part
                            if part < 2 and i < HEADS_END:
                                reflect_row(i)
                        for k in expm_steps(j)[3:]:
                            exponential(k)
                else:
                    attention_mm(n, s)
                to_features(s + 1)
                token_major(("proj", n), s + 1, lambda b, n=n: WAs[n][:, PC:PC + C], lambda b, n=n: WBs[n][:, PC:PC + C], C, [4, 5, 6, 7])
                to_features(s + 2)
                if n == NL - 1:
                    o = claim("logits", 7)
                    for tt in range(T):
                        ready(s + 2, tt // 4)
                        tok = slice(tt * 128, (tt + 1) * 128)
                        pe.matmul(o[:, tt * E:(tt + 1) * E], tA[:, tok], WAs[n][:, GC:GC + E], start=True, stop=False)
                        last = tail_mm(o[:, tt * E:(tt + 1) * E], tB[:, tok], WBs[n][:, GC:GC + E])
                    last.then_inc(filled[7], 1)
                if n == 1:
                    pe.wait_ge(ones_set, 1)
                for e in range(E if n == NL - 1 else 1):
                    for b in range(B):
                        hidden(n, e, b, s + 2)
                        if b == 1:
                            back(n, e, 0)
                    back(n, e, 1)
                if n == 1:
                    to_features(6)
                    subspace_map()
                    pe.wait_ge(m_done, 2)
                    token_major(("rot",), 6, lambda b: MA[:, b, :], lambda b: MB[:, b, :], C, [4, 5, 6, 7])

        @block.sync
        def _(sp):
            sp.dma_start(QA[:], t["aug"]).then_inc(basis_in, 16)
            for name, dst in (("ident", ident[:]), ("condA", cA[:, 0, :]), ("condB", cB[:, 0, :]), ("silu_fix", silu_fix[:])):
                sp.dma_start(dst, t[name]).then_inc(const_in, 16)

            def vectors(n):
                sp.dma_start(adaA[n % 2], ada_h[n][0:128, :]).then_inc(ada_in[n], 16)
                sp.dma_start(adaB[n % 2], ada_h[n][128:145, :]).then_inc(ada_in[n], 16)

            def weights(n):
                sp.dma_start(WAs[n][:, 0:COLS[n]], t[f"wa{n}"]).then_inc(wa_in[n], 16)
                ne = E if n == NL - 1 else 1
                if n == NL - 1:
                    sp.wait_ge(wb_done, 2)
                sp.dma_start(W2s[n][:, 0:ne, :, :], t[f"w2{n}"]).then_inc(wa_in[n], 16)

            def tail_weights(n):
                sp.dma_start(raws[n][0:96, 0:COLS[n]], t[f"wb{n}"]).then_inc(raw_in[n], 16)

            vectors(0)
            for name, dst in (("neg_lo", neg_lo[:]), ("tri", tri[:]), ("thr", thr[:])):
                sp.dma_start(dst, t[name]).then_inc(tables_in, 16)
            sp.dma_start(x[:], t["x"].rearrange("(t p) c -> p t c", p=128)).then_inc(x_in, 16)
            sp.dma_start(skA, t["skew_w"][0:128, :]).then_inc(skew_in, 16)
            sp.dma_start(skB, t["skew_w"][128:145, :]).then_inc(skew_in, 16)
            for name, dst in (("sgn", sgn[:]), ("eye2", eye2[:])):
                sp.dma_start(dst, t[name]).then_inc(sgn_in, 16)
            tail_weights(0)
            weights(0)
            vectors(1)
            for b in range(B):
                evacuated(sp, ("gate", 0, b))
            vectors(2)
            sp.wait_ge(wb_done, 1)
            tail_weights(1)
            weights(1)
            sp.wait_ge(x_done, 8)
            weights(2)
            sp.wait_ge(head_norm, T)
            tail_weights(2)
            for pair in range(T // 2):
                sp.wait_ge(x_final, pair + 1)
                sp.dma_start(out.rearrange("(t p) c -> p t c", p=128)[:, 2 * pair:2 * pair + 2, :],
                             x[:, 2 * pair:2 * pair + 2, :]).then_inc(stored, 16)
            sp.wait_ge(stored, 16 * (T // 2))

        @block.vector
        def _(dve):
            steps = [0]

            def then(ins):
                steps[0] += 1
                ins.then_inc(dve_step, 1)
                dve.wait_ge(dve_step, steps[0])

            dve.memset(mt[:], 0.0).then_inc(preset, 1)
            dve.memset(xe[:], 0.0).then_inc(preset, 1)
            dve.wait_ge(preset, 2)
            for k in range(3):
                at = 128 + 32 * k + TAIL
                dve.memset(xe[:, :, at:at + 1], 1.0).then_inc(preset, 1)
            dve.memset(UTx[:], 0.0).then_inc(preset, 1)
            dve.memset(tiny[:], 1e-15)
            dve.memset(power[:, 0:T], -0.5).then_inc(preset, 1)
            dve.memset(power[:, T:T + 1], 0.5).then_inc(preset, 1)
            dve.wait_ge(preset, 8)

            dve.wait_ge(silu_exp, 2)
            dve.tensor_scalar(cA[:, 2, :], cA[:, 1, :], 1.0, None, ALU.add)
            then(dve.tensor_scalar(cB[:, 2, :], cB[:, 1, :], 1.0, None, ALU.add))
            dve.reciprocal(cA[:, 2, :], cA[:, 2, :])
            then(dve.reciprocal(cB[:, 2, :], cB[:, 2, :]))
            dve.tensor_tensor(cA[:, 3, :], cA[:, 0, :], cA[:, 2, :], ALU.mult)
            then(dve.tensor_tensor(cB[:, 2, :], cB[:, 0, :], cB[:, 2, :], ALU.mult))
            then(dve.tensor_scalar(cB[:, 3, :], cB[:, 2, :], silu_fix[:, 0:1], silu_fix[:, 1:2], ALU.mult, ALU.add))
            dve.tensor_copy(srepA[:], cA[:, 3, :].unsqueeze(2).broadcast_to([128, B, 128]))
            dve.tensor_copy(srepB[:], cB[:, 3, :].unsqueeze(2).broadcast_to([17, B, 128])).then_inc(silu_done, 1)

            def ada_vectors(n):
                v = full(dve, ("ada", n))[:, 0:16].rearrange("p (k a b) -> p k a b", k=4, a=2)
                for kind in range(4):
                    dve.tensor_scalar(mod[:, n, kind, 0, :], v[:, kind, 0, :], float(kind % 2), None, ALU.add)
                    ins = dve.tensor_scalar(mod[0:96, n, kind, 1, :], v[0:96, kind, 1, :], float(kind % 2), None, ALU.add)
                ins.then_inc(empty(("ada", n)), 1)

            def gate_vectors(n):
                for b in range(B):
                    o = full(dve, ("gate", n, b))
                    dve.tensor_copy(gates[:, n, b, :], o[:, 0:2 * C]).then_inc(empty(("gate", n, b)), 1)

            def generators():
                dve.wait_ge(sgn_in, 32)
                o = full(dve, "skew")
                for b in range(B):
                    ins = dve.tensor_tensor(skew[64 * b:64 * b + 64, :], o[0:ROT, b:2 * ROT:2], sgn[:], ALU.mult)
                ins.then_inc(empty("skew"), 1)
                evacuated(dve, "skew")
                dve.tensor_reduce(n1[:, 0:1], skew[:], AX.X, ALU.add, apply_absolute_value=True).then_inc(rowsum, 1)

            def exponential_start():
                dve.wait_ge(norm_max, 1)
                then(dve.tensor_tensor(sq[:, 0], n1[:, 1:2].broadcast_to([128, NSQ]), thr[:], ALU.is_gt))
                dve.tensor_scalar(sq[:, 1], sq[:, 0], -1.0, 1.0, ALU.mult, ALU.add)
                then(dve.tensor_scalar(sq[:, 2], sq[:, 0], -0.5, 1.0, ALU.mult, ALU.add))
                w = NSQ
                while w > 1:
                    w //= 2
                    then(dve.tensor_tensor(sq[:, 2, 0:w], sq[:, 2, 0:w], sq[:, 2, w:2 * w], ALU.mult))
                then(dve.tensor_scalar(skp[:, 1, :], skew[:], sq[:, 2, 0:1], None, ALU.mult))
                dve.tensor_scalar(skp[:, 0, :], skp[:, 1, :], -1.0, None, ALU.mult)
                dve.tensor_copy(Rm_flat, eye2[:]).then_inc(rm_init, 1)

            def exponential(k):
                job = ("expm", k)
                o = full(dve, job)[:, 0:2 * ROT]
                if k < TAYLOR:
                    dve.scalar_tensor_tensor(Rm_flat, o, 1.0 / (TAYLOR - k), eye2[:], ALU.mult, ALU.add).then_inc(empty(job), 1)
                else:
                    dve.wait_ge(kept_done, k - TAYLOR + 1)
                    dve.scalar_tensor_tensor(Rm_flat, o, sq[:, 0, k - TAYLOR:k - TAYLOR + 1], Rk_flat,
                                             ALU.mult, ALU.add).then_inc(empty(job), 1)

            def exponential_end():
                evacuated(dve, ("expm", TAYLOR + NSQ - 1))
                dve.tensor_tensor(Rm_flat, Rm_flat, eye2[:], ALU.subtract).then_inc(rm_less_one, 1)

            def reflect_dots(i):
                dve.wait_ge(vrow_ready, i + 1)
                if i:
                    dve.wait_ge(basis_updated, i)
                for c in range(2):
                    ins = dve.tensor_tensor_reduce(out=junk[:, c, i:C], in0=QA[:, c, i:C], in1=vrow[:, i:C], scale=1.0,
                                                   scalar=0.0, op0=ALU.mult, op1=ALU.add, accum_out=dots[:, c:c + 1])
                ins.then_inc(dots_done, 1)

            def reflect_update(i):
                dve.wait_ge(reflector_done, i + 1)
                dve.wait_ge(dots_done, i + 1)
                beta, den = qs[:, 3:4], qs[:, 4:5]
                alpha = vrow[:, i:i + 1]
                dve.tensor_scalar(den, alpha, beta, qs[:, 0:1], ALU.mult, ALU.subtract)
                then(dve.scalar_tensor_tensor(ucol[:], QA[:, :, i], beta, dots[:], ALU.mult, ALU.subtract))
                dve.reciprocal(den, den)
                then(dve.tensor_scalar(alpha, alpha, beta, None, ALU.subtract))
                then(dve.tensor_scalar(ucol[:], ucol[:], den, -1.0, ALU.mult, ALU.mult))
                for c, done in ((0, row_updated), (1, basis_updated)):
                    dve.scalar_tensor_tensor(QA[:, c, i:C], vrow[:, i:C], ucol[:, c:c + 1], QA[:, c, i:C],
                                             ALU.mult, ALU.add).then_inc(done, 1)

            def subspace_map():
                o = full(dve, "UT")
                dve.tensor_copy(UTx[0:64, 0:C], o[0:ROT, 0:C])
                dve.tensor_copy(UTx[64:128, 0:C], o[0:ROT, 0:C]).then_inc(empty("UT"), 1)
                evacuated(dve, "UT")
                for k in range(1, 3):
                    ins = dve.tensor_copy(UTx[:, 128 + 32 * k:128 + 32 * k + TAIL], UTx[:, 128:C])
                ins.then_inc(ut_done, 1)
                o = full(dve, "RU")
                dve.tensor_copy(RU[:], o[:, 0:C]).then_inc(empty("RU"), 1)
                for b in range(B):
                    job = ("MA", b)
                    o = full(dve, job)
                    dve.tensor_copy(MA[:, b, :], o[:, 0:C])
                    dve.tensor_copy(MB[:, b, :], o[0:96, C:2 * C])
                    dve.tensor_copy(MBf[:, b, :], o[0:96, C:2 * C]).then_inc(empty(job), 1)
                    evacuated(dve, job)
                    dve.tensor_tensor(MB[64:96, b, :], MBf[64:96, b, :], MB[64:96, b, :].bitcast(F32), ALU.subtract).then_inc(m_done, 1)

            norms = [0]

            added = [0]

            def statistics(half):
                if added[0]:
                    dve.wait_ge(x_done, added[0])
                tiles = range(4 * half, 4 * half + 4)
                for tt in tiles:
                    ins = dve.bn_stats(stats[:, tt, :], x[:, tt, :])
                then(ins)
                for tt in tiles:
                    ins = dve.bn_aggr(mv[:, tt, :], stats[:, tt, :])
                then(ins)
                span = slice(4 * half, 4 * half + 4)
                dve.tensor_scalar(vare[:, span], mv[:, span, 1], EPS, None, ALU.add).then_inc(var_done, 1)

            def normalise(half):
                norms[0] += 1
                dve.wait_ge(rstd_done, norms[0])
                for tt in range(4 * half, 4 * half + 4):
                    dve.tensor_scalar(xe[:, tt, 0:C], x[:, tt, :], mv[:, tt, 0:1], rstd[:, tt:tt + 1],
                                      ALU.subtract, ALU.mult).then_inc(xe_nat, 1)

            def mains(s, n, kind):
                for half in range(2):
                    job = ("tA", s, half)
                    o = full(dve, job)
                    dst, o = by_quarters(tA[:, half * L:(half + 1) * L], s), in_order(o, s)
                    if kind is None:
                        ins = dve.tensor_copy(dst, o)
                    else:
                        ins = dve.tensor_scalar(dst, o, mod[:, n, kind + 1, 0, half:half + 1],
                                                mod[:, n, kind, 0, half:half + 1], ALU.mult, ALU.add)
                    ins.then_inc(empty(job), 1)
                    evacuated(dve, ("tB", s, half))
                    cols = slice(half * L, (half + 1) * L)
                    dve.tensor_tensor(tB[32:64, cols], tBf[32:64, cols], tB[32:64, cols].bitcast(F32),
                                      ALU.subtract).then_inc(tB_done, 1)

            def low_tail_weights(n):
                dve.wait_ge(raw_in[n], 16)
                dve.wait_ge(wb_high, n + 1)
                dve.tensor_tensor(WBs[n][64:96, 0:COLS[n]], raws[n][64:96, 0:COLS[n]],
                                  WBs[n][64:96, 0:COLS[n]].bitcast(F32), ALU.subtract).then_inc(wb_done, 1)

            for i in range(FIRST_ROWS):
                if i == 0:
                    dve.wait_ge(basis_in, 16)
                reflect_dots(i)
                if i == 2:
                    ada_vectors(0)
                    dve.wait_ge(x_in, 16)
                    statistics(0)
                    statistics(1)
                    normalise(0)
                    normalise(1)
                if i == 3:
                    gate_vectors(0)
                if i == 4:
                    mains(0, 0, 0)
                if i == 6:
                    low_tail_weights(0)
                if i == 11:
                    generators()
                for n in (1, 2):
                    if i == 10 + 2 * n:
                        ada_vectors(n)
                        gate_vectors(n)
                if i == 13:
                    dve.memset(ws[:, 0:4096], 0.0).then_inc(preset, 1)
                reflect_update(i)
            dve.wait_ge(tables_in, 48)
            dve.memset(G[64:65, :, 4, :], 1.0).then_inc(preset, 1)

            def residual(name, n, which, half):
                for pair in (2 * half, 2 * half + 1):
                    job = (*name, pair)
                    o = full(dve, job)
                    gt = gates[:, n, half, which * C:(which + 1) * C].unsqueeze(1).broadcast_to([128, 2, C])
                    dve.tensor_tensor(tmp[:, pair, :].rearrange("p (j c) -> p j c", j=2),
                                      o[:, 0:2 * C].rearrange("p (j c) -> p j c", j=2), gt, ALU.mult).then_inc(empty(job), 1)
                    evacuated(dve, job)
                    xs = x[:, 2 * pair:2 * pair + 2, :].rearrange("p t c -> p (t c)")
                    dve.tensor_tensor(xs, xs, tmp[:, pair, :], ALU.add).then_inc(x_done, 1)
                    added[0] += 1
                    if which == 1:
                        for step in mlp_step(n, 2, pair):
                            reflect_dots(step)
                            reflect_update(step)

            def normalised(n, i):
                b, g = divmod(i, NG)
                job = ("ot", n, i)
                o = full(dve, job)
                then(dve.reciprocal(rden[:], o[:, D::32]))
                heads = o.rearrange("p (q c d) -> p q c d", q=4, c=GR)
                dst = xe[:, 4 * b:4 * b + 4, g * GR * D:(g + 1) * GR * D].rearrange("p q (c d) -> p q c d", c=GR)
                rd = rden[:].rearrange("p (q c) -> p q c", q=4)
                for qt in range(4):
                    ins = dve.tensor_tensor(dst[:, qt], heads[:, qt, :, 0:D], rd[:, qt].unsqueeze(2).broadcast_to([128, GR, D]), ALU.mult)
                ins.then_inc(empty(job), 1)

            def split(n, i, part):
                job = ("qk", n, i, part)
                o = full(dve, job)
                unit = n // 2 * 8 + i
                dve.wait_ge(hi_done, 2 * unit + 2 - part)
                if part == 1 and unit:
                    dve.wait_ge(km_act, MASKS_ON_ACT * unit)
                    dve.wait_ge(km_pool, (GR - MASKS_ON_ACT) * unit)
                dve.scalar_tensor_tensor(k_tmp[:] if part else q1[:, i % 2, :], hi_tmp[:, part, :].bitcast(F32),
                                         neg_lo[:, part:part + 1], o, ALU.mult, ALU.add).then_inc(empty(job), 1)

            def attention(n):
                split(n, 0, 1)
                split(n, 0, 0)
                for u in range(UNITS + SCORES_AFTER + 2):
                    g, part = divmod(u, 4)
                    maxima = unit_of(u)
                    for j, c in enumerate((0, 2, 1, 3)):
                        if maxima:
                            job = ("mx", n, g, part, c)
                            o = full(dve, job)
                            dve.tensor_reduce(nmx[:, g % 2, part * 4 + c:part * 4 + c + 1], o, AX.X, ALU.max,
                                              negate=True).then_inc(empty(job), 1)
                            for step in row_steps(n, 4 * u + j, DOTS_AT):
                                reflect_dots(step)
                            for step in row_steps(n, 4 * u + j, UPDATE_AT):
                                reflect_update(step)
                        if j == 0 and part in (2, 3) and g + 1 < B * NG:
                            split(n, g + 1, part == 2)
                        if j == 1 and part == 0 and 0 <= g - 3 < B * NG:
                            normalised(n, g - 3)
                    if part == 0 and 0 <= g - 1 < B * NG:
                        job = ("mt", n, g - 1)
                        o = full(dve, job)
                        dve.tensor_tensor(q2[:, (g - 1) % 2, :], q1[:, (g - 1) % 2, :].bitcast(F32), o, ALU.add).then_inc(empty(job), 1)
                normalised(n, B * NG - 1)
                dve.wait_ge(empty(("ot", n, B * NG - 1)), use[("ot", n, B * NG - 1)][1])

            def heads():
                def exponentials(j, part):
                    for k in expm_steps(j)[part:part + 1]:
                        exponential(k)

                for j in range(T + 1):
                    first, second = HEADS_ROW + 2 * j, HEADS_ROW + 2 * j + 1
                    if j < T:
                        reflect_dots(first)
                        S = hS[:, j % 4]
                        dve.wait_ge(hprod_done, 2 * (j + 1))
                        if j >= 4:
                            dve.wait_ge(ho_done, j - 3)
                        dve.tensor_reduce(S, prod[j % 2].rearrange("p (h k d) -> p h k d", h=H, k=H), AX.X, ALU.add).then_inc(hsum_done, 1)
                    exponentials(j, 0)
                    if j < T:
                        reflect_update(first)
                        dve.wait_ge(hsum_done, j + 1)
                        then(dve.tensor_reduce(hmax[:, j % 2], S, AX.X, ALU.max))
                        dve.tensor_tensor(S, S, hmax[:, j % 2].unsqueeze(2).broadcast_to([128, H, H]), ALU.subtract).then_inc(hs_done, 1)
                    t1 = j - 1
                    S1 = hS[:, t1 % 4]
                    if j >= 1:
                        dve.wait_ge(hp_done, t1 + 1)
                        dve.tensor_reduce(hden[:, t1], S1, AX.X, ALU.add)
                    if j < T:
                        reflect_dots(second)
                    if j >= 1:
                        pv = prod[2].rearrange("p (h d k) -> p h d k", h=H, d=D)
                        vv = hq[:, t1, 2 * C:3 * C].rearrange("p (k d) -> p d k", k=H)
                        if t1:
                            dve.wait_ge(ho_done, t1)
                        then(dve.tensor_tensor(pv[:, 0:H // 2], S1[:, 0:H // 2].unsqueeze(2).broadcast_to([128, H // 2, D, H]),
                                               vv.unsqueeze(1).broadcast_to([128, H // 2, D, H]), ALU.mult))
                    exponentials(j, 1)
                    if j < T:
                        reflect_update(second)
                    if j >= 1:
                        dve.reciprocal(hden[:, t1], hden[:, t1])
                        dve.wait_ge(values_done, t1 + 1)
                        dve.tensor_reduce(hO[:, t1, :].rearrange("p (h d) -> p h d", h=H), pv, AX.X, ALU.add).then_inc(ho_done, 1)
                    exponentials(j, 2)
                    if j >= 1:
                        dve.wait_ge(ho_done, t1 + 1)
                        o = hO[:, t1, :].rearrange("p (h d) -> p h d", h=H)
                        dve.tensor_tensor(o, o, hden[:, t1].unsqueeze(2).broadcast_to([128, H, D]), ALU.mult).then_inc(head_norm, 1)
                dve.wait_ge(head_norm, T)
                for hh in (0, 1):
                    for u in range(4):
                        dve.tensor_copy(*head_block(1, u, hh)).then_inc(head_rows[1], 1)
                dve.memset(G[64:65, :, 4, :], 1.0).then_inc(ones_set, 1)

            for n in range(NL):
                s = [0, 3, 7][n]
                if n == 2:
                    for half in range(B):
                        statistics(half)
                if n:
                    for half in range(B):
                        normalise(half)
                    mains(s, n, 0)
                if n == 1:
                    heads()
                else:
                    attention(n)
                mains(s + 1, n, None)
                for half in range(B):
                    residual(("proj", n), n, 0, half)
                    statistics(half)
                for half in range(B):
                    normalise(half)
                mains(s + 2, n, 2)
                if n == 0:
                    exponential_start()
                for b in range(B):
                    for m in range(5):
                        for step in mlp_step(n, b, m):
                            reflect_dots(step)
                        for step in mlp_expm(n, b, m):
                            exponential(step)
                        for step in mlp_step(n, b, m):
                            reflect_update(step)
                if n < NL - 1:
                    if n == 0:
                        low_tail_weights(1)
                    for half in range(B):
                        residual(("f2", n, 0), n, 1, half)
                        if n == 0:
                            statistics(half)
                    dve.wait_ge(x_done, added[0])
                else:
                    o = full(dve, "logits")
                    dve.tensor_copy(lg[:].rearrange("p t e -> p (t e)"), o[:, 0:T * E]).then_inc(empty("logits"), 1)
                    evacuated(dve, "logits")
                    then(dve.tensor_reduce(m1[:], lg[:], AX.X, ALU.max))
                    other = lg[:].unsqueeze(2).broadcast_to([128, T, E, E])
                    own = lg[:].unsqueeze(3).broadcast_to([128, T, E, E])
                    dve.tensor_tensor(ahead, other, own, ALU.is_gt)
                    then(dve.tensor_tensor(tied, other, own, ALU.is_equal))
                    then(dve.tensor_tensor(tied, tied, tri[:].unsqueeze(1).broadcast_to([128, T, E, E]), ALU.mult))
                    then(dve.tensor_tensor(ahead, ahead, tied, ALU.add))
                    then(dve.tensor_reduce(cnt[:, 0], ahead, AX.X, ALU.add))
                    then(dve.tensor_scalar(cnt[:, 0], cnt[:, 0], 1.5, None, ALU.is_lt))
                    dve.tensor_tensor(cw[:], lg[:], m1[:].unsqueeze(2).broadcast_to([128, T, E]), ALU.subtract).then_inc(lg_ready, 1)
                    dve.wait_ge(lg_exp, 1)
                    then(dve.tensor_tensor(cw[:], cnt[:, 1], cnt[:, 0], ALU.mult))
                    then(dve.tensor_reduce(den[:], cw[:], AX.X, ALU.add))
                    then(dve.reciprocal(den[:], den[:]))
                    then(dve.tensor_tensor(cw[:], cw[:], den[:].unsqueeze(2).broadcast_to([128, T, E]), ALU.mult))
                    for e in range(E):
                        for pair in range(T // 2):
                            job = ("f2", n, e, pair)
                            o = full(dve, job)
                            for j in range(2):
                                tt = 2 * pair + j
                                if e == 0:
                                    ins = dve.tensor_scalar(acc[:, tt, :], o[:, j * C:(j + 1) * C], cw[:, tt, e:e + 1], None, ALU.mult)
                                else:
                                    ins = dve.scalar_tensor_tensor(acc[:, tt, :], o[:, j * C:(j + 1) * C], cw[:, tt, e:e + 1],
                                                                   acc[:, tt, :], ALU.mult, ALU.add)
                            ins.then_inc(empty(job), 1)
                            evacuated(dve, job)
                            if e == E - 1:
                                gt = gates[:, n, pair // 2, C:2 * C].unsqueeze(1).broadcast_to([128, 2, C])
                                xs, ac = x[:, 2 * pair:2 * pair + 2, :], acc[:, 2 * pair:2 * pair + 2, :]
                                then(dve.tensor_tensor(ac, ac, gt, ALU.mult))
                                dve.tensor_tensor(xs, xs, ac, ALU.add).then_inc(x_final, 1)
                if n == 1:
                    for tt in range(T):
                        dve.tensor_copy(xe[:, tt, 0:C], x[:, tt, :]).then_inc(xe_nat, 1)
                    mains(6, n, None)
                    exponential_end()
                    subspace_map()
                    low_tail_weights(2)
                    for pair in range(T // 2):
                        job = ("rot", pair)
                        o = full(dve, job)
                        xs = x[:, 2 * pair:2 * pair + 2, :].rearrange("p t c -> p (t c)")
                        ins = dve.tensor_tensor(xs, xs, o[:, 0:2 * C], ALU.add).then_inc(empty(job), 1)
                    evacuated(dve, job)

        @block.scalar
        def _(act):
            act.wait_ge(const_in, 16 * 4)
            act.activation(cA[:, 1, :], cA[:, 0, :], ACT.Exp, scale=-1.0).then_inc(silu_exp, 1)
            act.activation(cB[:, 1, :], cB[:, 0, :], ACT.Exp, scale=-1.0).then_inc(silu_exp, 1)
            def reflect_row(i):
                job = ("house", i)
                o = full(act, job)
                if i:
                    act.wait_ge(basis_updated, i)
                act.activation(vrow[:, i:C], o[:, 0:C - i], ACT.Copy).then_inc(vrow_ready, 1)
                act.activation(vsq[:, i:C], o[:, 0:C - i], ACT.Square, bias=tiny[:], accum_out=qs[:, 0:1]).then_inc(empty(job), 1)

            def tails(s, n, kind):
                for half in range(2):
                    job = ("tB", s, half)
                    o = full(act, job)
                    for dst, rows in ((tB, slice(0, 96)), (tBf, slice(32, 64))):
                        d, r = by_quarters(dst[rows, half * L:(half + 1) * L], s), in_order(o[rows, :], s)
                        if kind is None:
                            ins = act.activation(d, r, ACT.Copy)
                        else:
                            ins = act.activation(d, r, ACT.Identity, scale=mod[rows, n, kind + 1, 1, half:half + 1],
                                                 bias=mod[rows, n, kind, 1, half:half + 1])
                    ins.then_inc(empty(job), 1)

            def out_copy(n, i):
                job = ("pv", n, i)
                act.activation(oT[:, i % 2, :], full(act, job), ACT.Copy).then_inc(empty(job), 1)

            def high(n, i, part):
                job = ("qk", n, i, part)
                o = full(act, job)
                if i:
                    evacuated(act, ("qk", n, i - 1, part))
                act.activation(hi_tmp[:, part, :], o, ACT.Copy).then_inc(hi_done, 1)

            def masks(n, i, heads=range(MASKS_ON_ACT)):
                evacuated(act, ("qk", n, i, 1))
                for c in heads:
                    act.activation(km[:, i % 3, c, :], k_tmp[:], ACT.Copy, scale=neg_lo[:, 2 + c:3 + c]).then_inc(km_act, 1)

            def attention(n):
                for pair in range(T // 2):
                    job = ("v", n, pair)
                    o = full(act, job)
                    act.activation(Vh[:, 2 * pair:2 * pair + 2, :, 0:10].rearrange("p t h d -> p (t h) d"),
                                   o[:, 0:320].rearrange("p (h d) -> p h d", d=10), ACT.Copy).then_inc(empty(job), 1)
                high(n, 0, 1)
                high(n, 0, 0)
                masks(n, 0)
                for u in range(UNITS + SCORES_AFTER + 2):
                    g, part = divmod(u, 4)
                    scores = unit_of(u - SCORES_AFTER)
                    for pr in range(2):
                        if scores:
                            job = ("st", n, *scores, pr)
                            full(act, job)
                            buf = (2 * (u - SCORES_AFTER) + pr) % 4
                            act.activation(Pb[:, buf], psum[:, 2 * pr:2 * pr + 2, :], ACT.Exp,
                                           scale=float(D) ** -0.5).then_inc(empty(job), 1)
                        for m in range(2):
                            for step in row_steps(n, 4 * u + 2 * pr + m):
                                reflect_row(step)
                        if part in (2, 3) and pr == 0 and g + 1 < B * NG:
                            masks(n, g + 1, [part - 2])
                    if part == 2 and 0 <= (u - 10) // 4 < B * NG:
                        out_copy(n, (u - 10) // 4)
                    if part in (1, 2) and g + 1 < B * NG:
                        high(n, g + 1, part == 1)

            def kept(k):
                if k >= TAYLOR:
                    evacuated(act, ("expm", k - 1))
                    act.activation(Rk_flat, Rm_flat, ACT.Copy, scale=sq[:, 1, k - TAYLOR:k - TAYLOR + 1]).then_inc(kept_done, 1)

            def heads():
                for j in range(T):
                    job = ("hqkv", j)
                    act.activation(hq[:, j, :], full(act, job)[:, 0:3 * C], ACT.Copy).then_inc(empty(job), 1)
                reflect_row(HEADS_ROW)
                for j in range(T + 1):
                    for k in expm_steps(j)[0:1]:
                        kept(k)
                    if j < T:
                        reflect_row(HEADS_ROW + 2 * j + 1)
                        act.wait_ge(hs_done, j + 1)
                        act.activation(hS[:, j % 4], hS[:, j % 4], ACT.Exp, scale=float(D) ** -0.5).then_inc(hp_done, 1)
                    for k in expm_steps(j)[1:2]:
                        kept(k)
                    if j < T - 1:
                        reflect_row(HEADS_ROW + 2 * j + 2)
                    for k in expm_steps(j)[2:]:
                        kept(k)
                    if j >= T // 2 + 1:
                        act.wait_ge(head_norm, T // 2)
                        for u in range(4):
                            act.activation(*head_block(0, u, j - T // 2 - 1), ACT.Copy).then_inc(head_rows[0], 1)
                act.wait_ge(head_norm, T)
                for hh in (2, 3):
                    for u in range(4):
                        act.activation(*head_block(1, u, hh), ACT.Copy).then_inc(head_rows[1], 1)

            def high_tail_weights(n):
                act.wait_ge(raw_in[n], 16)
                act.activation(WBs[n][:, 0:COLS[n]], raws[n][0:96, 0:COLS[n]], ACT.Copy).then_inc(wb_high, 1)

            act.wait_ge(preset, 8)
            for i in range(FIRST_ROWS):
                reflect_row(i)
                if i == 3:
                    evacuated(act, ("ada", 0))
                    tails(0, 0, 0)
                if i == 5:
                    high_tail_weights(0)
            act.wait_ge(preset, 10)
            act.wait_ge(tables_in, 48)
            for n in range(NL):
                s = [0, 3, 7][n]
                if n:
                    evacuated(act, ("ada", n))
                    tails(s, n, 0)
                if n == 1:
                    heads()
                else:
                    attention(n)
                tails(s + 1, n, None)
                tails(s + 2, n, 2)
                if n == NL - 1:
                    act.wait_ge(lg_ready, 1)
                    act.activation(cnt[:, 1], cw[:], ACT.Exp).then_inc(lg_exp, 1)
                func = ACT.Gelu if n == 1 else ACT.Gelu_apprx_tanh
                for e in range(E if n == NL - 1 else 1):
                    for b in range(B):
                        for m, (c0, w) in enumerate(MC):
                            job = ("f1", n, e, b, m)
                            o = full(act, job)
                            act.activation(G[0:w, b, m, :], o[0:w, :], func).then_inc(empty(job), 1)
                            for step in mlp_step(n, b, m):
                                reflect_row(step)
                            for step in mlp_expm(n, b, m):
                                kept(step)
                if n == 0:
                    high_tail_weights(1)
                for pair in range(T // 2):
                    for step in mlp_step(n, 2, pair):
                        reflect_row(step)
                if n == 1:
                    tails(6, n, None)
                    high_tail_weights(2)

        @block.gpsimd
        def _(pool):

            raised = {}

            def signal(ins, s):
                raised[s.name] = raised.get(s.name, 0) + 1
                ins.then_inc(s, 1)
                pool.wait_ge(s, raised[s.name])

            halves = [0]

            def tail_copies(half, job=None):
                if job == "heads":
                    pool.wait_ge(head_rows[half], 16)
                elif job:
                    evacuated(pool, job)
                else:
                    halves[0] += 1
                    pool.wait_ge(xe_nat, 4 * halves[0])
                rows = xe[:, 4 * half:4 * half + 4, :]
                for k in range(1, 3):
                    at = 128 + 32 * k
                    signal(pool.tensor_copy(rows[:, :, at:at + TAIL], rows[:, :, 128:C]), xe_dup)

            def max_rows(n, i):
                for c in (1, 3):
                    evacuated(pool, ("mx", n, i, 3, c))
                m = nmx[:, i % 2, :]
                signal(pool.tensor_copy(mhi[:, i % 2, :], m), pool_step)
                signal(pool.tensor_copy(mt[:, i % 2, 27::32], mhi[:, i % 2, :].bitcast(F32)), mt_done)
                signal(pool.tensor_tensor(mt[:, i % 2, 28::32], m, mhi[:, i % 2, :].bitcast(F32), ALU.subtract), mt_done)

            norms = [0]

            def rstds():
                for half in range(B):
                    norms[0] += 1
                    pool.wait_ge(var_done, norms[0])
                    span = slice(4 * half, 4 * half + 4)
                    signal(pool.tensor_tensor(rstd[:, span], vare[:, span], power[:, span], ALU.pow), rstd_done)
                for half in range(B):
                    tail_copies(half)

            def masks(n, i):
                evacuated(pool, ("qk", n, i, 1))
                if i >= 3:
                    for pr in range(2):
                        evacuated(pool, ("st", n, i - 3, 3, pr))
                for c in range(MASKS_ON_ACT, GR):
                    signal(pool.tensor_scalar(km[:, i % 3, c, :], k_tmp[:], neg_lo[:, 2 + c:3 + c], None, ALU.mult), km_pool)

            def attention(n):
                masks(n, 0)
                for u in range(UNITS + 1):
                    g, part = divmod(u, 4)
                    if part == 0 and g:
                        max_rows(n, g - 1)
                    if part == 2 and g + 1 < B * NG:
                        masks(n, g + 1)
                    for m in range(4):
                        for step in row_steps(n, 4 * u + m, DOTS_AT):
                            reflector(step)
                    if u == 28:
                        tail_copies(0, ("ot", n, 3))
                tail_copies(1, ("ot", n, 7))

            def heads():
                def products(j, half):
                    if half == 0:
                        evacuated(pool, ("hqkv", j))
                        if j >= 2:
                            pool.wait_ge(hsum_done, j - 1)
                    hh = slice(half * H // 2, (half + 1) * H // 2)
                    q, k = (hq[:, j, p * C:(p + 1) * C].rearrange("p (h d) -> p h d", h=H) for p in range(2))
                    pj = prod[j % 2].rearrange("p (h k d) -> p h k d", h=H, k=H)[:, hh]
                    signal(pool.tensor_tensor(pj, q[:, hh].unsqueeze(2).broadcast_to([128, H // 2, H, D]),
                                              k.unsqueeze(1).broadcast_to([128, H // 2, H, D]), ALU.mult), hprod_done)

                for j in range(2):
                    products(j, 0)
                    products(j, 1)
                def values(t1):
                    pool.wait_ge(hp_done, t1 + 1)
                    if t1:
                        pool.wait_ge(ho_done, t1)
                    hh = slice(H // 2, H)
                    pv = prod[2].rearrange("p (h d k) -> p h d k", h=H, d=D)[:, hh]
                    vv = hq[:, t1, 2 * C:3 * C].rearrange("p (k d) -> p d k", k=H)
                    signal(pool.tensor_tensor(pv, hS[:, t1 % 4][:, hh].unsqueeze(2).broadcast_to([128, H // 2, D, H]),
                                              vv.unsqueeze(1).broadcast_to([128, H // 2, D, H]), ALU.mult), values_done)

                for j in range(T):
                    reflector(HEADS_ROW + 2 * j)
                    if j:
                        values(j - 1)
                    if j + 2 < T:
                        products(j + 2, 0)
                    reflector(HEADS_ROW + 2 * j + 1)
                    if j + 2 < T:
                        products(j + 2, 1)
                values(T - 1)
                tail_copies(0, "heads")
                pool.wait_ge(ho_done, T)
                signal(pool.memset(ws[:, 0:4096], 0.0), pads_set)
                tail_copies(1, "heads")


            def reflector(i):
                sigma, root, sign2, beta = (qs[:, c:c + 1] for c in range(4))
                alpha = vrow[:, i:i + 1]
                pool.wait_ge(vrow_ready, i + 1)
                if i:
                    pool.wait_ge(basis_updated, i)
                signal(pool.tensor_scalar(sign2, alpha, 0.0, -2.0, ALU.is_ge, ALU.mult), pool_step)
                evacuated(pool, ("house", i))
                signal(pool.tensor_tensor(root, sigma, power[:, T:T + 1], ALU.pow), pool_step)
                signal(pool.tensor_scalar(beta, sign2, 1.0, root, ALU.add, ALU.mult), reflector_done)

            for i in range(FIRST_ROWS):
                reflector(i)
                if i == 2:
                    rstds()
                if i == 12:
                    pool.wait_ge(rowsum, 1)
                    signal(pool.partition_all_reduce(n1[:, 1:2], n1[:, 0:1], 128, RED.max), norm_max)
            pool.wait_ge(tables_in, 48)
            for n in range(NL):
                s = [0, 3, 7][n]
                if n:
                    rstds()
                if n == 1:
                    heads()
                else:
                    attention(n)
                rstds()
                for b in range(B):
                    for m in range(5):
                        for step in mlp_step(n, b, m):
                            reflector(step)
                for pair in range(T // 2):
                    for step in mlp_step(n, 2, pair):
                        reflector(step)
                if n == 1:
                    for half in range(2):
                        tail_copies(half)


def constants():
    import numpy as np

    ident = np.eye(128, dtype=np.float32)
    r = np.arange(128) % 32
    neg_lo = np.zeros((128, 2 + GR), np.float32)
    neg_lo[:, 0] = np.where((r >= D) & (r < 2 * D), -1, 0)
    neg_lo[:, 1] = np.where((r >= 2 * D) & (r < 3 * D), -1, 0)
    for c in range(GR):
        neg_lo[:, 2 + c] = np.arange(128) // 32 == c
    silu_fix = np.zeros((17, 2), np.float32)
    silu_fix[:16, 0] = 1
    silu_fix[16, 1] = 1
    tri = np.broadcast_to(np.tril(np.ones((E, E), np.float32), -1), (128, E, E))
    thr = np.broadcast_to(2.0 ** np.arange(NSQ, dtype=np.float32), (128, NSQ))
    sgn = np.triu(np.ones((ROT, ROT), np.float32), 1) - np.tril(np.ones((ROT, ROT), np.float32), -1)
    eye2 = np.tile(np.eye(ROT, dtype=np.float32), (2, 2))
    return {"ident": ident, "neg_lo": neg_lo, "silu_fix": silu_fix, "tri": tri, "thr": thr, "sgn": sgn, "eye2": eye2}


def lay_out(v):
    import numpy as np

    f = {k: np.asarray(a) for k, a in v.items()}
    a = constants()
    a["x"] = f["x"].reshape(B * L, C)
    cond = np.zeros((145, 2), np.float32)
    cond[:C] = f["cond_1152"].T
    a["condA"], a["condB"] = cond[:128], cond[128:]

    def with_bias(w, b):
        return np.concatenate([w, b.reshape(1, -1)], 0)

    def cols_tail3(w):
        o = np.zeros((w.shape[0], 224), np.float32)
        o[:, :128] = w[:, :128]
        for k in range(3):
            o[:, 128 + 32 * k:144 + 32 * k] = w[:, 128:]
        return o

    def rows_tail3(w):
        o = np.zeros((96, w.shape[1]), np.float32)
        for k in range(3):
            o[32 * k:32 * k + 17] = w[128:145]
        return o

    def qkv(w):
        q, k, vv = (w[:, j * C:(j + 1) * C].reshape(-1, H, D) for j in range(3))
        oq = np.zeros((w.shape[0], H, 32), np.float32)
        ok = np.zeros((w.shape[0], H, 32), np.float32)
        for j in range(3):
            oq[:, :, j * D:(j + 1) * D] = q
            ok[:, :, j * D:(j + 1) * D] = k
        ok[C, :, 27:29] = 1
        ov = np.zeros((w.shape[0], H, D + 1), np.float32)
        ov[:, :, :D] = vv
        ov[C, :, D] = 1
        return [o.reshape(w.shape[0], -1) for o in (oq, ok, ov)]

    def fc2(ws, bs):
        o = np.zeros((128, len(ws), 5, C), np.float32)
        for e, (w, b) in enumerate(zip(ws, bs)):
            for m, (c0, n) in enumerate(MC):
                o[:n, e, m] = w[c0:c0 + n]
            o[64, e, 4] = b
        return o

    names = [("L0_cond_W_qkv", "L0_cond_b_qkv", "L0_cond_W_proj", "L0_cond_b_proj", "L0_cond_W_ada", "L0_cond_b_ada"),
             ("L1_cond_qkv_w", "L1_cond_qkv_b", "L1_cond_proj_w", "L1_cond_proj_b", "L1_cond_ada_w", "L1_cond_ada_b"),
             ("L3_cond_w_qkv", "L3_cond_b_qkv", "L3_cond_w_proj", "L3_cond_b_proj", "L3_cond_w_adaln", "L3_cond_b_adaln")]
    ffs = [([f["L0_cond_W_fc1"]], [f["L0_cond_b_fc1"]], [f["L0_cond_W_fc2"]], [f["L0_cond_b_fc2"]]),
           ([f["L1_cond_fc1_w"]], [f["L1_cond_fc1_b"]], [f["L1_cond_fc2_w"]], [f["L1_cond_fc2_b"]]),
           (f["L3_cond_w1"], f["L3_cond_b1"], f["L3_cond_w2"], f["L3_cond_b2"])]
    for n, ((wq, bq, wp, bp, wa, ba), (w1, b1, w2, b2)) in enumerate(zip(names, ffs)):
        w = with_bias(f[wq], f[bq])
        if n == 1:
            parts = [np.concatenate([w, np.zeros((145, PC - 3 * C), np.float32)], 1)]
        else:
            parts = qkv(w)
        parts.append(with_bias(f[wp], f[bp]))
        parts += [with_bias(w, b) for w, b in zip(w1, b1)]
        if n == NL - 1:
            parts.append(with_bias(f["L3_cond_w_gate"], np.zeros(E, np.float32)))
        w = np.concatenate(parts, 1)
        a[f"wa{n}"] = w[:128]
        a[f"wb{n}"] = rows_tail3(w)
        a[f"w2{n}"] = fc2(w2, b2)
        w = with_bias(f[wa], f[ba])
        six = [w[:, k * C:(k + 1) * C] for k in range(6)]
        a[f"ada{n}"] = np.concatenate([cols_tail3(six[k]) for k in (0, 1, 3, 4)] + [six[2], six[5]], 1)

    iu, ju = np.triu_indices(ROT, 1)
    sk = np.zeros((145, ROT, ROT), np.float32)
    w = with_bias(f["L2_cond_W"].T, f["L2_cond_b"])
    sk[:, ju, iu] = w
    sk[:, iu, ju] = w
    a["skew_w"] = sk.reshape(145, -1)
    aug = np.zeros((256, C), np.float32)
    aug[:ROT] = f["L2_cond_P"].T
    aug[ROT:ROT + C] = np.eye(C, dtype=np.float32)
    a["aug"] = aug.reshape(2, 128, C).transpose(1, 0, 2)
    return {k: np.ascontiguousarray(z) for k, z in a.items()}


def kernel(**inputs):
    import concourse.bacc as bacc
    from concourse.bass_utils import run_bass_kernel_spmd

    arrays = lay_out(inputs)
    nc = bacc.Bacc("TRN2", target_bir_lowering=False, num_devices=1)
    t = {k: nc.dram_tensor(f"in_{k}", z.shape, F32, kind="ExternalInput").ap() for k, z in arrays.items()}
    out = nc.dram_tensor("x_out", (B * L, C), F32, kind="ExternalOutput").ap()
    build(nc, t, out)
    r = run_bass_kernel_spmd(nc, [{f"in_{k}": z for k, z in arrays.items()}], core_ids=[0])
    return r.results[0]["x_out"].reshape(B, L, C)
```
